# Optimizing a Trainium2 kernel written in Bass

```python
import numpy as np
import jax
import jax.numpy as jnp

def _softmax(x, axis=-1):
    return jax.nn.softmax(x, axis=axis)

def _gelu(x):
    return jax.nn.gelu(x, approximate=True)

def _silu(x):
    return jax.nn.silu(x)

def _sigmoid(x):
    return jax.nn.sigmoid(x)

def _layernorm(x, axis=-1, eps=1e-05):
    m = jnp.mean(x, axis=axis, keepdims=True)
    v = jnp.var(x, axis=axis, keepdims=True)
    return (x - m) / jnp.sqrt(v + eps)

def _scatter_add(tgt, idx, src, axis=0):
    return tgt.at[idx].add(src)

def _segment_sum(src, seg, n):
    return jax.ops.segment_sum(src, seg, n)
kernel_name = 'mk_seq_preln_d4_jaxref_r8_beb51e'

def setup_inputs(seed: int=0):
    np.random.seed(seed)
    _w = jnp.asarray

    def _L0_attn_setup():
        import jax, jax.numpy as jnp
        import numpy as np
        D_MODEL = 128
        EXP = 2
        D_IN = D_MODEL * EXP
        D_STATE = 16
        CONV_D = 4
        BATCH = 4
        SEQ = 256

        def _rmsnorm(x, w, eps=1e-06):
            return x * jax.lax.rsqrt(jnp.mean(x * x, axis=-1, keepdims=True) + eps) * w
        key = jax.random.key(seed)
        ks = jax.random.split(key, 8)
        sd = 1.0 / np.sqrt(D_MODEL)
        sdi = 1.0 / np.sqrt(D_IN)
        return {'x': jax.random.normal(ks[0], (BATCH, SEQ, D_MODEL), jnp.float32), 'norm_w': jnp.ones((D_MODEL,), jnp.float32), 'Win': jax.random.normal(ks[1], (D_MODEL, D_IN), jnp.float32) * sd, 'b_in': jnp.zeros((D_IN,), jnp.float32), 'conv_w': jax.random.normal(ks[2], (D_IN, 1, CONV_D), jnp.float32) * 0.5, 'conv_b': jnp.zeros((D_IN,), jnp.float32), 'A': jax.random.normal(ks[3], (D_IN, D_STATE, D_STATE), jnp.float32) * 0.1, 'Bm': jax.random.normal(ks[4], (D_IN, D_STATE, 1), jnp.float32), 'Cm': jax.random.normal(ks[5], (D_IN, 1, D_STATE), jnp.float32), 'Wout': jax.random.normal(ks[6], (D_IN, D_MODEL), jnp.float32) * sdi, 'b_out': jnp.zeros((D_MODEL,), jnp.float32)}
    _L0_attn_in = _L0_attn_setup()

    def _L0_ffn_setup():
        import jax, jax.numpy as jnp
        import numpy as np
        B, S, H, I, E, K = (2, 64, 128, 64, 64, 8)
        key = jax.random.key(seed)
        ks = jax.random.split(key, 8)
        return {'hidden_states': jax.random.normal(ks[0], (B, S, H), dtype=jnp.float32), 'router_w': jax.random.normal(ks[1], (H, E), dtype=jnp.float32) * 0.02, 'shared_gate_w': jax.random.normal(ks[2], (H, I), dtype=jnp.float32) * 0.02, 'shared_up_w': jax.random.normal(ks[3], (H, I), dtype=jnp.float32) * 0.02, 'shared_down_w': jax.random.normal(ks[4], (I, H), dtype=jnp.float32) * 0.02, 'expert_gate_k': jax.random.normal(ks[5], (E, H, I), dtype=jnp.float32) * 0.02, 'expert_up_k': jax.random.normal(ks[6], (E, H, I), dtype=jnp.float32) * 0.02, 'expert_down_k': jax.random.normal(ks[7], (E, I, H), dtype=jnp.float32) * 0.02}
    _L0_ffn_in = _L0_ffn_setup()

    def _L1_attn_setup():
        import jax, jax.numpy as jnp
        import numpy as np
        import math
        B, N, D = (64, 64, 128)
        SHELL_DIM, RFF_DIM, ORDER = (64, 32, 4)
        CHARGE_COUPLING, SHELL_COUPLING = (1.0, 0.5)
        DIST_COUPLING, DIST_SCALE = (0.3, 10.0)
        COMBINED_DIM = 64

        def _forward(x, W_charge, b_charge, W_shell, b_shell, omega, rff_bias, W_combine, W_v, b_v, W_out, b_out, log_temp):
            b, n, d = x.shape
            q = jnp.tanh(x @ W_charge.T + b_charge)[..., 0]
            coeffs = jnp.asarray([(-CHARGE_COUPLING) ** m / math.factorial(m) for m in range(ORDER + 1)], dtype=x.dtype)
            mags = jnp.sqrt(jnp.abs(coeffs) + 1e-10)
            phi_c = mags * q[..., None] ** jnp.arange(ORDER + 1)
            shell = x @ W_shell.T + b_shell
            shell = shell / jnp.maximum(jnp.linalg.norm(shell, axis=-1, keepdims=True), 1e-12)
            proj = shell @ omega.T + rff_bias
            rff_scale = math.sqrt(2.0 / (2 * RFF_DIM)) * math.sqrt(math.exp(-SHELL_COUPLING))
            phi_s = jnp.concatenate([jnp.cos(proj), jnp.sin(proj)], axis=-1) * rff_scale
            tp = (phi_c[..., :, None] * phi_s[..., None, :]).reshape(b, n, -1)
            phi = tp @ W_combine.T
            idx = jnp.arange(n)
            T = jnp.exp(-DIST_COUPLING * jnp.abs(idx[:, None] - idx[None, :]).astype(x.dtype) / DIST_SCALE)
            temp = jax.nn.softplus(log_temp) + 0.1
            logits = jnp.einsum('bnd,bmd->bnm', phi, phi) * T / temp
            causal = idx[:, None] >= idx[None, :]
            logits = jnp.where(causal, logits, -jnp.inf)
            attn = jax.nn.softmax(logits, axis=-1)
            V = x @ W_v.T + b_v
            out = jnp.einsum('bnm,bmd->bnd', attn, V)
            return out @ W_out.T + b_out
        key = jax.random.key(seed)
        ks = jax.random.split(key, 12)
        s = 0.02
        inp = {'x': jax.random.normal(ks[0], (B, N, D), dtype=jnp.float32), 'W_charge': jax.random.normal(ks[1], (1, D), dtype=jnp.float32) * s, 'b_charge': jnp.zeros((1,), dtype=jnp.float32), 'W_shell': jax.random.normal(ks[2], (SHELL_DIM, D), dtype=jnp.float32) * s, 'b_shell': jnp.zeros((SHELL_DIM,), dtype=jnp.float32), 'omega': jax.random.normal(ks[3], (RFF_DIM, SHELL_DIM), dtype=jnp.float32) * math.sqrt(SHELL_COUPLING), 'rff_bias': jax.random.uniform(ks[4], (RFF_DIM,), dtype=jnp.float32) * (2.0 * math.pi), 'W_combine': jax.random.normal(ks[5], (COMBINED_DIM, (ORDER + 1) * 2 * RFF_DIM), dtype=jnp.float32) * s, 'W_v': jax.random.normal(ks[6], (D, D), dtype=jnp.float32) * s, 'b_v': jnp.zeros((D,), dtype=jnp.float32), 'W_out': jax.random.normal(ks[7], (D, D), dtype=jnp.float32) * s, 'b_out': jnp.zeros((D,), dtype=jnp.float32), 'log_temp': jnp.zeros((), dtype=jnp.float32)}
        return inp
    _L1_attn_in = _L1_attn_setup()

    def _L1_ffn_setup():
        import jax, jax.numpy as jnp
        import numpy as np
        TOP_K = 2
        key = jax.random.key(seed)
        k1, k2, k3, k4 = jax.random.split(key, 4)
        B, S, D = (2, 256, 128)
        E, W = (8, 128)
        x = jax.random.normal(k1, (B, S, D), dtype=jnp.float32)
        router_w = jax.random.normal(k2, (E, D), dtype=jnp.float32) * 0.02
        w1 = jax.random.normal(k3, (D, E * W), dtype=jnp.float32) * 0.02
        w2 = jax.random.normal(k4, (E * W, D), dtype=jnp.float32) * 0.02
        return {'x': x, 'router_w': router_w, 'w1': w1, 'w2': w2}
    _L1_ffn_in = _L1_ffn_setup()

    def _L2_attn_setup():
        import jax, jax.numpy as jnp
        import numpy as np
        DIM = 128
        HEADS = 16
        HEAD_DIM = DIM // HEADS
        B, S = (4, 512)
        key = jax.random.key(seed)
        ks = jax.random.split(key, 8)
        sc = 1.0 / np.sqrt(DIM)
        return {'x': jax.random.normal(ks[0], (B, S, DIM), dtype=jnp.float32), 'Wq': jax.random.normal(ks[1], (DIM, DIM), dtype=jnp.float32) * sc, 'Wk': jax.random.normal(ks[2], (DIM, DIM), dtype=jnp.float32) * sc, 'Wv': jax.random.normal(ks[3], (DIM, DIM), dtype=jnp.float32) * sc, 'Wp': jax.random.normal(ks[4], (DIM, DIM), dtype=jnp.float32) * sc, 'bp': jnp.zeros((DIM,), dtype=jnp.float32), 'conv_w': jax.random.normal(ks[5], (DIM, 3), dtype=jnp.float32) * (1.0 / np.sqrt(3.0)), 'conv_b': jnp.zeros((DIM,), dtype=jnp.float32)}
    _L2_attn_in = _L2_attn_setup()

    def _L2_ffn_setup():
        import jax, jax.numpy as jnp
        import numpy as np
        B, S, D, F, E = (4, 256, 128, 512, 4)
        key = jax.random.key(seed)
        ks = jax.random.split(key, 8)
        sd = 1.0 / np.sqrt(D)
        sf = 1.0 / np.sqrt(F)
        return {'x': jax.random.normal(ks[0], (B, S, D), dtype=jnp.float32), 'W1': jax.random.uniform(ks[1], (E, D, F), jnp.float32, -sd, sd), 'b1': jax.random.uniform(ks[2], (E, F), jnp.float32, -sd, sd), 'W2': jax.random.uniform(ks[3], (E, F, D), jnp.float32, -sf, sf), 'b2': jax.random.uniform(ks[4], (E, D), jnp.float32, -sf, sf), 'Wu': jax.random.uniform(ks[5], (D, 1), jnp.float32, -sd, sd), 'bu': jax.random.uniform(ks[6], (1,), jnp.float32, -sd, sd)}
    _L2_ffn_in = _L2_ffn_setup()

    def _L3_attn_setup():
        import jax, jax.numpy as jnp
        import numpy as np
        B, T, C = (4, 512, 128)

        def wkv_scan(k, v, w, u):
            Bb, Tt, Cc = k.shape
            k_t = jnp.transpose(k, (1, 0, 2))
            v_t = jnp.transpose(v, (1, 0, 2))
            num0 = jnp.zeros((Bb, Cc), dtype=jnp.float32)
            den0 = jnp.zeros((Bb, Cc), dtype=jnp.float32)
            max0 = jnp.full((Bb, Cc), -1e+38, dtype=jnp.float32)

            def step(carry, kv):
                num, den, m = carry
                kk, vv = kv
                mo = jnp.maximum(m, kk + u)
                e1 = jnp.exp(m - mo)
                e2 = jnp.exp(kk + u - mo)
                out = (e1 * num + e2 * vv) / (e1 * den + e2)
                ms = jnp.maximum(m + w, kk)
                e1s = jnp.exp(m + w - ms)
                e2s = jnp.exp(kk - ms)
                return ((e1s * num + e2s * vv, e1s * den + e2s, ms), out)
            _, outs = jax.lax.scan(step, (num0, den0, max0), (k_t, v_t))
            return jnp.transpose(outs, (1, 0, 2))
        key = jax.random.key(seed)
        ks = jax.random.split(key, 10)
        x = jax.random.normal(ks[0], (B, T, C), dtype=jnp.float32)
        Wk = jax.random.normal(ks[1], (C, C), dtype=jnp.float32) * C ** (-0.5)
        Wv = jax.random.normal(ks[2], (C, C), dtype=jnp.float32) * C ** (-0.5)
        Wr = jax.random.normal(ks[3], (C, C), dtype=jnp.float32) * C ** (-0.5)
        Wo = jax.random.normal(ks[4], (C, C), dtype=jnp.float32) * C ** (-0.5)
        time_decay = jax.random.uniform(ks[5], (C,), minval=-6.0, maxval=-5.0, dtype=jnp.float32)
        time_first = jax.random.uniform(ks[6], (C,), minval=-3.0, maxval=0.0, dtype=jnp.float32)
        mix_k = jax.random.uniform(ks[7], (1, 1, C), dtype=jnp.float32)
        mix_v = jax.random.uniform(ks[8], (1, 1, C), dtype=jnp.float32)
        mix_r = jax.random.uniform(ks[9], (1, 1, C), dtype=jnp.float32)
        return {'x': x, 'Wk': Wk, 'Wv': Wv, 'Wr': Wr, 'Wo': Wo, 'time_decay': time_decay, 'time_first': time_first, 'mix_k': mix_k, 'mix_v': mix_v, 'mix_r': mix_r}
    _L3_attn_in = _L3_attn_setup()

    def _L3_ffn_setup():
        import jax, jax.numpy as jnp
        import numpy as np
        import math
        GOLDEN_CENTER = 1.0 / math.e
        GOLDEN_LOWER = 0.5 - math.log(4.0 / 3.0)
        GOLDEN_UPPER = 0.5
        B, T, D = (4, 256, 128)
        E = 8
        I = 512 // (E // 2)

        def _routing_weights(x, Wr, temperature):
            inh = jax.nn.sigmoid(x @ Wr / temperature)
            in_zone = (inh >= GOLDEN_LOWER) & (inh <= GOLDEN_UPPER)
            dist = jnp.abs(inh - GOLDEN_CENTER)
            w = jnp.exp(-dist / 0.1) * in_zone.astype(x.dtype)
            wsum = w.sum(axis=-1, keepdims=True)
            no_expert = wsum < 1e-08
            fb = jnp.exp(-dist / 0.3)
            _, top2 = jax.lax.top_k(fb, 2)
            fb_mask = jax.nn.one_hot(top2, E, dtype=x.dtype).sum(axis=-2)
            fb_w = fb * fb_mask
            fb_w = fb_w / jnp.clip(fb_w.sum(axis=-1, keepdims=True), 1e-08)
            w = jnp.where(no_expert, fb_w, w)
            wsum = w.sum(axis=-1, keepdims=True)
            return w / jnp.clip(wsum, 1e-08)
        key = jax.random.key(seed)
        k = jax.random.split(key, 6)
        s_d = 1.0 / math.sqrt(D)
        s_i = 1.0 / math.sqrt(I)
        return {'x': jax.random.normal(k[0], (B, T, D), jnp.float32), 'Wg': jax.random.normal(k[1], (E, D, I), jnp.float32) * s_d, 'Wu': jax.random.normal(k[2], (E, D, I), jnp.float32) * s_d, 'Wd': jax.random.normal(k[3], (E, I, D), jnp.float32) * s_i, 'Wr': jax.random.normal(k[4], (D, E), jnp.float32) * s_d, 'temperature': jnp.ones((1,), jnp.float32)}
    _L3_ffn_in = _L3_ffn_setup()
    _d = {'L0_attn_x': _L0_attn_in['x'], 'L0_attn_norm_w': _L0_attn_in['norm_w'], 'L0_attn_Win': _L0_attn_in['Win'], 'L0_attn_b_in': _L0_attn_in['b_in'], 'L0_attn_conv_w': _L0_attn_in['conv_w'], 'L0_attn_conv_b': _L0_attn_in['conv_b'], 'L0_attn_A': _L0_attn_in['A'], 'L0_attn_Bm': _L0_attn_in['Bm'], 'L0_attn_Cm': _L0_attn_in['Cm'], 'L0_attn_Wout': _L0_attn_in['Wout'], 'L0_attn_b_out': _L0_attn_in['b_out'], 'L0_ffn_router_w': _L0_ffn_in['router_w'], 'L0_ffn_shared_gate_w': _L0_ffn_in['shared_gate_w'], 'L0_ffn_shared_up_w': _L0_ffn_in['shared_up_w'], 'L0_ffn_shared_down_w': _L0_ffn_in['shared_down_w'], 'L0_ffn_expert_gate_k': _L0_ffn_in['expert_gate_k'], 'L0_ffn_expert_up_k': _L0_ffn_in['expert_up_k'], 'L0_ffn_expert_down_k': _L0_ffn_in['expert_down_k'], 'L1_attn_W_charge': _L1_attn_in['W_charge'], 'L1_attn_b_charge': _L1_attn_in['b_charge'], 'L1_attn_W_shell': _L1_attn_in['W_shell'], 'L1_attn_b_shell': _L1_attn_in['b_shell'], 'L1_attn_omega': _L1_attn_in['omega'], 'L1_attn_rff_bias': _L1_attn_in['rff_bias'], 'L1_attn_W_combine': _L1_attn_in['W_combine'], 'L1_attn_W_v': _L1_attn_in['W_v'], 'L1_attn_b_v': _L1_attn_in['b_v'], 'L1_attn_W_out': _L1_attn_in['W_out'], 'L1_attn_b_out': _L1_attn_in['b_out'], 'L1_attn_log_temp': _L1_attn_in['log_temp'], 'L1_ffn_router_w': _L1_ffn_in['router_w'], 'L1_ffn_w1': _L1_ffn_in['w1'], 'L1_ffn_w2': _L1_ffn_in['w2'], 'L2_attn_Wq': _L2_attn_in['Wq'], 'L2_attn_Wk': _L2_attn_in['Wk'], 'L2_attn_Wv': _L2_attn_in['Wv'], 'L2_attn_Wp': _L2_attn_in['Wp'], 'L2_attn_bp': _L2_attn_in['bp'], 'L2_attn_conv_w': _L2_attn_in['conv_w'], 'L2_attn_conv_b': _L2_attn_in['conv_b'], 'L2_ffn_W1': _L2_ffn_in['W1'], 'L2_ffn_b1': _L2_ffn_in['b1'], 'L2_ffn_W2': _L2_ffn_in['W2'], 'L2_ffn_b2': _L2_ffn_in['b2'], 'L2_ffn_Wu': _L2_ffn_in['Wu'], 'L2_ffn_bu': _L2_ffn_in['bu'], 'L3_attn_Wk': _L3_attn_in['Wk'], 'L3_attn_Wv': _L3_attn_in['Wv'], 'L3_attn_Wr': _L3_attn_in['Wr'], 'L3_attn_Wo': _L3_attn_in['Wo'], 'L3_attn_time_decay': _L3_attn_in['time_decay'], 'L3_attn_time_first': _L3_attn_in['time_first'], 'L3_attn_mix_k': _L3_attn_in['mix_k'], 'L3_attn_mix_v': _L3_attn_in['mix_v'], 'L3_attn_mix_r': _L3_attn_in['mix_r'], 'L3_ffn_Wg': _L3_ffn_in['Wg'], 'L3_ffn_Wu': _L3_ffn_in['Wu'], 'L3_ffn_Wd': _L3_ffn_in['Wd'], 'L3_ffn_Wr': _L3_ffn_in['Wr'], 'L3_ffn_temperature': _L3_ffn_in['temperature']}
    _x0 = _d['L0_attn_x']
    _d['L0_attn_x'] = jax.random.normal(jax.random.fold_in(jax.random.key(seed), 1), (16, 256, 128), dtype=_x0.dtype)
    del _x0
    return _d

def reference(L0_attn_x, L0_attn_norm_w, L0_attn_Win, L0_attn_b_in, L0_attn_conv_w, L0_attn_conv_b, L0_attn_A, L0_attn_Bm, L0_attn_Cm, L0_attn_Wout, L0_attn_b_out, L0_ffn_router_w, L0_ffn_shared_gate_w, L0_ffn_shared_up_w, L0_ffn_shared_down_w, L0_ffn_expert_gate_k, L0_ffn_expert_up_k, L0_ffn_expert_down_k, L1_attn_W_charge, L1_attn_b_charge, L1_attn_W_shell, L1_attn_b_shell, L1_attn_omega, L1_attn_rff_bias, L1_attn_W_combine, L1_attn_W_v, L1_attn_b_v, L1_attn_W_out, L1_attn_b_out, L1_attn_log_temp, L1_ffn_router_w, L1_ffn_w1, L1_ffn_w2, L2_attn_Wq, L2_attn_Wk, L2_attn_Wv, L2_attn_Wp, L2_attn_bp, L2_attn_conv_w, L2_attn_conv_b, L2_ffn_W1, L2_ffn_b1, L2_ffn_W2, L2_ffn_b2, L2_ffn_Wu, L2_ffn_bu, L3_attn_Wk, L3_attn_Wv, L3_attn_Wr, L3_attn_Wo, L3_attn_time_decay, L3_attn_time_first, L3_attn_mix_k, L3_attn_mix_v, L3_attn_mix_r, L3_ffn_Wg, L3_ffn_Wu, L3_ffn_Wd, L3_ffn_Wr, L3_ffn_temperature):

    def _L0_attn_ref(x, norm_w, Win, b_in, conv_w, conv_b, A, Bm, Cm, Wout, b_out):
        import jax, jax.numpy as jnp
        import numpy as np
        D_MODEL = 128
        EXP = 2
        D_IN = D_MODEL * EXP
        D_STATE = 16
        CONV_D = 4
        BATCH = 4
        SEQ = 256

        def _rmsnorm(x, w, eps=1e-06):
            return x * jax.lax.rsqrt(jnp.mean(x * x, axis=-1, keepdims=True) + eps) * w
        res = x
        h = _rmsnorm(x, norm_w)
        u = h @ Win + b_in
        u = u.transpose(0, 2, 1)
        u = jax.lax.conv_general_dilated(u, conv_w, window_strides=(1,), padding=[(CONV_D - 1, 0)], feature_group_count=D_IN, dimension_numbers=('NCH', 'OIH', 'NCH')) + conv_b[None, :, None]
        u = u.transpose(0, 2, 1)
        Bv = Bm[:, :, 0]
        Cv = Cm[:, 0, :]

        def step(hc, u_t):
            hc = jnp.einsum('bdr,drs->bds', hc, A) + u_t[:, :, None] * Bv[None]
            y = jnp.einsum('bds,ds->bd', hc, Cv)
            return (hc, y)
        h0 = jnp.zeros((x.shape[0], D_IN, D_STATE), u.dtype)
        _, ys = jax.lax.scan(step, h0, u.transpose(1, 0, 2))
        y = ys.transpose(1, 0, 2)
        return y @ Wout + b_out + res

    def _L0_ffn_ref(hidden_states, router_w, shared_gate_w, shared_up_w, shared_down_w, expert_gate_k, expert_up_k, expert_down_k):
        import jax, jax.numpy as jnp
        import numpy as np
        B, S, H, I, E, K = (2, 64, 128, 64, 64, 8)
        logits = jnp.einsum('bsh,he->bse', hidden_states.astype(jnp.float32), router_w)
        affinity = jax.nn.sigmoid(logits)
        top_scores, top_idx = jax.lax.top_k(affinity, K)
        top_w = top_scores / (jnp.sum(top_scores, axis=-1, keepdims=True) + 1e-09)
        one_hot = jax.nn.one_hot(top_idx, E, dtype=top_w.dtype)
        router_mask = jnp.einsum('bske,bsk->bse', one_hot, top_w).astype(hidden_states.dtype)
        shared = jnp.einsum('bsi,ih->bsh', jax.nn.silu(hidden_states @ shared_gate_w) * (hidden_states @ shared_up_w), shared_down_w)
        gate_out = jnp.einsum('bsh,ehi->bsei', hidden_states, expert_gate_k)
        up_out = jnp.einsum('bsh,ehi->bsei', hidden_states, expert_up_k)
        expert_act = jax.nn.silu(gate_out) * up_out
        routed = jnp.einsum('bsei,eih->bsh', expert_act * router_mask[..., None], expert_down_k)
        return shared + routed

    def _L1_attn_ref(x, W_charge, b_charge, W_shell, b_shell, omega, rff_bias, W_combine, W_v, b_v, W_out, b_out, log_temp):
        import jax, jax.numpy as jnp
        import numpy as np
        import math
        B, N, D = (64, 64, 128)
        SHELL_DIM, RFF_DIM, ORDER = (64, 32, 4)
        CHARGE_COUPLING, SHELL_COUPLING = (1.0, 0.5)
        DIST_COUPLING, DIST_SCALE = (0.3, 10.0)
        COMBINED_DIM = 64

        def _forward(x, W_charge, b_charge, W_shell, b_shell, omega, rff_bias, W_combine, W_v, b_v, W_out, b_out, log_temp):
            b, n, d = x.shape
            q = jnp.tanh(x @ W_charge.T + b_charge)[..., 0]
            coeffs = jnp.asarray([(-CHARGE_COUPLING) ** m / math.factorial(m) for m in range(ORDER + 1)], dtype=x.dtype)
            mags = jnp.sqrt(jnp.abs(coeffs) + 1e-10)
            phi_c = mags * q[..., None] ** jnp.arange(ORDER + 1)
            shell = x @ W_shell.T + b_shell
            shell = shell / jnp.maximum(jnp.linalg.norm(shell, axis=-1, keepdims=True), 1e-12)
            proj = shell @ omega.T + rff_bias
            rff_scale = math.sqrt(2.0 / (2 * RFF_DIM)) * math.sqrt(math.exp(-SHELL_COUPLING))
            phi_s = jnp.concatenate([jnp.cos(proj), jnp.sin(proj)], axis=-1) * rff_scale
            tp = (phi_c[..., :, None] * phi_s[..., None, :]).reshape(b, n, -1)
            phi = tp @ W_combine.T
            idx = jnp.arange(n)
            T = jnp.exp(-DIST_COUPLING * jnp.abs(idx[:, None] - idx[None, :]).astype(x.dtype) / DIST_SCALE)
            temp = jax.nn.softplus(log_temp) + 0.1
            logits = jnp.einsum('bnd,bmd->bnm', phi, phi) * T / temp
            causal = idx[:, None] >= idx[None, :]
            logits = jnp.where(causal, logits, -jnp.inf)
            attn = jax.nn.softmax(logits, axis=-1)
            V = x @ W_v.T + b_v
            out = jnp.einsum('bnm,bmd->bnd', attn, V)
            return out @ W_out.T + b_out
        return _forward(x, W_charge, b_charge, W_shell, b_shell, omega, rff_bias, W_combine, W_v, b_v, W_out, b_out, log_temp)

    def _L1_ffn_ref(x, router_w, w1, w2):
        import jax, jax.numpy as jnp
        import numpy as np
        TOP_K = 2
        B, S, D = x.shape
        E = router_w.shape[0]
        W = w1.shape[1] // E
        T = B * S
        xf = x.reshape(T, D)
        router_logits = jnp.einsum('td,ed->te', xf, router_w)
        router_probs = jax.nn.sigmoid(router_logits.astype(jnp.float32))
        top_w, sel = jax.lax.top_k(router_probs, TOP_K)
        top_w = top_w / (top_w.sum(axis=-1, keepdims=True) + 1e-20)
        top_w = top_w.astype(x.dtype)
        W1e = w1.reshape(D, E, W).transpose(1, 0, 2)
        W2e = w2.reshape(E, W, D)
        h = jnp.einsum('td,edw->etw', xf, W1e)
        a = jnp.square(jax.nn.relu(h))
        y = jnp.einsum('etw,ewd->etd', a, W2e)
        cw = jnp.zeros((T, E), dtype=x.dtype).at[jnp.arange(T)[:, None], sel].set(top_w)
        out = jnp.einsum('etd,te->td', y, cw)
        return out.reshape(B, S, D)

    def _L2_attn_ref(x, Wq, Wk, Wv, Wp, bp, conv_w, conv_b):
        import jax, jax.numpy as jnp
        import numpy as np
        DIM = 128
        HEADS = 16
        HEAD_DIM = DIM // HEADS
        B, S = (4, 512)
        b, s, d = x.shape

        def split_heads(t):
            return t.reshape(b, s, HEADS, HEAD_DIM).transpose(0, 2, 1, 3)
        q = split_heads(x @ Wq.T)
        k = split_heads(x @ Wk.T)
        v = split_heads(x @ Wv.T)
        q = jax.nn.elu(q) + 1.0
        k = jax.nn.elu(k) + 1.0
        kv_state = jnp.einsum('bhnd,bhne->bhde', k, v)
        k_state = k.sum(axis=2)
        attn_out = jnp.einsum('bhnd,bhde->bhne', q, kv_state)
        denom = jnp.maximum(jnp.einsum('bhnd,bhd->bhn', q, k_state), 1e-06)[..., None]
        attn_out = (attn_out / denom).transpose(0, 2, 1, 3).reshape(b, s, d)
        xp = jnp.pad(x, ((0, 0), (1, 1), (0, 0)))
        local = xp[:, :-2, :] * conv_w[:, 0] + xp[:, 1:-1, :] * conv_w[:, 1] + xp[:, 2:, :] * conv_w[:, 2] + conv_b
        return (attn_out + local) @ Wp.T + bp

    def _L2_ffn_ref(x, W1, b1, W2, b2, Wu, bu):
        import jax, jax.numpy as jnp
        import numpy as np
        B, S, D, F, E = (4, 256, 128, 512, 4)
        n_exp = W1.shape[0]
        seq = x.shape[1]
        u = jax.nn.sigmoid(jnp.einsum('bsd,do->bso', x, Wu) + bu)[..., 0]
        k = jnp.clip(jnp.ceil(u * n_exp), 1, n_exp).astype(jnp.int32)
        h = jax.nn.relu(jnp.einsum('bsd,edf->bsef', x, W1) + b1)
        y = jnp.einsum('bsef,efd->bsed', h, W2) + b2
        s_idx = jnp.arange(seq)
        out = jnp.zeros_like(x)
        for i in range(1, n_exp + 1):
            e_idx = (s_idx + i - 1) % n_exp
            y_i = jnp.take_along_axis(y, e_idx[None, :, None, None], axis=2)[:, :, 0, :]
            w = jnp.where(k >= i, u / i, 0.0)
            out = out + w[..., None] * y_i
        return out

    def _L3_attn_ref(x, Wk, Wv, Wr, Wo, time_decay, time_first, mix_k, mix_v, mix_r):
        import jax, jax.numpy as jnp
        import numpy as np
        B, T, C = (4, 512, 128)

        def wkv_scan(k, v, w, u):
            Bb, Tt, Cc = k.shape
            k_t = jnp.transpose(k, (1, 0, 2))
            v_t = jnp.transpose(v, (1, 0, 2))
            num0 = jnp.zeros((Bb, Cc), dtype=jnp.float32)
            den0 = jnp.zeros((Bb, Cc), dtype=jnp.float32)
            max0 = jnp.full((Bb, Cc), -1e+38, dtype=jnp.float32)

            def step(carry, kv):
                num, den, m = carry
                kk, vv = kv
                mo = jnp.maximum(m, kk + u)
                e1 = jnp.exp(m - mo)
                e2 = jnp.exp(kk + u - mo)
                out = (e1 * num + e2 * vv) / (e1 * den + e2)
                ms = jnp.maximum(m + w, kk)
                e1s = jnp.exp(m + w - ms)
                e2s = jnp.exp(kk - ms)
                return ((e1s * num + e2s * vv, e1s * den + e2s, ms), out)
            _, outs = jax.lax.scan(step, (num0, den0, max0), (k_t, v_t))
            return jnp.transpose(outs, (1, 0, 2))
        prev_x = jnp.pad(x, ((0, 0), (1, 0), (0, 0)))[:, :-1, :]
        r_in = x * mix_r + prev_x * (1.0 - mix_r)
        k_in = x * mix_k + prev_x * (1.0 - mix_k)
        v_in = x * mix_v + prev_x * (1.0 - mix_v)
        receptance = jnp.einsum('btc,dc->btd', r_in, Wr)
        key = jnp.einsum('btc,dc->btd', k_in, Wk)
        value = jnp.einsum('btc,dc->btd', v_in, Wv)
        w = -jnp.exp(time_decay)
        u = time_first
        wkv_out = wkv_scan(key, value, w, u)
        rwkv = jax.nn.sigmoid(receptance) * wkv_out
        return jnp.einsum('btc,dc->btd', rwkv, Wo)

    def _L3_ffn_ref(x, Wg, Wu, Wd, Wr, temperature):
        import jax, jax.numpy as jnp
        import numpy as np
        import math
        GOLDEN_CENTER = 1.0 / math.e
        GOLDEN_LOWER = 0.5 - math.log(4.0 / 3.0)
        GOLDEN_UPPER = 0.5
        B, T, D = (4, 256, 128)
        E = 8
        I = 512 // (E // 2)

        def _routing_weights(x, Wr, temperature):
            inh = jax.nn.sigmoid(x @ Wr / temperature)
            in_zone = (inh >= GOLDEN_LOWER) & (inh <= GOLDEN_UPPER)
            dist = jnp.abs(inh - GOLDEN_CENTER)
            w = jnp.exp(-dist / 0.1) * in_zone.astype(x.dtype)
            wsum = w.sum(axis=-1, keepdims=True)
            no_expert = wsum < 1e-08
            fb = jnp.exp(-dist / 0.3)
            _, top2 = jax.lax.top_k(fb, 2)
            fb_mask = jax.nn.one_hot(top2, E, dtype=x.dtype).sum(axis=-2)
            fb_w = fb * fb_mask
            fb_w = fb_w / jnp.clip(fb_w.sum(axis=-1, keepdims=True), 1e-08)
            w = jnp.where(no_expert, fb_w, w)
            wsum = w.sum(axis=-1, keepdims=True)
            return w / jnp.clip(wsum, 1e-08)
        weights = _routing_weights(x, Wr, temperature)
        gate = jnp.einsum('btd,edi->beti', x, Wg)
        up = jnp.einsum('btd,edi->beti', x, Wu)
        h = jax.nn.silu(gate) * up
        e_out = jnp.einsum('beti,eid->betd', h, Wd)
        out = jnp.einsum('bte,betd->btd', weights, e_out)
        return out
    x = L0_attn_x
    x = x + _L0_attn_ref(_layernorm(x, axis=-1), L0_attn_norm_w, L0_attn_Win, L0_attn_b_in, L0_attn_conv_w, L0_attn_conv_b, L0_attn_A, L0_attn_Bm, L0_attn_Cm, L0_attn_Wout, L0_attn_b_out)
    x = x + _L0_ffn_ref(_layernorm(x, axis=-1), L0_ffn_router_w, L0_ffn_shared_gate_w, L0_ffn_shared_up_w, L0_ffn_shared_down_w, L0_ffn_expert_gate_k, L0_ffn_expert_up_k, L0_ffn_expert_down_k)
    x = x + _L1_attn_ref(_layernorm(x, axis=-1), L1_attn_W_charge, L1_attn_b_charge, L1_attn_W_shell, L1_attn_b_shell, L1_attn_omega, L1_attn_rff_bias, L1_attn_W_combine, L1_attn_W_v, L1_attn_b_v, L1_attn_W_out, L1_attn_b_out, L1_attn_log_temp)
    x = x + _L1_ffn_ref(_layernorm(x, axis=-1), L1_ffn_router_w, L1_ffn_w1, L1_ffn_w2)
    x = x + _L2_attn_ref(_layernorm(x, axis=-1), L2_attn_Wq, L2_attn_Wk, L2_attn_Wv, L2_attn_Wp, L2_attn_bp, L2_attn_conv_w, L2_attn_conv_b)
    x = x + _L2_ffn_ref(_layernorm(x, axis=-1), L2_ffn_W1, L2_ffn_b1, L2_ffn_W2, L2_ffn_b2, L2_ffn_Wu, L2_ffn_bu)
    x = x + _L3_attn_ref(_layernorm(x, axis=-1), L3_attn_Wk, L3_attn_Wv, L3_attn_Wr, L3_attn_Wo, L3_attn_time_decay, L3_attn_time_first, L3_attn_mix_k, L3_attn_mix_v, L3_attn_mix_r)
    x = x + _L3_ffn_ref(_layernorm(x, axis=-1), L3_ffn_Wg, L3_ffn_Wu, L3_ffn_Wd, L3_ffn_Wr, L3_ffn_temperature)
    return x

_drawn_inputs = setup_inputs


def setup_inputs(seed=0):
    import zlib

    import numpy as np

    out = dict(_drawn_inputs(seed))
    spreads = {'L0_attn_norm_w': (1.0, 0.2),
     'L0_attn_b_in': (0.0, 0.1),
     'L0_attn_conv_b': (0.0, 0.1),
     'L0_attn_b_out': (0.0, 0.37),
     'L1_attn_b_shell': (0.0, 0.8),
     'L1_attn_b_v': (0.0, 0.8),
     'L1_attn_b_out': (0.0, 0.367),
     'L2_attn_bp': (0.0, 0.379),
     'L2_attn_conv_b': (0.0, 0.358)}
    factors = {'L0_ffn_router_w': 8.0,
     'L0_ffn_shared_gate_w': 8.0,
     'L0_ffn_shared_up_w': 8.0,
     'L0_ffn_shared_down_w': 8.0,
     'L0_ffn_expert_gate_k': 8.0,
     'L0_ffn_expert_up_k': 8.0,
     'L0_ffn_expert_down_k': 8.0,
     'L1_attn_W_charge': 8.0,
     'L1_attn_W_shell': 8.0,
     'L1_attn_omega': 8.0,
     'L1_attn_rff_bias': 8.0,
     'L1_attn_W_combine': 8.0,
     'L1_attn_W_v': 8.0,
     'L1_attn_W_out': 8.0,
     'L1_ffn_router_w': 8.0,
     'L1_ffn_w1': 8.0,
     'L1_ffn_w2': 8.0,
     'L2_attn_Wq': 8.0,
     'L2_attn_Wk': 5.923,
     'L2_ffn_b1': 8.0,
     'L2_ffn_b2': 8.0,
     'L2_ffn_Wu': 5.607,
     'L3_attn_Wk': 4.266,
     'L3_attn_Wr': 5.651,
     'L3_attn_time_decay': 8.0,
     'L3_attn_time_first': 8.0,
     'L3_attn_mix_k': 8.0,
     'L3_attn_mix_v': 8.0,
     'L3_attn_mix_r': 8.0}
    for name, (base, spread) in spreads.items():
        noise = np.random.default_rng([zlib.crc32(name.encode()), seed]).standard_normal(out[name].shape)
        drawn = base * np.exp(spread * noise) if base else spread * noise
        out[name] = jnp.asarray(drawn.astype(out[name].dtype))
    for name, factor in factors.items():
        out[name] = (out[name] * factor).astype(out[name].dtype)
    return out
```

```python
from contextlib import ExitStack

import concourse.bass as bass
from concourse import mybir

F32 = mybir.dt.float32
F32R = mybir.dt.float32r
BF16 = mybir.dt.bfloat16
ALU = mybir.AluOpType
ACT = mybir.ActivationFunctionType
AX_X = mybir.AxisListType.X

P = 128
BATCH, SEQ, D = 16, 256, 128
TOKENS = BATCH * SEQ
TILES = TOKENS // P
GROUP = 512
GROUPS = TOKENS // GROUP
GT = GROUP // P
GB = GROUP // SEQ
PADDED = SEQ + 2
GCOLS = GB * PADDED
EPS = 1e-5


class Chip:

    def __init__(self, nc, io, stack):
        self.nc, self.io, self.stack = nc, io, stack
        self.turn0 = 0

    def sb(self, name, shape, dt=F32, stack=None):
        return (stack or self.stack).enter_context(self.nc.sbuf_tensor(name, shape, dt))

    def ps(self, name, shape=(P, 512), dt=F32, stack=None):
        return (stack or self.stack).enter_context(self.nc.psum_tensor(name, list(shape), dt))

    def sem(self, name, stack=None):
        return (stack or self.stack).enter_context(self.nc.semaphore(name))


def share(k):
    k.x = k.sb("x", [P, TILES, D])
    k.xh = k.sb("xn_hi", [P, BATCH * PADDED], F32R)
    k.xl = k.sb("xn_lo", [P, BATCH * PADDED], F32R)
    k.ident = k.sb("ident", [P, P])
    k.identb = k.sb("identb", [P, P], BF16)
    k.half_neg = k.sb("half_neg", [P, 1])
    k.eps = k.sb("eps", [P, 1])
    k.tick = k.sb("tick", [P, 1])
    k.yT = k.sb("y_features", [P, GROUP])
    k.stats = k.sb("ln_stats", [P, GT, 6])
    k.moments = k.sb("ln_moments", [P, GT, 2])
    k.var = k.sb("ln_var", [P, GT])
    k.rstd = k.sb("ln_rstd", [P, GT])
    k.xn = k.sb("xn_tokens", [P, GT, D])
    k.ypsum = k.ps("ypsum")
    k.turn = k.ps("turn")
    k.consts_done = k.sem("consts_done")
    k.pads_done = k.sem("pads_done")
    k.y_done = k.sem("y_done")
    k.y_copied = k.sem("y_copied")
    k.y_turned = k.sem("y_turned")
    k.x_done = k.sem("x_done")
    k.stats_done = k.sem("stats_done")
    k.moments_done = k.sem("moments_done")
    k.var_done = k.sem("var_done")
    k.rstd_done = k.sem("rstd_done")
    k.xn_done = k.sem("xn_done")
    k.xn_turned = k.sem("xn_turned")
    k.hi_done = k.sem("hi_done")
    k.lo_done = k.sem("lo_done")
    k.stored = k.sem("stored")


def lo_hi(k, g):
    def view(t, shift=0):
        v = t[:, bass.ds(g * GCOLS, GCOLS)].rearrange("p (b s) -> p b s", b=GB)
        return v[:, :, 1 + shift:1 + shift + SEQ]
    return view


def mm3(pe, out, w_hi, w_lo, x_hi, x_lo, start=True, stop=True):
    pe.matmul(out, w_hi, x_hi, start=start, stop=False)
    pe.matmul(out, w_hi, x_lo, start=False, stop=False)
    return pe.matmul(out, w_lo, x_hi, start=False, stop=stop)


def build_constants(k):
    nc = k.nc
    with nc.Block() as block:
        @block.gpsimd
        def _(pool):
            pool.memset(k.ident[:, :], 0.0).then_inc(k.consts_done, 1)
            pool.memset(k.half_neg[:, :], -0.5).then_inc(k.consts_done, 1)
            pool.memset(k.eps[:, :], EPS).then_inc(k.consts_done, 1)
            pool.wait_ge(k.consts_done, 3)
            pool.affine_select(out=k.ident[:, :], in_=k.ident[:, :], compare_op=ALU.not_equal, fill=1.0,
                               base=0, pattern=[[-1, P]], channel_multiplier=1).then_inc(k.consts_done, 1)
            pool.wait_ge(k.consts_done, 4)
            pool.tensor_copy(k.identb[:, :], k.ident[:, :]).then_inc(k.consts_done, 1)

        @block.vector
        def _(dve):
            for t in (k.xh, k.xl):
                v = t[:, :].rearrange("p (b s) -> p b s", b=BATCH)
                dve.memset(v[:, :, 0:PADDED:PADDED - 1].bitcast(F32), 0.0).then_inc(k.pads_done, 1)



def post_add_scalar(k, act, n, bias):
    act.wait_ge(k.y_done, n + 1)
    if bias is None:
        act.activation(k.yT[:, :], k.ypsum[:, :], ACT.Copy).then_inc(k.y_copied, 1)
    else:
        act.activation(k.yT[:, :], k.ypsum[:, :], ACT.Identity, bias=bias).then_inc(k.y_copied, 1)


def post_add_tensor(k, pe, n):
    pe.wait_ge(k.y_copied, n + 1)
    if not isinstance(n, int) or n > 0:
        pe.wait_ge(k.lo_done, n)
    for j in range(GT):
        last = pe.transpose(k.turn[:, j * P:(j + 1) * P], k.yT[:, j * P:(j + 1) * P], k.ident[:, :])
    last.then_inc(k.y_turned, 1)


def post_add_vector(k, dve, n, g):
    x = k.x[:, bass.ds(g * GT, GT), :]
    dve.wait_ge(k.y_turned, n + 1)
    dve.tensor_tensor(x, x, k.turn[:, :].rearrange("p (j d) -> p j d", j=GT), ALU.add).then_inc(k.x_done, 1)


def post_norm_vector(k, dve, n, g):
    dve.wait_ge(k.x_done, n + 1)
    dve.memset(k.tick[:, :], 0.0)
    for j in range(GT):
        last = dve.bn_stats(k.stats[:, j, :], k.x[:, bass.ds(g * GT + j, 1), :].rearrange("p a d -> p (a d)"))
    last.then_inc(k.stats_done, 1)
    dve.wait_ge(k.stats_done, n + 1)
    dve.memset(k.tick[:, :], 0.0)
    for j in range(GT):
        last = dve.bn_aggr(k.moments[:, j, :], k.stats[:, j, :])
    last.then_inc(k.moments_done, 1)
    dve.wait_ge(k.moments_done, n + 1)
    dve.wait_ge(k.rstd_done, n + 1)
    for j in range(GT):
        last = dve.tensor_scalar(k.xn[:, j, :], k.x[:, bass.ds(g * GT + j, 1), :].rearrange("p a d -> p (a d)"),
                                 k.moments[:, j, 0:1], k.rstd[:, j:j + 1], ALU.subtract, ALU.mult)
    last.then_inc(k.xn_done, 1)


def post_norm_gpsimd(k, pool, n):
    pool.wait_ge(k.moments_done, n + 1)
    pool.tensor_tensor(k.var[:, :], k.moments[:, :, 1], k.eps[:, 0:1].to_broadcast([P, GT]), ALU.add).then_inc(k.var_done, 1)
    pool.wait_ge(k.var_done, n + 1)
    pool.tensor_tensor(k.rstd[:, :], k.var[:, :], k.half_neg[:, 0:1].to_broadcast([P, GT]), ALU.pow)\
        .then_inc(k.rstd_done, 1)


def post_turn_tensor(k, pe, n):
    pe.wait_ge(k.xn_done, n + 1)
    for j in range(GT):
        last = pe.transpose(k.turn[:, j * P:(j + 1) * P], k.xn[:, j, :], k.ident[:, :])
    last.then_inc(k.xn_turned, 1)


def post_turn_scalar(k, act, n, g):
    act.wait_ge(k.xn_turned, n + 1)
    act.activation(lo_hi(k, g)(k.xh), k.turn[:, :].rearrange("p (b s) -> p b s", b=GB), ACT.Copy)\
        .then_inc(k.hi_done, 1)


def post_turn_vector(k, dve, n, g):
    dve.wait_ge(k.hi_done, n + 1)
    view = lo_hi(k, g)
    dve.tensor_tensor(view(k.xl), k.turn[:, :].rearrange("p (b s) -> p b s", b=GB), view(k.xh).bitcast(F32),
                      ALU.subtract).then_inc(k.lo_done, 1)



class Route:

    def __init__(self, kind, experts, index):
        self.kind, self.e, self.index = kind, experts, index
        self.halves = 2 if experts == 64 else 1
        self.rows = 3 * experts // self.halves
        self.logits = 1 if kind == "steps" else experts


class Chain:

    def __init__(self, eng, sem, base):
        self.eng, self.sem, self.base, self.n = eng, sem, base, 0

    def then(self, instruction):
        self.n += 1
        instruction.then_inc(self.sem, 1)
        self.eng.wait_ge(self.sem, self.base + self.n)


ROUTE_LINKS = {"top8": 9, "top2": 12, "steps": 7, "zone": 25}


def share_routes(k):
    k.logT = k.sb("logits_experts", [P, GROUP])
    k.aff = k.sb("affinity", [P, GT, 64])
    k.best = k.sb("best8", [P, GT, 8])
    k.rep = k.sb("best_marked", [P, GT, 64])
    k.sel = k.sb("selected", [P, GT, 64])
    k.tot = k.sb("selected_sum", [P, GT])
    k.inv = k.sb("selected_inverse", [P, GT])
    k.parts = k.sb("weights_bf16", [P, GT, 192], BF16)
    k.rest = k.sb("weights_rest", [P, GT, 64])
    k.w = k.sb("weights", [P, GT, 64])
    k.pair = k.sb("pairs", [P, 2, GT, 64])
    k.rank = k.sb("rank", [P, GT, 8])
    k.exps = k.sb("zone_exps", [P, 2, GT, 8])
    k.zone = k.sb("zone_parts", [P, 4, GT, 8])
    k.small = k.sb("zone_sums", [P, 4, GT])
    k.mask = k.sb("mask", [96, 2, TOKENS], BF16)
    k.lower = k.sb("lower8", [P, 8, 8])
    k.mod4 = k.sb("mod4", [P, 4])
    k.turn4 = k.sb("step_expert", [P, 4, 4])
    k.sel64 = k.sb("sel64", [96, 16, P], BF16)
    k.sel8 = k.sb("sel8", [24, 8, P], BF16)
    k.sel4 = k.sb("sel4", [12, 4, P], BF16)
    k.logits_done = k.sem("logits_done")
    k.logits_copied = k.sem("logits_copied")
    k.logits_turned = k.sem("logits_turned")
    k.aff_done = k.sem("aff_done")
    k.dist_done = k.sem("dist_done")
    k.exps_done = k.sem("exps_done")
    k.route_link = k.sem("route_link")
    k.parts_done = k.sem("parts_done")
    k.parts_turned = k.sem("parts_turned")
    k.masks_done = k.sem("masks_done")
    k.tables_done = k.sem("tables_done")
    k.tables_link = k.sem("tables_link")
    k.params_in = k.sem("params_in")
    k.params_done = k.sem("params_done")
    k.route_base = 0


def build_tables(k):
    with k.nc.Block() as block:
        @block.gpsimd
        def _(pool):
            link = Chain(pool, k.tables_link, 0)
            link.then(pool.memset(k.sel64[:, :, :], 0.0))
            link.then(pool.memset(k.sel8[:, :, :], 0.0))
            link.then(pool.memset(k.sel4[:, :, :], 0.0))
            link.then(pool.memset(k.lower[:, :, :], 1.0))
            for part in range(3):
                link.then(pool.affine_select(
                    out=k.sel64[:, :, :].rearrange("p c (e i) -> p c e i", e=2),
                    in_=k.sel64[:, :, :].rearrange("p c (e i) -> p c e i", e=2), compare_op=ALU.not_equal,
                    fill=1.0, base=-32 * part, pattern=[[-2, 16], [-1, 2], [0, 64]], channel_multiplier=1))
                link.then(pool.affine_select(
                    out=k.sel8[:, :, :], in_=k.sel8[:, :, :], compare_op=ALU.not_equal, fill=1.0,
                    base=-8 * part, pattern=[[-1, 8], [0, P]], channel_multiplier=1))
                link.then(pool.affine_select(
                    out=k.sel4[:, :, :], in_=k.sel4[:, :, :], compare_op=ALU.not_equal, fill=1.0,
                    base=-4 * part, pattern=[[-1, 4], [0, P]], channel_multiplier=1))
            link.then(pool.affine_select(out=k.lower[:, :, :], in_=k.lower[:, :, :], compare_op=ALU.is_gt,
                                         fill=0.0, base=0, pattern=[[1, 8], [-1, 8]], channel_multiplier=0))

        @block.vector
        def _(dve):
            dve.memset(k.logT[:, :], 0.0).then_inc(k.tables_done, 1)
            dve.tensor_reduce(k.mod4[:, :], k.ident[:, :].rearrange("p (q m) -> p m q", m=4), AX_X, ALU.add)\
                .then_inc(k.tables_done, 1)
            dve.wait_ge(k.tables_done, 2)
            for e in range(4):
                for i in range(4):
                    m = (e - i) % 4
                    dve.tensor_copy(k.turn4[:, e, i:i + 1], k.mod4[:, m:m + 1]).then_inc(k.tables_done, 1)


def route_tensor(k, pe, step, n, g, r):
    m = r.index * GROUPS + g
    if step == 0:
        pe.wait_ge(k.lo_done, n + 1)
        view = lo_hi(k, g)
        mm3(pe, k.turn[:, :], k.router_hi[r.kind], k.router_lo[r.kind], view(k.xh), view(k.xl))\
            .then_inc(k.logits_done, 1)
    if step == 1:
        pe.wait_ge(k.logits_copied, m + 1)
        for j in range(GT):
            last = pe.transpose(k.turn[:, j * P:(j + 1) * P], k.logT[:, j * P:(j + 1) * P], k.ident[:, :])
        last.then_inc(k.logits_turned, 1)
    if step == 2:
        pe.wait_ge(k.parts_done, m + 1)
        turnb = k.turn[:, :].bitcast(BF16).rearrange("p (h s) -> p h s", h=2)
        for h in range(r.halves):
            for j in range(GT):
                last = pe.transpose(turnb[0:r.rows, h, j * P:(j + 1) * P],
                                    k.parts[:, j, h * r.rows:(h + 1) * r.rows], k.identb[:, :])
        last.then_inc(k.parts_turned, 1)


def route_scalar(k, act, step, n, g, r):
    m = r.index * GROUPS + g
    e = r.logits
    logits = k.turn[:, :].rearrange("p (j e) -> p j e", j=GT)[:, :, 0:e]
    if step == 0:
        act.wait_ge(k.logits_done, m + 1)
        act.activation(k.logT[0:e, :], k.turn[0:e, :], ACT.Copy).then_inc(k.logits_copied, 1)
    if step == 1:
        act.wait_ge(k.logits_turned, m + 1)
        if r.kind == "zone":
            act.activation(k.aff[:, :, 0:e], logits, ACT.Sigmoid, scale=k.inv_temp[:, 0:1]).then_inc(k.aff_done, 1)
        elif r.kind == "steps":
            act.activation(k.aff[:, :, 0:e], logits, ACT.Sigmoid, bias=k.bu[:, 0:1]).then_inc(k.aff_done, 1)
        else:
            act.activation(k.aff[:, :, 0:e], logits, ACT.Sigmoid).then_inc(k.aff_done, 1)
    if step == 2 and r.kind == "zone":
        act.wait_ge(k.dist_done, g + 1)
        act.activation(k.exps[:, 0, :, :], k.zone[:, 0, :, :], ACT.Exp, scale=-1.0 / 0.1)
        act.activation(k.exps[:, 1, :, :], k.zone[:, 0, :, :], ACT.Exp, scale=-1.0 / 0.3).then_inc(k.exps_done, 1)
    if step == 3:
        act.wait_ge(k.parts_turned, m + 1)
        turnb = k.turn[:, :].bitcast(BF16).rearrange("p (h s) -> p h s", h=2)
        act.activation(k.mask[0:r.rows, 0:r.halves, bass.ds(g * GROUP, GROUP)], turnb[0:r.rows, 0:r.halves, :],
                       ACT.Copy).then_inc(k.masks_done, 1)


def top2_vector(k, dve, link, p):
    gt, eq = (k.pair[:, i, :, :].rearrange("p j (e f) -> p j e f", e=8) for i in range(2))
    other = p.unsqueeze(2).to_broadcast([P, GT, 8, 8])
    own = p.unsqueeze(3).to_broadcast([P, GT, 8, 8])
    dve.tensor_tensor(gt, other, own, ALU.is_gt)
    link.then(dve.tensor_tensor(eq, other, own, ALU.is_equal))
    link.then(dve.tensor_tensor(eq, eq, k.lower[:, :, :].unsqueeze(1).to_broadcast([P, GT, 8, 8]), ALU.mult))
    link.then(dve.tensor_tensor(gt, gt, eq, ALU.add))
    link.then(dve.tensor_reduce(k.rank[:, :, :], gt, AX_X, ALU.add))
    link.then(dve.scalar_tensor_tensor(out=k.sel[:, :, 0:8], in0=k.rank[:, :, :], scalar=2.0, in1=p,
                                       op0=ALU.is_lt, op1=ALU.mult))


def route_vector(k, dve, step, n, g, r):
    m = r.index * GROUPS + g
    e = r.e
    links = ROUTE_LINKS[r.kind]
    C0, LOW, HIGH = 1.0 / 2.718281828459045, 0.5 - 0.28768207245178085, 0.5
    aff = k.aff[:, :, 0:r.logits]
    if step == 0 and r.kind == "zone":
        link = Chain(dve, k.route_link, k.route_base + g * links)
        dve.wait_ge(k.aff_done, m + 1)
        link.then(dve.tensor_scalar(k.zone[:, 1, :, :], aff, C0, None, ALU.subtract))
        link.then(dve.tensor_scalar(k.zone[:, 2, :, :], aff, LOW, None, ALU.is_ge))
        link.then(dve.scalar_tensor_tensor(out=k.zone[:, 3, :, :], in0=aff, scalar=HIGH, in1=k.zone[:, 2, :, :],
                                           op0=ALU.is_le, op1=ALU.mult))
        dve.scalar_tensor_tensor(out=k.zone[:, 0, :, :], in0=k.zone[:, 1, :, :], scalar=-1.0,
                                 in1=k.zone[:, 1, :, :], op0=ALU.mult, op1=ALU.max).then_inc(k.dist_done, 1)
    if step != 1:
        return
    link = Chain(dve, k.route_link, k.route_base + g * links)
    dve.wait_ge(k.aff_done, m + 1)
    sel, w = k.sel[:, :, 0:e], k.w[:, :, 0:e]

    def scale(out, values, total, floor, how):
        link.then(dve.tensor_scalar(k.tot[:, :], total, floor, None, how))
        link.then(dve.reciprocal(k.inv[:, :], k.tot[:, :]))
        link.then(dve.tensor_tensor(out, values, k.inv[:, :].unsqueeze(2).to_broadcast([P, GT, e]), ALU.mult))

    if r.kind == "top8":
        dve.memset(k.tick[:, :], 0.0)
        for j in range(GT):
            last = dve.max(k.best[:, j, :], k.aff[:, j, :])
        link.then(last)
        dve.memset(k.tick[:, :], 0.0)
        for j in range(GT):
            dve.match_replace(k.rep[:, j, :], k.best[:, j, :], k.aff[:, j, :], -1.0)
        link.then(dve.tensor_reduce(k.small[:, 0, :], k.best[:, :, :], AX_X, ALU.add))
        link.then(dve.scalar_tensor_tensor(out=sel, in0=k.rep[:, :, :], scalar=-1.0, in1=aff,
                                           op0=ALU.is_equal, op1=ALU.mult))
        scale(w, sel, k.small[:, 0, :], 1e-9, ALU.add)
    if r.kind == "top2":
        top2_vector(k, dve, link, aff)
        link.then(dve.tensor_reduce(k.small[:, 0, :], sel, AX_X, ALU.add))
        scale(w, sel, k.small[:, 0, :], 1e-20, ALU.add)
    if r.kind == "steps":
        u = k.aff[:, :, 0:1]
        for i in range(4):
            last = dve.scalar_tensor_tensor(out=k.sel[:, :, i:i + 1], in0=u, scalar=i / 4.0, in1=u,
                                            op0=ALU.is_gt, op1=ALU.mult)
        link.then(last)
        for i in range(4):
            last = dve.tensor_scalar(k.rank[:, :, i:i + 1], k.sel[:, :, i:i + 1], 1.0 / (i + 1), None, ALU.mult)
        link.then(last)
        pick = k.pair[:, 0, :, 0:16].rearrange("p j (e i) -> p j e i", e=4)
        link.then(dve.tensor_tensor(pick, k.rank[:, :, 0:4].unsqueeze(2).to_broadcast([P, GT, 4, 4]),
                                    k.turn4[:, :, :].unsqueeze(1).to_broadcast([P, GT, 4, 4]), ALU.mult))
        link.then(dve.tensor_reduce(w, pick, AX_X, ALU.add))
    if r.kind == "zone":
        link.n = 3
        dve.wait_ge(k.exps_done, g + 1)
        inzone, fallback = k.zone[:, 2, :, :], k.exps[:, 1, :, :]
        link.then(dve.tensor_tensor(inzone, k.exps[:, 0, :, :], k.zone[:, 3, :, :], ALU.mult))
        link.then(dve.tensor_reduce(k.small[:, 1, :], inzone, AX_X, ALU.add))
        link.then(dve.tensor_scalar(k.small[:, 2, :], k.small[:, 1, :], 1e-8, None, ALU.is_lt))
        top2_vector(k, dve, link, fallback)
        link.then(dve.tensor_reduce(k.small[:, 0, :], sel, AX_X, ALU.add))
        scale(w, sel, k.small[:, 0, :], 1e-8, ALU.max)
        link.then(dve.tensor_tensor(w, w, inzone, ALU.subtract))
        link.then(dve.tensor_tensor(w, w, k.small[:, 2, :].unsqueeze(2).to_broadcast([P, GT, e]), ALU.mult))
        link.then(dve.tensor_tensor(sel, w, inzone, ALU.add))
        link.then(dve.tensor_reduce(k.small[:, 3, :], sel, AX_X, ALU.add))
        scale(w, sel, k.small[:, 3, :], 1e-8, ALU.max)
    half = e // r.halves
    parts = k.parts[:, :, 0:r.halves * r.rows].rearrange("p j (h q e) -> p j h q e", h=r.halves, q=3)

    def each(op):
        for h in range(r.halves):
            last = op(parts[:, :, h, :, :], slice(h * half, (h + 1) * half))
        return last

    link.then(each(lambda q, s: dve.tensor_copy(q[:, :, 0, :], k.w[:, :, s])))
    link.then(each(lambda q, s: dve.tensor_tensor(k.rest[:, :, s], k.w[:, :, s], q[:, :, 0, :], ALU.subtract)))
    link.then(each(lambda q, s: dve.tensor_copy(q[:, :, 1, :], k.rest[:, :, s])))
    assert link.n == links, (r.kind, link.n)
    each(lambda q, s: dve.tensor_tensor(q[:, :, 2, :], k.rest[:, :, s], q[:, :, 1, :], ALU.subtract))\
        .then_inc(k.parts_done, 1)



STEPS = 16


def post_tensor(k, pe, step, n, g, route):
    if step == 1:
        post_add_tensor(k, pe, n)
    if step == 4:
        post_turn_tensor(k, pe, n)
    if route and step in (7, 9, 14):
        route_tensor(k, pe, {7: 0, 9: 1, 14: 2}[step], n, g, route)


def post_scalar(k, act, step, n, g, route, bias=None):
    if step == 0:
        post_add_scalar(k, act, n, bias)
    if step == 5:
        post_turn_scalar(k, act, n, g)
    if route and step in (8, 10, 12, 15):
        route_scalar(k, act, {8: 0, 10: 1, 12: 2, 15: 3}[step], n, g, route)


def post_vector(k, dve, step, n, g, route):
    if step == 2:
        post_add_vector(k, dve, n, g)
        post_norm_vector(k, dve, n, g)
    if step == 6:
        post_turn_vector(k, dve, n, g)
    if route and step in (11, 13):
        route_vector(k, dve, {11: 0, 13: 1}[step], n, g, route)


def post_gpsimd(k, pool, n):
    post_norm_gpsimd(k, pool, n)


def steps_at(c, chunks):
    return [s for s in range(STEPS) if s * chunks // STEPS == c]



def share_moe(k):
    k.chunk0 = k.mid0 = k.loaded0 = k.split0 = 0
    k.loaded = k.sem("loaded")
    k.padded = k.sem("padded")
    k.hi_split = k.sem("hi_split")
    k.lo_split = k.sem("lo_split")
    k.g_done = k.sem("g_done")
    k.u_done = k.sem("u_done")
    k.r_done = k.sem("r_done")
    k.t_done = k.sem("t_done")
    k.a_done = k.sem("a_done")


class Moe:

    def __init__(self, name, kind, chunks, route, sel, sel_of, shared=False):
        self.name, self.kind, self.chunks, self.route = name, kind, chunks, route
        self.sel, self.sel_of, self.shared = sel, sel_of, shared
        self.all = chunks + shared


def moe_stage(k, s, gate, up, down, next_route, bias1=None, b2=None, shared=None, last=False):
    nc, C = k.nc, s.all
    base = k.turn0
    with ExitStack() as st:
        sb = lambda name, shape, dt=F32: k.sb(f"{s.name}_{name}", shape, dt, st)
        gate_hi, gate_lo = sb("gate_hi", [P, C, P], F32R), sb("gate_lo", [P, C, P], F32R)
        if up is not None:
            up_hi, up_lo = sb("up_hi", [P, C, P], F32R), sb("up_lo", [P, C, P], F32R)
        down_w = sb("down", [P, C, P])
        loaded, padded, hi_split, lo_split = k.loaded, k.padded, k.hi_split, k.lo_split
        loaded0, split0, chunk0, mid0 = k.loaded0, k.split0, k.chunk0, k.mid0
        raws = 1 if up is None else 2
        total = loaded0 + 16 * (raws + 1 + (3 if s.shared else 0))
        n_hidden = 64
        with ExitStack() as early:
            raw = [k.sb(f"{s.name}_raw{i}", [P, C, P], F32, early) for i in range(raws)]
            with nc.Block() as block:
                @block.sync
                def _(sp):
                    for t, src in zip(raw, (gate, up)):
                        sp.dma_start(t[:, 0:s.chunks, :], src).then_inc(loaded, 16)
                    if s.shared:
                        for t, src in zip(raw, shared[:2]):
                            sp.dma_start(t[:, C - 1, 0:n_hidden], src).then_inc(loaded, 16)
                        sp.dma_start(down_w[0:n_hidden, C - 1, :], shared[2]).then_inc(loaded, 16)
                    sp.dma_start(down_w[:, 0:s.chunks, :], down).then_inc(loaded, 16)
                    sp.wait_ge(loaded, total)


                his = (gate_hi, up_hi) if up is not None else (gate_hi,)
                los = (gate_lo, up_lo) if up is not None else (gate_lo,)

                if s.shared:
                    @block.gpsimd
                    def _(pool):
                        link = Chain(pool, padded, 0)
                        for i in range(raws):
                            link.then(pool.memset(raw[i][:, C - 1, n_hidden:], 0.0))
                        pool.memset(down_w[n_hidden:, C - 1, :], 0.0).then_inc(padded, 1)

                @block.scalar
                def _(act):
                    act.wait_ge(loaded, total)
                    if s.shared:
                        act.wait_ge(padded, 3)
                    for i in range(raws):
                        act.activation(his[i][:, :, :], raw[i][:, :, :], ACT.Copy).then_inc(hi_split, 1)

                @block.vector
                def _(dve):
                    dve.wait_ge(loaded, total)
                    for i in range(raws):
                        dve.wait_ge(hi_split, split0 + i + 1)
                        dve.tensor_tensor(los[i][:, :, :], raw[i][:, :, :], his[i][:, :, :].bitcast(F32), ALU.subtract)\
                            .then_inc(lo_split, 1)
        r = [sb(f"r{i}", [P, GROUP]) for i in range(2)]
        t = [sb(f"t{i}", [P, GROUP]) for i in range(2)]
        a = [sb(f"a{i}", [P, GROUP]) for i in range(2)]
        G = [k.ps(f"{s.name}_G{i}", stack=st) for i in range(2)]
        U = [k.ps(f"{s.name}_U{i}", stack=st) for i in range(2)]
        M = [k.ps(f"{s.name}_M{i}", stack=st) for i in range(2)]
        g_done, u_done, r_done, t_done, a_done = k.g_done, k.u_done, k.r_done, k.t_done, k.a_done

        def masked(c):
            return not (s.shared and c == C - 1)

        def before(eng, sem, g, c):
            if not isinstance(g, int) or g * C + c >= 2:
                eng.wait_ge(sem, chunk0 + g * C + c - 1)

        with nc.Block() as block:
            @block.tensor
            def _(pe):
                def down_product(g, c):
                    pe.wait_ge(a_done, chunk0 + g * C + c + 1)
                    if c == 0:
                        pe.wait_ge(k.y_copied, base + g)
                    product = pe.matmul(k.ypsum[:, :], down_w[:, c, :], a[c % 2][:, :],
                                        start=(c == 0), stop=(c == C - 1))
                    if c == 0 and b2 is not None:
                        for q in range(3):
                            pe.matmul(k.ypsum[:, :], b2[0:s.route.rows, q, :],
                                      k.mask[0:s.route.rows, 0, bass.ds(g * GROUP, GROUP)],
                                      start=False, stop=False)
                    if c == C - 1:
                        product.then_inc(k.y_done, 1)

                def main(g, post):
                    view = lo_hi(k, g)
                    xh, xl = view(k.xh), view(k.xl)
                    for c in range(C):
                        if post:
                            for step in steps_at(c, C):
                                post_tensor(k, pe, step, base + g - 1, g - 1, next_route)
                        b = c % 2
                        before(pe, r_done, g, c)
                        before(pe, a_done, g, c)
                        mm3(pe, G[b][:, :], gate_hi[:, c, :], gate_lo[:, c, :], xh, xl).then_inc(g_done, 1)
                        if up is not None:
                            product = mm3(pe, U[b][:, :], up_hi[:, c, :], up_lo[:, c, :], xh, xl)
                        if masked(c):
                            half, which = s.sel_of(c)
                            product = pe.matmul(M[b][:, :], s.sel[0:s.route.rows, which, :],
                                                k.mask[0:s.route.rows, half, bass.ds(g * GROUP, GROUP)],
                                                start=True, stop=True)
                        product.then_inc(u_done, 1)
                        if c > 0:
                            down_product(g, c - 1)
                    down_product(g, C - 1)

                main(0, False)
                with pe.Fori(1, GROUPS) as g:
                    main(g, True)
                for step in range(STEPS):
                    post_tensor(k, pe, step, base + GROUPS - 1, GROUPS - 1, next_route)

            @block.scalar
            def _(act):
                how = {"gated": ACT.Silu, "relu2": ACT.Relu, "relu": ACT.Relu}[s.kind]

                def main(g, post):
                    for c in range(C):
                        if post:
                            for step in steps_at(c, C):
                                post_scalar(k, act, step, base + g - 1, g - 1, next_route)
                            before(act, a_done, g, c)
                        act.wait_ge(g_done, chunk0 + g * C + c + 1)
                        kw = {"bias": bias1[:, c:c + 1]} if bias1 is not None else {}
                        act.activation(r[c % 2][:, :], G[c % 2][:, :], how, **kw).then_inc(r_done, 1)

                main(0, False)
                with act.Fori(1, GROUPS) as g:
                    main(g, True)
                for step in range(STEPS):
                    post_scalar(k, act, step, base + GROUPS - 1, GROUPS - 1, next_route)

            @block.vector
            def _(dve):
                def main(g, post):
                    for c in range(C):
                        if post:
                            for step in steps_at(c, C):
                                post_vector(k, dve, step, base + g - 1, g - 1, next_route)
                        b = c % 2
                        dve.wait_ge(u_done, chunk0 + g * C + c + 1)
                        dve.wait_ge(r_done, chunk0 + g * C + c + 1)
                        act_, mid, out = r[b][:, :], t[b][:, :], a[b][:, :]
                        if s.kind == "relu":
                            dve.tensor_tensor(out, act_, M[b][:, :], ALU.mult).then_inc(a_done, 1)
                        elif not masked(c):
                            dve.tensor_tensor(out, act_, U[b][:, :], ALU.mult).then_inc(a_done, 1)
                            dve.memset(k.tick[:, :], 0.0).then_inc(t_done, 1)
                        else:
                            dve.tensor_tensor(mid, act_, M[b][:, :], ALU.mult).then_inc(t_done, 1)
                            dve.wait_ge(t_done, mid0 + g * C + c + 1)
                            dve.tensor_tensor(out, mid, U[b][:, :] if s.kind == "gated" else act_, ALU.mult)\
                               .then_inc(a_done, 1)

                main(0, False)
                with dve.Fori(1, GROUPS) as g:
                    main(g, True)
                for step in range(STEPS):
                    post_vector(k, dve, step, base + GROUPS - 1, GROUPS - 1, next_route)

            @block.gpsimd
            def _(pool):
                with pool.Fori(0, GROUPS) as g:
                    post_gpsimd(k, pool, base + g)

            if last:
                @block.sync
                def _(sp):
                    out = k.io["out"].rearrange("(t p) d -> p t d", p=P)
                    for g in range(GROUPS):
                        sp.wait_ge(k.x_done, base + g + 1)
                        sp.dma_start(out[:, g * GT:(g + 1) * GT, :], k.x[:, g * GT:(g + 1) * GT, :])\
                          .then_inc(k.stored, 16)
                    sp.wait_ge(k.stored, 16 * GROUPS)
    k.turn0 += GROUPS
    k.chunk0 += GROUPS * C
    k.mid0 += 0 if s.kind == "relu" else GROUPS * C
    k.loaded0 = total
    k.split0 += raws
    if next_route:
        k.route_base += GROUPS * ROUTE_LINKS[next_route.kind]


def load_params(k):
    io = k.io
    k.inv_temp = k.sb("inv_temp", [P, 1])
    k.bu = k.sb("bu", [P, 1])
    k.b1 = k.sb("ffn2_b1", [P, 16])
    k.b2p = k.sb("ffn2_b2_parts", [12, 3, P], BF16)
    first = {"top8": 0, "top2": 64, "steps": 72, "zone": 73}
    used, width = 81, 73 + P + 1
    router_hi, router_lo = k.sb("router_hi", [P, width], F32R), k.sb("router_lo", [P, width], F32R)
    k.router_hi = {kind: router_hi[:, at:at + P] for kind, at in first.items()}
    k.router_lo = {kind: router_lo[:, at:at + P] for kind, at in first.items()}
    with ExitStack() as early:
        router = k.sb("router_raw", [P, width], F32, early)
        temp, b2, b2r = (k.sb(n, s, F32, early) for n, s in (("temp", [P, 1]), ("b2", [12, P]), ("b2_rest", [12, P])))
        with k.nc.Block() as block:
            @block.sync
            def _(sp):
                n = 0
                with k.nc.allow_non_contiguous_dma(reason="a few columns of parameters"):
                    for out, src in (
                        (router[:, 0:64], io["L0_ffn_router_w"]),
                        (router[:, 64:72], io["L1_ffn_router_w"].rearrange("e d -> d e")),
                        (router[:, 72:73], io["L2_ffn_Wu"]),
                        (router[:, 73:81], io["L3_ffn_Wr"]),
                        (temp[:, :], io["L3_ffn_temperature"].partition_broadcast(P)),
                        (k.bu[:, :], io["L2_ffn_bu"].partition_broadcast(P)),
                        (k.b1[:, :], io["L2_ffn_b1"].rearrange("e (c p) -> p (e c)", p=P)),
                        (b2[0:4, :], io["L2_ffn_b2"]),
                        (b2[4:8, :], io["L2_ffn_b2"]),
                        (b2[8:12, :], io["L2_ffn_b2"]),
                    ):
                        sp.dma_start(out, src).then_inc(k.params_in, 16)
                        n += 16
                k.params_total = n
                sp.wait_ge(k.params_in, n)

            @block.vector
            def _(dve):
                link = Chain(dve, k.params_done, 0)
                link.then(dve.memset(router[:, used:], 0.0))
                dve.wait_ge(k.params_in, k.params_total)
                link.then(dve.tensor_copy(router_hi[:, :], router[:, :]))
                link.then(dve.tensor_tensor(router_lo[:, :], router[:, :], router_hi[:, :].bitcast(F32), ALU.subtract))
                link.then(dve.reciprocal(k.inv_temp[:, :], temp[:, :]))
                link.then(dve.tensor_copy(k.b2p[:, 0, :], b2[:, :]))
                link.then(dve.tensor_tensor(b2r[:, :], b2[:, :], k.b2p[:, 0, :], ALU.subtract))
                link.then(dve.tensor_copy(k.b2p[:, 1, :], b2r[:, :]))
                link.then(dve.tensor_tensor(k.b2p[:, 2, :], b2r[:, :], k.b2p[:, 1, :], ALU.subtract))


ROUTES = {"ffn0": Route("top8", 64, 0), "ffn1": Route("top2", 8, 1),
          "ffn2": Route("steps", 4, 2), "ffn3": Route("zone", 8, 3)}


def ffn0(k, after):
    io = k.io
    s = Moe("ffn0", "gated", 32, ROUTES["ffn0"], k.sel64, lambda c: (c // 16, c % 16), shared=True)
    moe_stage(k, s, io["L0_ffn_expert_gate_k"].rearrange("e h i -> h e i"),
              io["L0_ffn_expert_up_k"].rearrange("e h i -> h e i"),
              io["L0_ffn_expert_down_k"].rearrange("(c e) i h -> (e i) c h", e=2), after,
              shared=(io["L0_ffn_shared_gate_w"], io["L0_ffn_shared_up_w"], io["L0_ffn_shared_down_w"]))


def ffn1(k, after):
    io = k.io
    s = Moe("ffn1", "relu2", 8, ROUTES["ffn1"], k.sel8, lambda c: (0, c))
    moe_stage(k, s, io["L1_ffn_w1"].rearrange("d (e w) -> d e w", e=8), None,
              io["L1_ffn_w2"].rearrange("(e w) d -> w e d", e=8), after)


def ffn2(k, after):
    io = k.io
    s = Moe("ffn2", "relu", 16, ROUTES["ffn2"], k.sel4, lambda c: (0, c // 4))
    moe_stage(k, s, io["L2_ffn_W1"].rearrange("e d f -> d e f"), None,
              io["L2_ffn_W2"].rearrange("e (c f) d -> f (e c) d", f=P), after, bias1=k.b1, b2=k.b2p)


def ffn3(k, after):
    io = k.io
    s = Moe("ffn3", "gated", 8, ROUTES["ffn3"], k.sel8, lambda c: (0, c))
    moe_stage(k, s, io["L3_ffn_Wg"].rearrange("e d i -> d e i"), io["L3_ffn_Wu"].rearrange("e d i -> d e i"),
              io["L3_ffn_Wd"].rearrange("e i d -> i e d"), after, last=True)



def events(k, stage, names, stack):
    return {n: k.sem(f"{stage}_{n}", stack) for n in names.split()}


def load_attn(k):
    io, nc = k.io, k.nc
    sb = k.sb
    raw = {}

    a = k.a = {}
    split_shapes = [("shell_w", [P, 65])] + [(n, [P, P]) for n in (
        "vo_w", "q_w", "k_w", "v_w", "tap0", "tap1", "tap2", "now_k", "now_v", "now_r", "old_k", "old_v", "old_r")]
    for name, shape in split_shapes:
        a[name] = (sb(name + "_hi", shape, F32R), sb(name + "_lo", shape, F32R))
    for name, shape in (("omega_t", [65, 33]), ("combine_t", [64, 320]), ("vo_bias", [P, 1]), ("wp_t", [P, P]),
                        ("wp_bias", [P, 1]), ("wo_t", [P, P]), ("w_log", [P, 1]), ("rff", [P, 64]),
                        ("decay", [P, 384]), ("causal", [P, 384]), ("blocks", [P, P]), ("ones", [P, 1]),
                        ("u", [P, 1]), ("b_shell", [65, 1])):
        a[name] = sb("a_" + name, shape)
    with ExitStack() as early:
        def load(name, shape, src):
            raw[name] = sb(f"raw_{name}", shape, F32, early)
            loads.append((raw[name], src))
            return raw[name]

        loads = []
        square = ("L1_attn_W_v", "L1_attn_W_out", "L2_attn_Wq", "L2_attn_Wk", "L2_attn_Wv", "L2_attn_Wp",
                  "L3_attn_Wk", "L3_attn_Wv", "L3_attn_Wr", "L3_attn_Wo")
        for name in square:
            load(name, [P, P], io[name])
        load("shell", [64, P], io["L1_attn_W_shell"])
        load("charge", [P, 1], io["L1_attn_W_charge"].rearrange("a d -> d a"))
        load("omega", [32, 64], io["L1_attn_omega"])
        load("combine", [64, 320], io["L1_attn_W_combine"])
        column = lambda x: x.rearrange("(p a) -> p a", a=1)
        load("b_v", [P, 1], column(io["L1_attn_b_v"]))
        load("b_out", [P, 1], column(io["L1_attn_b_out"]))
        load("conv_b", [P, 1], column(io["L2_attn_conv_b"]))
        load("conv_w", [P, 3], io["L2_attn_conv_w"])
        load("bp", [P, 1], column(io["L2_attn_bp"]))
        load("log_temp", [P, 1], io["L1_attn_log_temp"].partition_broadcast(P))
        load("rff_row", [P, 32], io["L1_attn_rff_bias"].partition_broadcast(P))
        for m in "kvr":
            load(f"mix_{m}", [P, 1], io[f"L3_attn_mix_{m}"].rearrange("a b d -> d (a b)"))
        load("decay", [P, 1], column(io["L3_attn_time_decay"]))
        loads += [(a["u"], column(io["L3_attn_time_first"])),
                  (a["b_shell"][0:64, :], column(io["L1_attn_b_shell"])),
                  (a["b_shell"][64:65, :], column(io["L1_attn_b_charge"]))]

        for name, shape in split_shapes:
            a[name] = (sb(f"{name}_full", shape, F32, early), *a[name])
        inv_temp, e0, e1, e2 = (sb(n, [P, 1], F32, early) for n in ("att_inv_temp", "tmp_e0", "tmp_e1", "tmp_e2"))
        wout_t = sb("wout_t", [P, P], F32, early)
        rest = {m: sb(f"rest_{m}", [P, 1], F32, early) for m in "kvr"}
        dist = sb("dist", [P, 384], F32, early)
        bank = [k.ps(f"prep{i}", stack=early) for i in range(5)]
        ev = events(k, "prep", "in tables act turned copied link pe2 link2", early)
        total = 16 * len(loads)
        turns = [("L1_attn_W_out", wout_t[:, :]), ("L2_attn_Wq", a["q_w"][0][:, :]), ("L2_attn_Wk", a["k_w"][0][:, :]),
                 ("L2_attn_Wv", a["v_w"][0][:, :]), ("L2_attn_Wp", a["wp_t"][:, :]), ("L3_attn_Wo", a["wo_t"][:, :]),
                 ("L3_attn_Wk", None), ("L3_attn_Wv", None), ("L3_attn_Wr", None)]
        scale = (2.0 / 64) ** 0.5 * 2.718281828459045 ** -0.25
        factorial = [1.0, 1.0, 2.0, 6.0, 24.0]
        mags = [(1.0 / f + 1e-10) ** 0.5 * scale for f in factorial]

        with nc.Block() as block:
            @block.sync
            def _(sp):
                with nc.allow_non_contiguous_dma(reason="a few columns of parameters"):
                    for t, src in loads:
                        sp.dma_start(t[:, :], src).then_inc(ev["in"], 16)
                sp.wait_ge(ev["in"], total)

            @block.gpsimd
            def _(pool):
                link = Chain(pool, ev["tables"], 0)
                link.then(pool.memset(a["ones"][:, :], 1.0))
                link.then(pool.iota(dist[:, 0:128], pattern=[[-1, 128]], base=0, channel_multiplier=1,
                                    allow_small_or_imprecise_dtypes=True))
                link.then(pool.iota(dist[:, 128:384], pattern=[[-1, 256]], base=128, channel_multiplier=1,
                                    allow_small_or_imprecise_dtypes=True))
                link.then(pool.memset(a["causal"][:, :], 0.0))
                link.then(pool.affine_select(out=a["causal"][:, 0:128], in_=a["causal"][:, 0:128], fill=-1e30,
                                             compare_op=ALU.is_ge, base=0, pattern=[[-1, 128]], channel_multiplier=1))
                link.then(pool.affine_select(out=a["causal"][:, 128:384], in_=a["causal"][:, 128:384], fill=-1e30,
                                             compare_op=ALU.is_ge, base=128, pattern=[[-1, 256]], channel_multiplier=1))
                b = a["blocks"][:, :].rearrange("p (h e) -> p h e", e=8)
                link.then(pool.memset(b, 1.0))
                link.then(pool.affine_select(out=b, in_=b, fill=0.0, compare_op=ALU.is_ge, base=0,
                                             pattern=[[-8, 16], [0, 8]], channel_multiplier=1))
                link.then(pool.affine_select(out=b, in_=b, fill=0.0, compare_op=ALU.is_ge, base=7,
                                             pattern=[[8, 16], [0, 8]], channel_multiplier=-1))

            @block.scalar
            def _(act):
                act.wait_ge(ev["in"], total)
                act.activation(e0[:, :], raw["log_temp"][:, :], ACT.Abs).then_inc(ev["act"], 1)
                act.wait_ge(ev["act"], 1)
                act.activation(e1[:, :], e0[:, :], ACT.Exp, scale=-1.0).then_inc(ev["act"], 1)
                act.wait_ge(ev["act"], 2)
                act.activation(e2[:, :], e1[:, :], ACT.Ln, bias=1.0).then_inc(ev["act"], 1)
                act.wait_ge(ev["tables"], 3)
                act.activation(a["decay"][:, :], dist[:, :], ACT.Exp, scale=-0.3 / 10.0).then_inc(ev["act"], 1)
                act.activation(a["w_log"][:, :], raw["decay"][:, :], ACT.Exp).then_inc(ev["act"], 1)

            @block.tensor
            def _(pe):
                pe.wait_ge(ev["in"], total)
                for i, (name, _) in enumerate(turns):
                    pe.transpose(bank[i // 4][:, (i % 4) * P:(i % 4 + 1) * P], raw[name][:, :], k.ident[:, :])\
                      .then_inc(ev["turned"], 1)
                pe.transpose(bank[2][:, 128:192], raw["shell"][:, :], k.ident[0:64, 0:64])
                pe.transpose(bank[2][0:64, 192:224], raw["omega"][:, :], k.ident[0:32, 0:32])
                for m in range(5):
                    last = pe.transpose(bank[3][0:64, m * 64:(m + 1) * 64], raw["combine"][:, m * 64:(m + 1) * 64],
                                        k.ident[0:64, 0:64])
                last.then_inc(ev["turned"], 1)
                pe.wait_ge(ev["copied"], 9)
                pe.matmul(bank[4][:, 0:128], raw["L1_attn_W_v"][:, :], wout_t[:, :], start=True, stop=True)
                pe.matmul(bank[4][:, 128:129], wout_t[:, :], raw["b_v"][:, :], start=True, stop=True)
                pe.matmul(bank[4][:, 129:130], a["wp_t"][:, :], raw["conv_b"][:, :], start=True, stop=True)\
                  .then_inc(ev["pe2"], 1)

            @block.vector
            def _(dve):
                link = Chain(dve, ev["link"], 0)
                dve.wait_ge(ev["in"], total)
                for m in "kvr":
                    last = dve.tensor_scalar(rest[m][:, :], raw[f"mix_{m}"][:, :], -1.0, 1.0, ALU.mult, ALU.add)
                link.then(last)
                dve.memset(a["omega_t"][:, :], 0.0).then_inc(ev["link2"], 1)
                dve.wait_ge(ev["link2"], 1)
                dve.wait_ge(ev["turned"], 10)
                src = lambda i: bank[i // 4][:, (i % 4) * P:(i % 4 + 1) * P]
                for i, (name, out) in enumerate(turns):
                    if out is not None:
                        dve.tensor_copy(out, src(i)).then_inc(ev["copied"], 1)
                    else:
                        m = name[-1].lower()
                        dve.tensor_scalar(a[f"now_{m}"][0][:, :], src(i), raw[f"mix_{m}"][:, 0:1], None, ALU.mult)
                        dve.tensor_scalar(a[f"old_{m}"][0][:, :], src(i), rest[m][:, 0:1], None, ALU.mult)\
                           .then_inc(ev["copied"], 1)
                dve.tensor_copy(a["shell_w"][0][:, 0:64], bank[2][:, 128:192])
                dve.tensor_copy(a["shell_w"][0][:, 64:65], raw["charge"][:, :])
                dve.tensor_copy(a["omega_t"][0:64, 0:32], bank[2][0:64, 192:224])
                dve.memset(a["omega_t"][64:65, 32:33], 1.0)
                for m in range(5):
                    dve.tensor_scalar(a["combine_t"][:, m * 64:(m + 1) * 64], bank[3][0:64, m * 64:(m + 1) * 64],
                                      mags[m], None, ALU.mult)
                dve.tensor_scalar(a["rff"][:, 0:32], raw["rff_row"][:, :], 1.5707963267948966, None, ALU.add)
                dve.tensor_copy(a["rff"][:, 32:64], raw["rff_row"][:, :])
                dve.wait_ge(ev["act"], 5)
                link.then(dve.tensor_scalar(e0[:, :], raw["log_temp"][:, :], 0.0, 0.1, ALU.max, ALU.add))
                link.then(dve.tensor_tensor(e0[:, :], e0[:, :], e2[:, :], ALU.add))
                link.then(dve.reciprocal(inv_temp[:, :], e0[:, :]))
                link.then(dve.tensor_scalar(a["decay"][:, :], a["decay"][:, :], inv_temp[:, 0:1], None, ALU.mult))
                link.then(dve.tensor_scalar(a["w_log"][:, :], a["w_log"][:, :], -1.0, None, ALU.mult))
                dve.wait_ge(ev["copied"], 9)
                for j in range(3):
                    last = dve.tensor_scalar(a[f"tap{j}"][0][:, :], a["wp_t"][:, :], raw["conv_w"][:, j:j + 1], None,
                                             ALU.mult)
                link.then(last)
                dve.wait_ge(ev["pe2"], 1)
                dve.tensor_copy(a["vo_w"][0][:, :], bank[4][:, 0:128])
                dve.tensor_tensor(a["vo_bias"][:, :], bank[4][:, 128:129], raw["b_out"][:, :], ALU.add)
                link.then(dve.tensor_tensor(a["wp_bias"][:, :], bank[4][:, 129:130], raw["bp"][:, :], ALU.add))
                pairs = [v for v in a.values() if isinstance(v, tuple)]
                for full, hi, _ in pairs:
                    last = dve.tensor_copy(hi[:, :], full[:, :])
                link.then(last)
                for full, hi, lo in pairs:
                    last = dve.tensor_tensor(lo[:, :], full[:, :], hi[:, :].bitcast(F32), ALU.subtract)
                link.then(last)


def serial_stage(k, block, tensor, scalar, vector, gpsimd, next_route, bias=None):
    base = k.turn0

    @block.tensor
    def _(pe):
        with pe.Fori(0, GROUPS) as g:
            tensor(pe, g)
            for step in range(STEPS):
                post_tensor(k, pe, step, base + g, g, next_route)

    @block.scalar
    def _(act):
        with act.Fori(0, GROUPS) as g:
            scalar(act, g)
            for step in range(STEPS):
                post_scalar(k, act, step, base + g, g, next_route, bias)

    @block.vector
    def _(dve):
        with dve.Fori(0, GROUPS) as g:
            vector(dve, g)
            for step in range(STEPS):
                post_vector(k, dve, step, base + g, g, next_route)

    @block.gpsimd
    def _(pool):
        with pool.Fori(0, GROUPS) as g:
            if gpsimd is not None:
                gpsimd(pool, g)
            post_gpsimd(k, pool, base + g)


def finish_stage(k, next_route):
    k.turn0 += GROUPS
    if next_route:
        k.route_base += GROUPS * ROUTE_LINKS[next_route.kind]


def attn1(k, next_route):
    a = k.a
    TWO_PI, MAGIC = 6.283185307179586, 12582912.0
    C1 = 6.28125
    C2 = TWO_PI - C1
    with ExitStack() as st:
        sb = lambda name, shape, dt=F32: k.sb(f"at1_{name}", shape, dt, st)
        shell, square = sb("shell", [65, GROUP]), sb("square", [64, GROUP])
        r2, r, q = sb("r2", [P, GT]), sb("r", [P, GT]), sb("q", [P, GT])
        ang, turns = sb("ang", [P, GT, 64]), sb("turns", [P, GT, 64])
        phis, phi = sb("phis", [P, GT, P]), sb("phi", [P, GT, P])
        phisT, phiT = sb("phisT", [64, GROUP]), sb("phiT", [64, GROUP])
        Z = sb("Z", [P, GT, 320])
        VT, V = sb("VT", [P, GROUP]), sb("V", [P, GT, D])
        L = sb("L", [P, GB, 384])
        PT = sb("PT", [P, GB, 384])
        top, total, inv = sb("top", [P, GB, 2]), sb("total", [P, GB, 2]), sb("inv", [P, GB, 2])
        A = [k.ps(f"at1_bank{i}", stack=st) for i in range(6)]
        ev = events(k, "at1", "shell_psum shell_done proj_done r2_done r_done q_done ang_done phis_done phis_turned "
                    "phisT_done z_psum z_copied phi_done phi_turned phiT_done v_psum vT_done v_turned v_done "
                    "zeros logits_psum top_done exp_done p_done p_turned pT_done link", st)
        LINKS = 15
        base = k.turn0

        def tensor(pe, g):
            view = lo_hi(k, g)
            xh, xl = view(k.xh), view(k.xl)
            mm3(pe, A[0][0:65, :], a["shell_w"][1][:, :], a["shell_w"][2][:, :], xh, xl).then_inc(ev["shell_psum"], 1)
            mm3(pe, A[5][:, :], a["vo_w"][1][:, :], a["vo_w"][2][:, :], xh, xl).then_inc(ev["v_psum"], 1)
            pe.wait_ge(ev["shell_done"], g + 1)
            for j in range(GT):
                tile = slice(j * P, (j + 1) * P)
                pe.matmul(A[1][:, j * 33:(j + 1) * 33], shell[:, tile], a["omega_t"][:, :], start=True, stop=True)
            for j in range(GT):
                tile = slice(j * P, (j + 1) * P)
                last = pe.matmul(A[1][:, 132 + j:133 + j], square[:, tile], a["ones"][0:64, :], start=True, stop=True)
            last.then_inc(ev["proj_done"], 1)
            pe.wait_ge(ev["vT_done"], g + 1)
            for j in range(GT):
                last = pe.transpose(A[0][:, j * P:(j + 1) * P], VT[:, j * P:(j + 1) * P], k.ident[:, :])
            last.then_inc(ev["v_turned"], 1)
            pe.wait_ge(ev["phis_done"], g + 1)
            for j in range(GT):
                last = pe.transpose(A[2][:, j * P:(j + 1) * P], phis[:, j, :], k.ident[:, :])
            last.then_inc(ev["phis_turned"], 1)
            pe.wait_ge(ev["phisT_done"], g + 1)
            for j in range(GT):
                if j >= 2:
                    pe.wait_ge(ev["z_copied"], g * GT + j - 1)
                pe.matmul(A[3 + j % 2][:, 0:320], phisT[:, j * P:(j + 1) * P], a["combine_t"][:, :],
                          start=True, stop=True).then_inc(ev["z_psum"], 1)
            pe.wait_ge(ev["phi_done"], g + 1)
            for j in range(GT):
                last = pe.transpose(A[2][:, j * P:(j + 1) * P], phi[:, j, :], k.ident[:, :])
            last.then_inc(ev["phi_turned"], 1)
            pe.wait_ge(ev["phiT_done"], g + 1)
            for b in range(GB):
                q0 = phiT[:, b * SEQ:b * SEQ + P]
                q1 = phiT[:, b * SEQ + P:(b + 1) * SEQ]
                pe.matmul(A[3 + b][:, 0:128], q0, q0, start=True, stop=True)
                pe.matmul(A[3 + b][:, 128:384], q1, phiT[:, b * SEQ:(b + 1) * SEQ], start=True, stop=True)\
                  .then_inc(ev["logits_psum"], 1)
            pe.wait_ge(ev["v_done"], g + 1)
            for b in range(GB):
                pe.wait_ge(ev["p_done"], g * GB + b + 1)
                pe.transpose(A[1 + b][:, 0:128], L[:, b, 0:128], k.ident[:, :])
                pe.transpose(A[1 + b][:, 128:256], L[:, b, 128:256], k.ident[:, :])
                pe.transpose(A[1 + b][:, 256:384], L[:, b, 256:384], k.ident[:, :]).then_inc(ev["p_turned"], 1)
            for b in range(GB):
                pe.wait_ge(ev["pT_done"], g * GB + b + 1)
                pe.matmul(k.ypsum[:, b * SEQ:(b + 1) * SEQ], V[:, 2 * b, :], PT[:, b, 0:256], start=True, stop=False)
                last = pe.matmul(k.ypsum[:, b * SEQ + P:(b + 1) * SEQ], V[:, 2 * b + 1, :], PT[:, b, 256:384],
                                 start=False, stop=True)
            last.then_inc(k.y_done, 1)

        def scalar(act, g):
            act.wait_ge(ev["shell_psum"], g + 1)
            act.activation(shell[:, :], A[0][0:65, :], ACT.Identity, bias=a["b_shell"][:, 0:1])
            act.activation(square[:, :], A[0][0:64, :], ACT.Square, bias=a["b_shell"][0:64, 0:1])\
               .then_inc(ev["shell_done"], 1)
            act.wait_ge(ev["v_psum"], g + 1)
            act.activation(VT[:, :], A[5][:, :], ACT.Identity, bias=a["vo_bias"][:, 0:1]).then_inc(ev["vT_done"], 1)
            act.wait_ge(ev["r2_done"], g + 1)
            act.activation(q[:, :], A[1][:, 0:132].rearrange("p (j e) -> p j e", j=GT)[:, :, 32], ACT.Tanh)\
               .then_inc(ev["q_done"], 1)
            act.wait_ge(ev["v_turned"], g + 1)
            act.activation(V[:, :, :], A[0][:, :].rearrange("p (j d) -> p j d", j=GT), ACT.Copy)\
               .then_inc(ev["v_done"], 1)
            act.wait_ge(ev["ang_done"], g + 1)
            act.activation(phis[:, :, 0:64], ang[:, :, :], ACT.Sin).then_inc(ev["phis_done"], 1)
            act.wait_ge(ev["phis_turned"], g + 1)
            act.activation(phisT[:, :], A[2][0:64, :], ACT.Copy).then_inc(ev["phisT_done"], 1)
            for j in range(GT):
                act.wait_ge(ev["z_psum"], g * GT + j + 1)
                act.activation(Z[:, j, :], A[3 + j % 2][:, 0:320], ACT.Copy).then_inc(ev["z_copied"], 1)
            act.wait_ge(ev["phi_turned"], g + 1)
            act.activation(phiT[:, :], A[2][0:64, :], ACT.Copy).then_inc(ev["phiT_done"], 1)
            for b in range(GB):
                act.wait_ge(ev["top_done"], g * GB + b + 1)
                act.activation(L[:, b, 0:128], L[:, b, 0:128], ACT.Exp, bias=top[:, b, 0:1],
                               accum_out=total[:, b, 0:1])
                act.activation(L[:, b, 128:384], L[:, b, 128:384], ACT.Exp, bias=top[:, b, 1:2],
                               accum_out=total[:, b, 1:2]).then_inc(ev["exp_done"], 1)
            for b in range(GB):
                act.wait_ge(ev["p_turned"], g * GB + b + 1)
                act.activation(PT[:, b, :], A[1 + b][:, 0:384], ACT.Copy).then_inc(ev["pT_done"], 1)

        def gpsimd(pool, g):
            pool.wait_ge(ev["r2_done"], g + 1)
            pool.tensor_tensor(r[:, :], r2[:, :], k.half_neg[:, 0:1].to_broadcast([P, GT]), ALU.pow)\
                .then_inc(ev["r_done"], 1)

        def vector(dve, g):
            link = Chain(dve, ev["link"], g * LINKS)
            dve.wait_ge(ev["proj_done"], g + 1)
            dve.tensor_scalar(r2[:, :], A[1][:, 132:136], 1e-24, None, ALU.max).then_inc(ev["r2_done"], 1)
            dve.wait_ge(ev["q_done"], g + 1)
            dve.wait_ge(ev["r_done"], g + 1)
            proj = A[1][:, 0:132].rearrange("p (j e) -> p j e", j=GT)[:, :, 0:32]
            rr = r[:, :].unsqueeze(2).to_broadcast([P, GT, 32])
            dve.tensor_tensor(ang[:, :, 0:32], proj, rr, ALU.mult)
            link.then(dve.tensor_tensor(ang[:, :, 32:64], proj, rr, ALU.mult))
            link.then(dve.tensor_tensor(ang[:, :, :], ang[:, :, :], a["rff"][:, :].unsqueeze(1)
                                        .to_broadcast([P, GT, 64]), ALU.add))
            link.then(dve.tensor_scalar(turns[:, :, :], ang[:, :, :], 1.0 / TWO_PI, MAGIC, ALU.mult, ALU.add))
            link.then(dve.tensor_scalar(turns[:, :, :], turns[:, :, :], MAGIC, None, ALU.subtract))
            link.then(dve.scalar_tensor_tensor(out=ang[:, :, :], in0=turns[:, :, :], scalar=-C1, in1=ang[:, :, :],
                                               op0=ALU.mult, op1=ALU.add))
            link.then(dve.scalar_tensor_tensor(out=ang[:, :, :], in0=turns[:, :, :], scalar=-C2, in1=ang[:, :, :],
                                               op0=ALU.mult, op1=ALU.add))
            dve.tensor_scalar(ang[:, :, :], ang[:, :, :], 3.1415925, -3.1415925, ALU.min, ALU.max)\
               .then_inc(ev["ang_done"], 1)
            dve.wait_ge(ev["z_copied"], g * GT + GT)
            for m in (3, 2, 1, 0):
                for j in range(GT):
                    prev = Z[:, j, 256:320] if m == 3 else phi[:, j, 0:64]
                    last = dve.scalar_tensor_tensor(out=phi[:, j, 0:64], in0=prev, scalar=q[:, j:j + 1],
                                                    in1=Z[:, j, m * 64:(m + 1) * 64], op0=ALU.mult, op1=ALU.add)
                if m:
                    link.then(last)
            last.then_inc(ev["phi_done"], 1)
            for b in range(GB):
                dve.wait_ge(ev["logits_psum"], g * GB + b + 1)
                link.then(dve.tensor_tensor(L[:, b, :], A[3 + b][:, 0:384], a["decay"][:, :], ALU.mult))
                link.then(dve.tensor_tensor(L[:, b, :], L[:, b, :], a["causal"][:, :], ALU.add))
                dve.tensor_reduce(top[:, b, 0:1], L[:, b, 0:128], AX_X, ALU.max, negate=True)
                dve.tensor_reduce(top[:, b, 1:2], L[:, b, 128:384], AX_X, ALU.max, negate=True)\
                   .then_inc(ev["top_done"], 1)
            for b in range(GB):
                dve.wait_ge(ev["exp_done"], g * GB + b + 1)
                link.then(dve.reciprocal(inv[:, b, :], total[:, b, :]))
                dve.tensor_scalar(L[:, b, 0:128], L[:, b, 0:128], inv[:, b, 0:1], None, ALU.mult)
                dve.tensor_scalar(L[:, b, 128:384], L[:, b, 128:384], inv[:, b, 1:2], None, ALU.mult)\
                   .then_inc(ev["p_done"], 1)
            assert link.n == LINKS, link.n

        with k.nc.Block() as block:
            @block.vector
            def _(dve):
                dve.memset(phis[:, :, :], 0.0)
                dve.memset(phi[:, :, :], 0.0).then_inc(ev["zeros"], 1)
                dve.wait_ge(ev["zeros"], 1)
        with k.nc.Block() as block:
            serial_stage(k, block, tensor, scalar, vector, gpsimd, next_route)
    finish_stage(k, next_route)


def attn2(k, next_route):
    a = k.a
    with ExitStack() as st:
        sb = lambda name, shape, dt=F32: k.sb(f"at2_{name}", shape, dt, st)
        low = [sb(f"low_{x}", [P, GROUP]) for x in "qk"]
        ex = [sb(f"exp_{x}", [P, GROUP]) for x in "qk"]
        pos = [sb(f"pos_{x}", [P, GROUP]) for x in "qk"]
        vT = sb("vT", [P, GROUP])
        kt, vt = sb("k_tokens", [P, GT, D]), sb("v_tokens", [P, GT, D])
        ks = sb("k_sum", [P, GB])
        kv, ksm = sb("kv", [P, GB, D]), sb("k_sum_heads", [P, GB, D])
        den, rec, att = sb("den", [P, GROUP]), sb("rec", [P, GROUP]), sb("att", [P, GROUP])
        A = [k.ps(f"at2_bank{i}", stack=st) for i in range(6)]
        ev = events(k, "at2", "q_psum k_psum v_psum q_low k_low q_exp k_exp q_done k_done vT_done k_turned v_turned "
                    "k_copied v_copied kv_psum kv_done num_psum att_done link", st)
        LINKS = 3

        def tensor(pe, g):
            view = lo_hi(k, g)
            xh, xl = view(k.xh), view(k.xl)
            for i, x in enumerate("qkv"):
                mm3(pe, A[i][:, :], a[f"{x}_w"][1][:, :], a[f"{x}_w"][2][:, :], xh, xl).then_inc(ev[f"{x}_psum"], 1)
            for j in range(3):
                mm3(pe, k.ypsum[:, :], a[f"tap{j}"][1][:, :], a[f"tap{j}"][2][:, :], view(k.xh, j - 1),
                    view(k.xl, j - 1), start=(j == 0), stop=False)
            for i, (name, src, done) in enumerate((("k", pos[1], "k_done"), ("v", vT, "vT_done"))):
                pe.wait_ge(ev[done], g + 1)
                for j in range(GT):
                    last = pe.transpose(A[3 + i][:, j * P:(j + 1) * P], src[:, j * P:(j + 1) * P], k.ident[:, :])
                last.then_inc(ev[f"{name}_turned"], 1)
            pe.wait_ge(ev["k_copied"], g + 1)
            pe.wait_ge(ev["v_copied"], g + 1)
            for b in range(GB):
                for j in range(2):
                    last = pe.matmul(A[5][:, b * D:(b + 1) * D], kt[:, 2 * b + j, :], vt[:, 2 * b + j, :],
                                     start=(j == 0), stop=(j == 1))
            last.then_inc(ev["kv_psum"], 1)
            pe.wait_ge(ev["q_done"], g + 1)
            pe.wait_ge(ev["kv_done"], g + 1)
            for b in range(GB):
                cols = slice(b * SEQ, (b + 1) * SEQ)
                pe.matmul(A[3][:, cols], kv[:, b, :], pos[0][:, cols], start=True, stop=True)
                last = pe.matmul(A[4][:, cols], ksm[:, b, :], pos[0][:, cols], start=True, stop=True)
            last.then_inc(ev["num_psum"], 1)
            pe.wait_ge(ev["att_done"], g + 1)
            pe.matmul(k.ypsum[:, :], a["wp_t"][:, :], att[:, :], start=False, stop=True).then_inc(k.y_done, 1)

        def scalar(act, g):
            for i, x in enumerate("qk"):
                act.wait_ge(ev[f"{x}_low"], g + 1)
                act.activation(ex[i][:, :], low[i][:, :], ACT.Exp).then_inc(ev[f"{x}_exp"], 1)
            act.wait_ge(ev["v_psum"], g + 1)
            act.activation(vT[:, :], A[2][:, :], ACT.Copy).then_inc(ev["vT_done"], 1)
            for i, (name, out) in enumerate((("k", kt), ("v", vt))):
                act.wait_ge(ev[f"{name}_turned"], g + 1)
                act.activation(out[:, :, :], A[3 + i][:, :].rearrange("p (j d) -> p j d", j=GT), ACT.Copy)\
                   .then_inc(ev[f"{name}_copied"], 1)

        def vector(dve, g):
            link = Chain(dve, ev["link"], g * LINKS)
            for i, x in enumerate("qk"):
                dve.wait_ge(ev[f"{x}_psum"], g + 1)
                dve.tensor_scalar(low[i][:, :], A[i][:, :], 0.0, None, ALU.min).then_inc(ev[f"{x}_low"], 1)
            for i, x in enumerate("qk"):
                dve.wait_ge(ev[f"{x}_exp"], g + 1)
                dve.scalar_tensor_tensor(out=pos[i][:, :], in0=A[i][:, :], scalar=0.0, in1=ex[i][:, :],
                                         op0=ALU.max, op1=ALU.add).then_inc(ev[f"{x}_done"], 1)
            dve.wait_ge(ev["k_done"], g + 1)
            link.then(dve.tensor_reduce(ks[:, :], pos[1][:, :].rearrange("p (b s) -> p b s", b=GB), AX_X, ALU.add))
            for b in range(GB):
                dve.tensor_scalar(ksm[:, b, :], a["blocks"][:, :], ks[:, b:b + 1], None, ALU.mult)
            dve.wait_ge(ev["kv_psum"], g + 1)
            dve.tensor_tensor(kv[:, :, :], A[5][:, 0:GB * D].rearrange("p (b d) -> p b d", b=GB),
                              a["blocks"][:, :].unsqueeze(1).to_broadcast([P, GB, D]), ALU.mult)\
               .then_inc(ev["kv_done"], 1)
            dve.wait_ge(ev["num_psum"], g + 1)
            link.then(dve.tensor_scalar(den[:, :], A[4][:, :], 1e-6, None, ALU.max))
            link.then(dve.reciprocal(rec[:, :], den[:, :]))
            dve.tensor_tensor(att[:, :], A[3][:, :], rec[:, :], ALU.mult).then_inc(ev["att_done"], 1)

        with k.nc.Block() as block:
            serial_stage(k, block, tensor, scalar, vector, None, next_route, a["wp_bias"][:, 0:1])
    finish_stage(k, next_route)


def attn3(k, next_route):
    a = k.a
    NONE = -1e38
    with ExitStack() as st:
        sb = lambda name, shape, dt=F32: k.sb(f"at3_{name}", shape, dt, st)
        peak, num, den = (sb(n, [P, GB, SEQ + 1]) for n in ("peak", "num", "den"))
        most = sb("most", [P, GB, SEQ])
        args, exps = sb("args", [P, 4, GROUP]), sb("exps", [P, 4, GROUP])
        rneg, rexp = sb("rneg", [P, GROUP]), sb("rexp", [P, GROUP])
        sv, ov, o1, o2 = (sb(n, [P, GB, SEQ]) for n in ("sv", "ov", "o1", "o2"))
        out = sb("out", [P, GROUP])
        A = [k.ps(f"at3_bank{i}", stack=st) for i in range(3)]
        ev = events(k, "at3", "k_psum v_psum r_psum args_done exps_done out_done link start rneg_done", st)
        LINKS = 9

        def split(t):
            return t.rearrange("p (b s) -> p b s", b=GB)

        def tensor(pe, g):
            view = lo_hi(k, g)
            for i, x in enumerate("kvr"):
                mm3(pe, A[i][:, :], a[f"now_{x}"][1][:, :], a[f"now_{x}"][2][:, :], view(k.xh), view(k.xl), stop=False)
                mm3(pe, A[i][:, :], a[f"old_{x}"][1][:, :], a[f"old_{x}"][2][:, :], view(k.xh, -1), view(k.xl, -1),
                    start=False).then_inc(ev[f"{x}_psum"], 1)
            pe.wait_ge(ev["out_done"], g + 1)
            pe.matmul(k.ypsum[:, :], a["wo_t"][:, :], out[:, :], start=True, stop=True).then_inc(k.y_done, 1)

        def scalar(act, g):
            act.wait_ge(ev["args_done"], g + 1)
            act.activation(exps[:, :, :], args[:, :, :], ACT.Exp)
            act.wait_ge(ev["rneg_done"], g + 1)
            act.activation(rexp[:, :], rneg[:, :], ACT.Exp).then_inc(ev["exps_done"], 1)

        def vector(dve, g):
            link = Chain(dve, ev["link"], g * LINKS)
            K, V, R = (split(A[i][:, :]) for i in range(3))
            before, after = peak[:, :, 0:SEQ], peak[:, :, 1:SEQ + 1]
            e1a, e2a, s1a, s2a = (split(args[:, i, :]) for i in range(4))
            e1, e2, s1, s2 = (split(exps[:, i, :]) for i in range(4))
            u, w = a["u"][:, 0:1], a["w_log"][:, 0:1]
            dve.wait_ge(ev["k_psum"], g + 1)
            for b in range(GB):
                last = dve.tensor_tensor_scan(peak[:, b, 1:SEQ + 1], w.to_broadcast([P, SEQ]),
                                              A[0][:, b * SEQ:(b + 1) * SEQ], NONE, ALU.add, ALU.max)
            link.then(last)
            link.then(dve.scalar_tensor_tensor(out=most[:, :, :], in0=K, scalar=u, in1=before,
                                               op0=ALU.add, op1=ALU.max))
            dve.tensor_tensor(e1a, before, most[:, :, :], ALU.subtract)
            dve.scalar_tensor_tensor(out=e2a, in0=K, scalar=u, in1=most[:, :, :], op0=ALU.add, op1=ALU.subtract)
            dve.scalar_tensor_tensor(out=s1a, in0=before, scalar=w, in1=after, op0=ALU.add, op1=ALU.subtract)
            dve.tensor_tensor(s2a, K, after, ALU.subtract).then_inc(ev["args_done"], 1)
            dve.wait_ge(ev["r_psum"], g + 1)
            dve.tensor_scalar(rneg[:, :], A[2][:, :], -1.0, 80.0, ALU.mult, ALU.min).then_inc(ev["rneg_done"], 1)
            dve.wait_ge(ev["v_psum"], g + 1)
            dve.wait_ge(ev["exps_done"], g + 1)
            link.then(dve.tensor_tensor(sv[:, :, :], s2, V, ALU.mult))
            for b in range(GB):
                cols = slice(b * SEQ, (b + 1) * SEQ)
                dve.tensor_tensor_scan(num[:, b, 1:SEQ + 1], exps[:, 2, cols], sv[:, b, :], 0.0, ALU.mult, ALU.add)
                last = dve.tensor_tensor_scan(den[:, b, 1:SEQ + 1], exps[:, 2, cols], exps[:, 3, cols], 0.0,
                                              ALU.mult, ALU.add)
            link.then(last)
            dve.tensor_tensor(ov[:, :, :], e2, V, ALU.mult)
            dve.tensor_tensor(o1[:, :, :], e1, num[:, :, 0:SEQ], ALU.mult)
            link.then(dve.tensor_tensor(o2[:, :, :], e1, den[:, :, 0:SEQ], ALU.mult))
            link.then(dve.tensor_tensor(o1[:, :, :], o1[:, :, :], ov[:, :, :], ALU.add))
            link.then(dve.tensor_tensor(o2[:, :, :], o2[:, :, :], e2, ALU.add))
            link.then(dve.scalar_tensor_tensor(out=o2[:, :, :], in0=split(rexp[:, :]), scalar=1.0, in1=o2[:, :, :],
                                               op0=ALU.add, op1=ALU.mult))
            link.then(dve.reciprocal(ov[:, :, :], o2[:, :, :]))
            dve.tensor_tensor(split(out[:, :]), o1[:, :, :], ov[:, :, :], ALU.mult).then_inc(ev["out_done"], 1)
            assert link.n == LINKS, link.n

        with k.nc.Block() as block:
            @block.vector
            def _(dve):
                dve.memset(peak[:, :, 0:1], NONE)
                dve.memset(num[:, :, 0:1], 0.0)
                dve.memset(den[:, :, 0:1], 0.0).then_inc(ev["start"], 1)
                dve.wait_ge(ev["start"], 1)
        with k.nc.Block() as block:
            serial_stage(k, block, tensor, scalar, vector, None, next_route)
    finish_stage(k, next_route)



CH, ST, TAPS = 256, 16, 4
CT = CH // P
PAD = SEQ + P
PACK = P // ST
PACKS = CH // PACK
TCH = 8
LOADS = CH // TCH
RING = 2


def ssm(k, next_route):
    io, nc = k.io, k.nc
    with ExitStack() as st:
        sb = lambda name, shape, dt=F32, stack=st: k.sb(f"ssm_{name}", shape, dt, stack)
        scratch_a = nc.dram_tensor("scratch_a16", (CH, ST * ST), F32, kind="Internal").ap()
        scratch_k = nc.dram_tensor("scratch_kernels", (CH, PAD * 3), BF16, kind="Internal").ap()
        wout = sb("wout", [P, CT, D])
        win_hi, win_lo = sb("win_hi", [P, CH], F32R), sb("win_lo", [P, CH], F32R)
        bias_t = sb("bias_t", [P, SEQ])
        Y = sb("Y", [P, CH, 2, BATCH])
        load_x(k, st)
        kernels(k, scratch_a, scratch_k, wout, win_hi, win_lo, bias_t)
        recurrence(k, scratch_k, win_hi, win_lo, Y)
        project(k, wout, bias_t, Y, next_route)
    finish_stage(k, next_route)


def load_x(k, st):
    nc = k.nc
    with ExitStack() as early:
        sb = lambda name, shape: k.sb(f"ln0_{name}", shape, F32, early)
        eps_rms, t1, t2, t3, t4 = sb("eps", [P, 1]), *(sb(f"t{i}", [P, GT]) for i in range(4))
        scale, h = sb("scale", [P, GT]), sb("h", [P, GT, D])
        flip = sb("flip", [P, P])
        ev = events(k, "ln0", "stats aggr pool scale_done h_done added turned hi lo eps flip", early)
        loads = [k.sem(f"x_loaded{g}", early) for g in range(GROUPS)]
        stats, moments = sb("stats", [P, GT, 6]), sb("moments", [P, GT, 2])
        with nc.Block() as block:
            @block.sync
            def _(sp):
                src = k.io["L0_attn_x"].rearrange("b (h p) d -> p (b h) d", p=P)
                for g in range(GROUPS):
                    sp.dma_start(k.x[:, g * GT:(g + 1) * GT, :], src[:, g * GT:(g + 1) * GT, :])\
                      .then_inc(loads[g], 16)

            @block.vector
            def _(dve):
                dve.memset(eps_rms[:, :], 1e-6).then_inc(ev["eps"], 1)
                for g in range(GROUPS):
                    dve.wait_ge(loads[g], 16)
                    for j in range(GT):
                        last = dve.bn_stats(stats[:, j, :], k.x[:, g * GT + j, :])
                    last.then_inc(ev["stats"], 1)
                    dve.wait_ge(ev["stats"], g + 1)
                    for j in range(GT):
                        last = dve.bn_aggr(moments[:, j, :], stats[:, j, :])
                    last.then_inc(ev["aggr"], 1)
                    dve.wait_ge(ev["scale_done"], g + 1)
                    if g:
                        dve.wait_ge(ev["turned"], g)
                    for j in range(GT):
                        mean = moments[:, j, 0:1]
                        dve.tensor_scalar(h[:, j, :], k.x[:, g * GT + j, :], mean, scale[:, j:j + 1],
                                          ALU.subtract, ALU.mult)
                        last = dve.tensor_scalar(k.xn[:, j, :], k.x[:, g * GT + j, :], mean, t2[:, j:j + 1],
                                                 ALU.subtract, ALU.mult)
                    last.then_inc(ev["h_done"], 1)
                    dve.wait_ge(ev["h_done"], g + 1)
                    xs = k.x[:, g * GT:(g + 1) * GT, :]
                    dve.tensor_tensor(xs, xs, k.xn[:, :, :], ALU.add).then_inc(ev["added"], 1)
                    dve.wait_ge(ev["added"], g + 1)
                    dve.wait_ge(ev["hi"], g + 1)
                    view = lo_hi(k, g)
                    dve.tensor_tensor(view(k.xl), k.turn[:, :].rearrange("p (b s) -> p b s", b=GB),
                                      view(k.xh).bitcast(F32), ALU.subtract).then_inc(ev["lo"], 1)

            @block.gpsimd
            def _(pool):
                neg = k.half_neg[:, 0:1].to_broadcast([P, GT])
                pool.memset(flip[:, :], 0.0).then_inc(ev["flip"], 1)
                pool.wait_ge(ev["flip"], 1)
                pool.affine_select(out=flip[:, :], in_=flip[:, :], compare_op=ALU.not_equal, fill=1.0,
                                   base=1 - P, pattern=[[1, P]], channel_multiplier=1).then_inc(ev["flip"], 1)
                pool.wait_ge(ev["flip"], 2)
                pool.wait_ge(ev["eps"], 1)
                for g in range(GROUPS):
                    link = Chain(pool, ev["pool"], 6 * g)
                    pool.wait_ge(ev["aggr"], g + 1)
                    if g:
                        pool.wait_ge(ev["h_done"], g)
                    link.then(pool.tensor_tensor(t1[:, :], moments[:, :, 1], k.eps[:, 0:1].to_broadcast([P, GT]),
                                                 ALU.add))
                    link.then(pool.tensor_tensor(t2[:, :], t1[:, :], neg, ALU.pow))
                    link.then(pool.tensor_tensor(t3[:, :], moments[:, :, 1], t2[:, :], ALU.mult))
                    link.then(pool.tensor_tensor(t3[:, :], t3[:, :], t2[:, :], ALU.mult))
                    link.then(pool.tensor_tensor(t3[:, :], t3[:, :], eps_rms[:, 0:1].to_broadcast([P, GT]), ALU.add))
                    link.then(pool.tensor_tensor(t4[:, :], t3[:, :], neg, ALU.pow))
                    pool.tensor_tensor(scale[:, :], t4[:, :], t2[:, :], ALU.mult).then_inc(ev["scale_done"], 1)

            @block.tensor
            def _(pe):
                pe.wait_ge(ev["flip"], 2)
                for g in range(GROUPS):
                    pe.wait_ge(ev["h_done"], g + 1)
                    if g:
                        pe.wait_ge(ev["lo"], g)
                    for j in range(GT):
                        last = pe.matmul(k.turn[:, j * P:(j + 1) * P], h[:, j, :], flip[:, :], start=True, stop=True)
                    last.then_inc(ev["turned"], 1)

            @block.scalar
            def _(act):
                for g in range(GROUPS):
                    act.wait_ge(ev["turned"], g + 1)
                    act.activation(lo_hi(k, g)(k.xh), k.turn[:, :].rearrange("p (b s) -> p b s", b=GB), ACT.Copy)\
                       .then_inc(ev["hi"], 1)


def kernels(k, scratch_a, scratch_k, wout, win_hi, win_lo, bias_t):
    io, nc = k.io, k.nc
    with ExitStack() as st:
        sb = lambda name, shape, dt=F32: k.sb(f"kern_{name}", shape, dt, st)
        compact = sb("compact", [P, PACKS, ST])
        mask = sb("mask", [P, PACK, ST])
        A, AT = sb("A", [P, PACKS, P]), sb("AT", [P, PACKS, P])
        rows = sb("rows", [P, CT, ST, ST])
        rows16 = sb("rows16", [P, CT, ST, ST])
        baby, giant = sb("baby", [P, CT, ST, ST]), sb("giant", [P, CT, ST, ST])
        part = sb("part", [P, CT, ST, ST])
        wide = sb("wide", [P, ST, ST, ST])
        K, KC = sb("K", [P, CT, TAPS - 1 + SEQ]), sb("KC", [P, CT, SEQ])
        sums = sb("sums", [P, 2, CT, SEQ])
        bias = sb("bias", [P, CT, SEQ])
        packed = sb("packed", [P, CT, PAD, 3], BF16)
        rest = part[:, :, :, :].rearrange("p t r s -> p t (r s)")
        taps, conv_b, b_in = sb("taps", [P, CT, TAPS]), sb("conv_b", [P, CT]), sb("b_in", [P, CT])
        norm_w, b_out, win = sb("norm_w", [P, 1]), sb("b_out", [P, 1]), sb("win", [P, CH])
        ones = sb("ones", [P, 1])
        bank = [k.ps(f"kern_bank{i}", stack=st) for i in range(6)]
        ev = events(k, "kern", "a_in in mask_done bd_done at_turned at_copied squared a_copied a16_out a16_in "
                    "link kern_done bias_psum k_out mask_link bias_done", st)
        LEVELS = 4
        QUADS = PACKS // 4
        channels = lambda v: v.rearrange("(t p) r -> p t r", p=P)
        with nc.Block() as block:
            @block.sync
            def _(sp):
                sp.dma_start(compact[:, :, :], io["L0_attn_A"].rearrange("(g c) r s -> (c r) g s", c=PACK))\
                  .then_inc(ev["a_in"], 16)
                loads = [
                    (rows[:, :, :, :].rearrange("p t r s -> p t (r s)"),
                     io["L0_attn_A"].rearrange("(t p) r s -> p t (r s)", p=P)),
                    (giant[:, :, 0, :], channels(io["L0_attn_Bm"].rearrange("d r a -> d (r a)"))),
                    (baby[:, :, 0, :], channels(io["L0_attn_Cm"].rearrange("d a r -> d (a r)"))),
                    (taps[:, :, :], channels(io["L0_attn_conv_w"].rearrange("d a r -> d (a r)"))),
                    (win[:, :], io["L0_attn_Win"]),
                    (wout[:, :, :], channels(io["L0_attn_Wout"])),
                    (conv_b[:, :], io["L0_attn_conv_b"].rearrange("(t p) -> p t", p=P)),
                    (b_in[:, :], io["L0_attn_b_in"].rearrange("(t p) -> p t", p=P)),
                    (norm_w[:, :], io["L0_attn_norm_w"].rearrange("(p a) -> p a", a=1)),
                    (b_out[:, :], io["L0_attn_b_out"].rearrange("(p a) -> p a", a=1)),
                ]
                with nc.allow_non_contiguous_dma(reason="a few columns of parameters"):
                    for out, src in loads:
                        sp.dma_start(out, src).then_inc(ev["in"], 16)
                k.kern_loads = 16 * len(loads)
                sp.wait_ge(ev["a_copied"], QUADS * (LEVELS + 1) - QUADS)
                to = scratch_a.rearrange("(g c) (r s) -> c r g s", c=PACK, r=ST)
                for c in range(PACK):
                    sp.dma_start(to[c], A[ST * c:ST * (c + 1), :, ST * c:ST * (c + 1)]).then_inc(ev["a16_out"], 16)
                sp.wait_ge(ev["a16_out"], 16 * PACK)
                sp.dma_start(rows16[:, :, :, :].rearrange("p t r s -> p t (r s)"), channels(scratch_a))\
                  .then_inc(ev["a16_in"], 16)
                sp.wait_ge(ev["kern_done"], 1)
                sp.dma_start(channels(scratch_k), packed[:, :, :, :].rearrange("p t a q -> p t (a q)"))\
                  .then_inc(ev["k_out"], 16)
                sp.wait_ge(ev["k_out"], 16)

            @block.gpsimd
            def _(pool):
                link = Chain(pool, ev["mask_link"], 0)
                link.then(pool.memset(mask[:, :, :], 1.0))
                link.then(pool.affine_select(out=mask[:, :, :], in_=mask[:, :, :], fill=0.0, compare_op=ALU.is_ge,
                                             base=0, pattern=[[-ST, PACK], [0, ST]], channel_multiplier=1))
                pool.affine_select(out=mask[:, :, :], in_=mask[:, :, :], fill=0.0, compare_op=ALU.is_ge,
                                   base=ST - 1, pattern=[[ST, PACK], [0, ST]], channel_multiplier=-1)\
                    .then_inc(ev["mask_done"], 1)

            @block.tensor
            def _(pe):
                for q in range(QUADS):
                    pe.wait_ge(ev["bd_done"], q + 1)
                    if q >= 6:
                        pe.wait_ge(ev["at_copied"], q - 5)
                    for i in range(4):
                        last = pe.transpose(bank[q % 6][:, i * P:(i + 1) * P], A[:, 4 * q + i, :], k.ident[:, :])
                    last.then_inc(ev["at_turned"], 1)
                n = 0
                for level in range(LEVELS):
                    for q in range(QUADS):
                        pe.wait_ge(ev["at_copied"], QUADS * level + q + 1)
                        if level:
                            pe.wait_ge(ev["a_copied"], QUADS * (level - 1) + q + 1)
                        b0, b1 = bank[2 * (n % 3)], bank[2 * (n % 3) + 1]
                        if n >= 3:
                            pe.wait_ge(ev["a_copied"], n - 2)
                            if QUADS + n - 2 <= QUADS * LEVELS:
                                pe.wait_ge(ev["at_copied"], QUADS + n - 2)
                        else:
                            pe.wait_ge(ev["at_copied"], QUADS)
                        for i in range(4):
                            g = 4 * q + i
                            last = pe.matmul(b0[:, i * P:(i + 1) * P], AT[:, g, :], A[:, g, :], start=True, stop=True)
                            if level < LEVELS - 1:
                                last = pe.matmul(b1[:, i * P:(i + 1) * P], A[:, g, :], AT[:, g, :],
                                                 start=True, stop=True)
                        last.then_inc(ev["squared"], 1)
                        n += 1
                pe.wait_ge(ev["bias_done"], 1)
                for t in range(CT):
                    last = pe.matmul(bank[0][:, 0:SEQ], wout[:, t, :], bias[:, t, :], start=(t == 0), stop=(t == CT - 1))
                last.then_inc(ev["bias_psum"], 1)

            @block.scalar
            def _(act):
                for q in range(QUADS):
                    act.wait_ge(ev["at_turned"], q + 1)
                    act.activation(AT[:, 4 * q:4 * q + 4, :], bank[q % 6][:, :].rearrange("p (i m) -> p i m", i=4),
                                   ACT.Copy).then_inc(ev["at_copied"], 1)
                n = 0
                for level in range(LEVELS - 1):
                    for q in range(QUADS):
                        act.wait_ge(ev["squared"], n + 1)
                        act.activation(AT[:, 4 * q:4 * q + 4, :],
                                       bank[2 * (n % 3) + 1][:, :].rearrange("p (i m) -> p i m", i=4), ACT.Copy)\
                           .then_inc(ev["at_copied"], 1)
                        n += 1

            @block.vector
            def _(dve):
                dve.wait_ge(ev["a_in"], 16)
                dve.wait_ge(ev["mask_done"], 1)
                for q in range(QUADS):
                    dve.tensor_tensor(A[:, 4 * q:4 * q + 4, :].rearrange("p g (c s) -> p g c s", c=PACK),
                                      compact[:, 4 * q:4 * q + 4, :].unsqueeze(2).to_broadcast([P, 4, PACK, ST]),
                                      mask[:, :, :].unsqueeze(1).to_broadcast([P, 4, PACK, ST]), ALU.mult)\
                       .then_inc(ev["bd_done"], 1)
                link = Chain(dve, ev["link"], 0)
                dve.memset(ones[:, :], 1.0)
                dve.memset(packed[:, :, :, :], 0.0)
                link.then(dve.memset(K[:, :, 0:TAPS - 1], 0.0))
                dve.wait_ge(ev["in"], k.kern_loads)
                link.then(dve.tensor_scalar(win[:, :], win[:, :], norm_w[:, 0:1], None, ALU.mult))
                link.then(dve.tensor_copy(win_hi[:, :], win[:, :]))
                dve.tensor_tensor(win_lo[:, :], win[:, :], win_hi[:, :].bitcast(F32), ALU.subtract)

                def baby_step(j):
                    link.then(dve.tensor_tensor(part[:, :, :, :], rows[:, :, :, :],
                                                baby[:, :, j, :].unsqueeze(2).to_broadcast([P, CT, ST, ST]), ALU.mult))
                    link.then(dve.tensor_reduce(baby[:, :, j + 1, :], part[:, :, :, :], AX_X, ALU.add))

                n, steps = 0, iter(range(ST - 1))
                for level in range(LEVELS):
                    for q in range(QUADS):
                        if q % 2 == 1 and (j := next(steps, None)) is not None:
                            baby_step(j)
                        dve.wait_ge(ev["squared"], n + 1)
                        dve.tensor_copy(A[:, 4 * q:4 * q + 4, :],
                                        bank[2 * (n % 3)][:, :].rearrange("p (i m) -> p i m", i=4))\
                           .then_inc(ev["a_copied"], 1)
                        n += 1
                for j in steps:
                    baby_step(j)
                dve.wait_ge(ev["a16_in"], 16)
                for i in range(ST - 1):
                    link.then(dve.tensor_tensor(part[:, :, :, :], rows16[:, :, :, :].rearrange("p t r s -> p t s r"),
                                                giant[:, :, i, :].unsqueeze(2).to_broadcast([P, CT, ST, ST]), ALU.mult))
                    link.then(dve.tensor_reduce(giant[:, :, i + 1, :], part[:, :, :, :], AX_X, ALU.add))
                for t in range(CT):
                    link.then(dve.tensor_tensor(wide[:, :, :, :], giant[:, t, :, :].unsqueeze(2)
                                                .to_broadcast([P, ST, ST, ST]),
                                                baby[:, t, :, :].unsqueeze(1).to_broadcast([P, ST, ST, ST]), ALU.mult))
                    link.then(dve.tensor_reduce(K[:, t, TAPS - 1:].rearrange("p (i j) -> p i j", i=ST),
                                                wide[:, :, :, :], AX_X, ALU.add))
                for t in range(CT):
                    lag = lambda m: K[:, t, TAPS - 1 - m:TAPS - 1 - m + SEQ]
                    link.then(dve.tensor_scalar(KC[:, t, :], lag(0), taps[:, t, 3:4], None, ALU.mult))
                    for m in range(1, TAPS):
                        link.then(dve.scalar_tensor_tensor(out=KC[:, t, :], in0=lag(m), scalar=taps[:, t, 3 - m:4 - m],
                                                           in1=KC[:, t, :], op0=ALU.mult, op1=ALU.add))
                link.then(dve.tensor_copy(packed[:, :, P:, 0], KC[:, :, :]))
                link.then(dve.tensor_tensor(rest[:, :, :], KC[:, :, :], packed[:, :, P:, 0], ALU.subtract))
                link.then(dve.tensor_copy(packed[:, :, P:, 1], rest[:, :, :]))
                dve.tensor_tensor(packed[:, :, P:, 2], rest[:, :, :], packed[:, :, P:, 1], ALU.subtract)\
                   .then_inc(ev["kern_done"], 1)
                for t in range(CT):
                    dve.tensor_tensor_scan(sums[:, 0, t, :], ones[:, 0:1].to_broadcast([P, SEQ]), K[:, t, TAPS - 1:],
                                           0.0, ALU.mult, ALU.add)
                    last = dve.tensor_tensor_scan(sums[:, 1, t, :], ones[:, 0:1].to_broadcast([P, SEQ]), KC[:, t, :],
                                                  0.0, ALU.mult, ALU.add)
                link.then(last)
                for t in range(CT):
                    last = dve.tensor_scalar(bias[:, t, :], sums[:, 0, t, :], conv_b[:, t:t + 1], None, ALU.mult)
                link.then(last)
                for t in range(CT):
                    last = dve.scalar_tensor_tensor(out=bias[:, t, :], in0=sums[:, 1, t, :], scalar=b_in[:, t:t + 1],
                                                    in1=bias[:, t, :], op0=ALU.mult, op1=ALU.add)
                last.then_inc(ev["bias_done"], 1)
                dve.wait_ge(ev["bias_psum"], 1)
                dve.tensor_scalar(bias_t[:, :], bank[0][:, 0:SEQ], b_out[:, 0:1], None, ALU.add)


def recurrence(k, scratch_k, win_hi, win_lo, Y):
    nc = k.nc
    with ExitStack() as st:
        sb = lambda name, shape, dt=F32: k.sb(f"rec_{name}", shape, dt, st)
        COLS = 3 * BATCH
        U = sb("U", [P, 2, CH, COLS], BF16)
        T = [sb(f"T{i}", [P, TCH, SEQ * 3], BF16) for i in range(RING)]
        rest = [sb(f"rest{i}", [P, CH]) for i in range(2)]
        bank = [k.ps(f"rec_bank{i}", stack=st) for i in range(4)]
        ev = events(k, "rec", "u_psum u_hi u_rest u_mid u_done t_used y_psum y_done", st)
        arrived = [k.sem(f"toeplitz_in{i}", st) for i in range(RING)]
        width = PAD * 3

        def toeplitz(load):
            return bass.AP(scratch_k.tensor, load * TCH * width + 3, [[3, P], [width, TCH], [1, SEQ * 3]])

        with nc.Block() as block:
            @block.sync
            def _(sp):
                for load in range(LOADS):
                    if load >= RING:
                        sp.wait_ge(ev["t_used"], load - RING + 1)
                    sp.dma_start(T[load % RING][:, :, :], toeplitz(load)).then_inc(arrived[load % RING], 16)

            @block.tensor
            def _(pe):
                for b in range(BATCH):
                    for half in range(2):
                        i = 2 * b + half
                        at = b * PADDED + 1 + half * P
                        if i >= 2:
                            pe.wait_ge(ev["u_rest"], i - 1)
                        mm3(pe, bank[i % 2][:, 0:CH], k.xh[:, at:at + P], k.xl[:, at:at + P], win_hi[:, :],
                            win_lo[:, :]).then_inc(ev["u_psum"], 1)
                pe.wait_ge(ev["u_done"], 2 * BATCH)
                with pe.Fori(0, LOADS // RING) as r:
                    for i in range(RING):
                        load = r * RING + i
                        pe.wait_ge(arrived[i], 16 * r + 16)
                        for c in range(TCH):
                            out = bank[2 * (i % 2) + c // 4]
                            if c % 4 == 0:
                                pe.wait_ge(ev["y_done"], 2 * load + c // 4 + 1)
                            t3 = T[i][:, c, :].rearrange("p (t q) -> p t q", q=3)
                            near, far = t3[:, 0:P, :], t3[:, P:SEQ, :]
                            u0, u1 = (U[:, h, bass.ds(load * TCH + c, 1), :].rearrange("p a n -> p (a n)")
                                      for h in range(2))
                            first = out[:, (c % 4) * 2 * COLS:(c % 4) * 2 * COLS + COLS]
                            second = out[:, (c % 4) * 2 * COLS + COLS:(c % 4 + 1) * 2 * COLS]
                            for q in range(3):
                                pe.matmul(first, near[:, :, q], u0, start=(q == 0), stop=(q == 2))
                            for q in range(3):
                                pe.matmul(second, far[:, :, q], u0, start=(q == 0), stop=False)
                                last = pe.matmul(second, near[:, :, q], u1, start=False, stop=(q == 2))
                            if c % 4 == 3:
                                last.then_inc(ev["y_psum"], 1)
                        last = pe.matmul(k.turn[0:32, 0:8], k.identb[:, 0:32], k.identb[:, 0:8], start=True, stop=True)
                        last.then_inc(ev["t_used"], 1)

            @block.scalar
            def _(act):
                with act.Fori(0, BATCH) as b:
                    for half in range(2):
                        i = b * 2 + half
                        parts = U[:, half, :, :].rearrange("p c (q b) -> p c q b", q=3)
                        act.wait_ge(ev["u_psum"], i + 1)
                        act.activation(parts[:, :, 0, bass.ds(b, 1)].rearrange("p c a -> p (c a)"),
                                       bank[half][:, 0:CH], ACT.Copy).then_inc(ev["u_hi"], 1)
                        act.wait_ge(ev["u_rest"], i + 1)
                        act.activation(parts[:, :, 1, bass.ds(b, 1)].rearrange("p c a -> p (c a)"),
                                       rest[half][:, :], ACT.Copy).then_inc(ev["u_mid"], 1)

            @block.vector
            def _(dve):
                dve.memset(k.tick[:, :], 0.0).then_inc(ev["y_done"], 4)
                with dve.Fori(0, BATCH) as b:
                    for half in range(2):
                        i = b * 2 + half
                        parts = U[:, half, :, :].rearrange("p c (q b) -> p c q b", q=3)
                        hi, mid, lo = (parts[:, :, q, bass.ds(b, 1)].rearrange("p c a -> p (c a)") for q in range(3))
                        dve.wait_ge(ev["u_hi"], i + 1)
                        dve.tensor_tensor(rest[half][:, :], bank[half][:, 0:CH], hi, ALU.subtract)\
                           .then_inc(ev["u_rest"], 1)
                        dve.wait_ge(ev["u_mid"], i + 1)
                        dve.tensor_tensor(lo, rest[half][:, :], mid, ALU.subtract).then_inc(ev["u_done"], 1)
                with dve.Fori(0, LOADS // RING) as r:
                    for i in range(RING):
                        load = r * RING + i
                        for h in range(2):
                            dve.wait_ge(ev["y_psum"], 2 * load + h + 1)
                            parts = bank[2 * (i % 2) + h][:, 0:8 * COLS].rearrange("p (c q b) -> p c b q", q=3, b=BATCH)
                            out = Y[:, bass.ds(load * TCH + 4 * h, 4), :, :].rearrange("p c h b -> p (c h) b")
                            dve.tensor_reduce(out, parts, AX_X, ALU.add).then_inc(ev["y_done"], 1)


def project(k, wout, bias_t, Y, next_route):
    nc = k.nc
    base = k.turn0
    with ExitStack() as st:
        yc = [[k.sb(f"proj_y{i}{t}", [P, GROUP], F32, st) for t in range(CT)] for i in range(2)]
        bank = [k.ps(f"proj_bank{i}", stack=st) for i in range(4)]
        ev = events(k, "proj", "turned copied", st)
        with nc.Block() as block:
            @block.tensor
            def _(pe):
                def turn_group(g):
                    for t in range(CT):
                        if g >= 2:
                            pe.wait_ge(ev["copied"], CT * (g - 2) + t + 1)
                        for j in range(GT):
                            b, half = g * GB + j // 2, j % 2
                            last = pe.transpose(bank[2 * (g % 2) + t][:, j * P:(j + 1) * P],
                                                Y[:, t * P:(t + 1) * P, half, b], k.ident[:, :])
                        last.then_inc(ev["turned"], 1)

                turn_group(0)
                for g in range(GROUPS):
                    if g + 1 < GROUPS:
                        turn_group(g + 1)
                    pe.wait_ge(ev["copied"], CT * (g + 1))
                    if g:
                        pe.wait_ge(k.y_copied, base + g)
                    for t in range(CT):
                        pe.matmul(k.ypsum[:, :], wout[:, t, :], yc[g % 2][t][:, :], start=(t == 0), stop=False)
                    for b in range(GB):
                        last = pe.matmul(k.ypsum[:, b * SEQ:(b + 1) * SEQ], k.ident[:, :], bias_t[:, :],
                                         start=False, stop=(b == GB - 1))
                    last.then_inc(k.y_done, 1)
                    for step in range(STEPS):
                        post_tensor(k, pe, step, base + g, g, next_route)

            @block.scalar
            def _(act):
                def copy_group(g):
                    for t in range(CT):
                        act.wait_ge(ev["turned"], CT * g + t + 1)
                        act.activation(yc[g % 2][t][:, :], bank[2 * (g % 2) + t][:, :], ACT.Copy)\
                           .then_inc(ev["copied"], 1)

                copy_group(0)
                for g in range(GROUPS):
                    for step in range(STEPS):
                        post_scalar(k, act, step, base + g, g, next_route)
                    if g + 1 < GROUPS:
                        copy_group(g + 1)

            @block.vector
            def _(dve):
                with dve.Fori(0, GROUPS) as g:
                    for step in range(STEPS):
                        post_vector(k, dve, step, base + g, g, next_route)

            @block.gpsimd
            def _(pool):
                with pool.Fori(0, GROUPS) as g:
                    post_gpsimd(k, pool, base + g)


def build(nc, io):
    with ExitStack() as stack:
        k = Chip(nc, io, stack)
        share(k)
        share_routes(k)
        share_moe(k)
        build_constants(k)
        build_tables(k)
        load_params(k)
        ssm(k, ROUTES["ffn0"])
        ffn0(k, None)
        load_attn(k)
        attn1(k, ROUTES["ffn1"])
        ffn1(k, None)
        attn2(k, ROUTES["ffn2"])
        ffn2(k, None)
        attn3(k, ROUTES["ffn3"])
        ffn3(k, None)



def kernel(**inputs):
    import numpy as np
    from concourse import bacc
    from concourse.bass_utils import run_bass_kernel_spmd

    nc = bacc.Bacc("TRN2", target_bir_lowering=False, num_devices=1)
    arrays, io = {}, {}
    for name, value in inputs.items():
        a = np.ascontiguousarray(value)
        a = a.reshape(1) if a.ndim == 0 else a
        arrays[f"in_{name}"] = a
        io[name] = nc.dram_tensor(f"in_{name}", a.shape, mybir.dt.from_np(a.dtype), kind="ExternalInput").ap()
    io["out"] = nc.dram_tensor("out", (TOKENS, D), F32, kind="ExternalOutput").ap()
    build(nc, io)
    r = run_bass_kernel_spmd(nc, [arrays], core_ids=[0])
    return r.results[0]["out"].reshape(BATCH, SEQ, D)
```

```python
from contextlib import ExitStack

import concourse.bass as bass
from concourse import mybir

F32 = mybir.dt.float32
F32R = mybir.dt.float32r
BF16 = mybir.dt.bfloat16
ALU = mybir.AluOpType
ACT = mybir.ActivationFunctionType
AX_X = mybir.AxisListType.X

P = 128
BATCH, SEQ, D = 16, 256, 128
TOKENS = BATCH * SEQ
TILES = TOKENS // P
GROUP = 512
GROUPS = TOKENS // GROUP
GT = GROUP // P
GB = GROUP // SEQ
PADDED = SEQ + 2
GCOLS = GB * PADDED
EPS = 1e-5


class Chip:

    def __init__(self, nc, io, stack):
        self.nc, self.io, self.stack = nc, io, stack
        self.turn0 = 0

    def sb(self, name, shape, dt=F32, stack=None):
        return (stack or self.stack).enter_context(self.nc.sbuf_tensor(name, shape, dt))

    def ps(self, name, shape=(P, 512), dt=F32, stack=None):
        return (stack or self.stack).enter_context(self.nc.psum_tensor(name, list(shape), dt))

    def sem(self, name, stack=None):
        return (stack or self.stack).enter_context(self.nc.semaphore(name))


def share(k):
    k.x = k.sb("x", [P, TILES, D])
    k.xh = k.sb("xn_hi", [P, BATCH * PADDED], F32R)
    k.xl = k.sb("xn_lo", [P, BATCH * PADDED], F32R)
    k.ident = k.sb("ident", [P, P])
    k.identb = k.sb("identb", [P, P], BF16)
    k.half_neg = k.sb("half_neg", [P, 1])
    k.eps = k.sb("eps", [P, 1])
    k.tick = k.sb("tick", [P, 1])
    k.yT = k.sb("y_features", [P, GROUP])
    k.stats = k.sb("ln_stats", [P, GT, 6])
    k.moments = k.sb("ln_moments", [P, GT, 2])
    k.var = k.sb("ln_var", [P, GT])
    k.rstd = k.sb("ln_rstd", [P, GT])
    k.xn = k.sb("xn_tokens", [P, GT, D])
    k.ypsum = k.ps("ypsum")
    k.turn = k.ps("turn")
    k.consts_done = k.sem("consts_done")
    k.pads_done = k.sem("pads_done")
    k.y_done = k.sem("y_done")
    k.y_copied = k.sem("y_copied")
    k.y_turned = k.sem("y_turned")
    k.x_done = k.sem("x_done")
    k.stats_done = k.sem("stats_done")
    k.moments_done = k.sem("moments_done")
    k.var_done = k.sem("var_done")
    k.rstd_done = k.sem("rstd_done")
    k.xn_done = k.sem("xn_done")
    k.xn_turned = k.sem("xn_turned")
    k.hi_done = k.sem("hi_done")
    k.lo_done = k.sem("lo_done")
    k.loads = [k.sem(f"load{i}") for i in range(9)]
    k.load_count = [0] * 9
    k.turn_left = k.lo_done
    k.stored = k.sem("stored")


def lo_hi(k, g):
    def view(t, shift=0):
        v = t[:, bass.ds(g * GCOLS, GCOLS)].rearrange("p (b s) -> p b s", b=GB)
        return v[:, :, 1 + shift:1 + shift + SEQ]
    return view


def mm3(pe, out, w_hi, w_lo, x_hi, x_lo, start=True, stop=True):
    pe.matmul(out, w_hi, x_hi, start=start, stop=False)
    pe.matmul(out, w_hi, x_lo, start=False, stop=False)
    return pe.matmul(out, w_lo, x_hi, start=False, stop=stop)


def build_constants(k):
    nc = k.nc
    with nc.Block() as block:
        @block.gpsimd
        def _(pool):
            pool.memset(k.ident[:, :], 0.0).then_inc(k.consts_done, 1)
            pool.memset(k.half_neg[:, :], -0.5).then_inc(k.consts_done, 1)
            pool.memset(k.eps[:, :], EPS).then_inc(k.consts_done, 1)
            pool.wait_ge(k.consts_done, 3)
            pool.affine_select(out=k.ident[:, :], in_=k.ident[:, :], compare_op=ALU.not_equal, fill=1.0,
                               base=0, pattern=[[-1, P]], channel_multiplier=1).then_inc(k.consts_done, 1)
            pool.wait_ge(k.consts_done, 4)
            pool.tensor_copy(k.identb[:, :], k.ident[:, :]).then_inc(k.consts_done, 1)

        @block.vector
        def _(dve):
            for t in (k.xh, k.xl):
                v = t[:, :].rearrange("p (b s) -> p b s", b=BATCH)
                dve.memset(v[:, :, 0:PADDED:PADDED - 1].bitcast(F32), 0.0).then_inc(k.pads_done, 1)



def post_add_scalar(k, act, n, bias):
    act.wait_ge(k.y_done, n + 1 - k.moe_groups)
    post_copy_scalar(k, act, bias)


def post_copy_scalar(k, act, bias):
    if bias is None:
        act.activation(k.yT[:, :], k.ypsum[:, :], ACT.Copy).then_inc(k.y_copied, 1)
    else:
        act.activation(k.yT[:, :], k.ypsum[:, :], ACT.Identity, bias=bias).then_inc(k.y_copied, 1)


def post_add_tensor(k, pe, n):
    pe.wait_ge(k.y_copied, n + 1)
    if not isinstance(n, int) or n > 0:
        pe.wait_ge(k.turn_left, n)
    for j in range(GT):
        last = pe.transpose(k.turn[:, j * P:(j + 1) * P], k.yT[:, j * P:(j + 1) * P], k.ident[:, :])
    last.then_inc(k.y_turned, 1)


def post_add_vector(k, dve, n, g):
    x = k.x[:, bass.ds(g * GT, GT), :]
    dve.wait_ge(k.y_turned, n + 1)
    dve.tensor_tensor(x, x, k.turn[:, :].rearrange("p (j d) -> p j d", j=GT), ALU.add).then_inc(k.x_done, 1)


def post_norm_part(k, dve, n, g, part):
    tile = lambda j: k.x[:, bass.ds(g * GT + j, 1), :].rearrange("p a d -> p (a d)")
    if part == 0:
        dve.wait_ge(k.x_done, n + 1)
        dve.memset(k.tick[:, :], 0.0)
    if part <= 1:
        for j in (2 * part, 2 * part + 1):
            last = dve.bn_stats(k.stats[:, j, :], tile(j))
    if part == 1:
        last.then_inc(k.stats_done, 1)
    if part == 2:
        dve.wait_ge(k.stats_done, n + 1)
        dve.memset(k.tick[:, :], 0.0)
        for j in range(GT):
            last = dve.bn_aggr(k.moments[:, j, :], k.stats[:, j, :])
        last.then_inc(k.moments_done, 1)
    if part == 3:
        dve.wait_ge(k.moments_done, n + 1)
        dve.wait_ge(k.rstd_done, n + 1)
    if part >= 3:
        for j in (2 * part - 6, 2 * part - 5):
            last = dve.tensor_scalar(k.xn[:, j, :], tile(j), k.moments[:, j, 0:1], k.rstd[:, j:j + 1],
                                     ALU.subtract, ALU.mult)
    if part == 4:
        last.then_inc(k.xn_done, 1)


def post_norm_vector(k, dve, n, g):
    for part in range(5):
        post_norm_part(k, dve, n, g, part)


def post_norm_gpsimd(k, pool, n):
    pool.wait_ge(k.moments_done, n + 1)
    pool.tensor_tensor(k.var[:, :], k.moments[:, :, 1], k.eps[:, 0:1].to_broadcast([P, GT]), ALU.add).then_inc(k.var_done, 1)
    pool.wait_ge(k.var_done, n + 1)
    pool.tensor_tensor(k.rstd[:, :], k.var[:, :], k.half_neg[:, 0:1].to_broadcast([P, GT]), ALU.pow)\
        .then_inc(k.rstd_done, 1)


def post_turn_tensor(k, pe, n):
    pe.wait_ge(k.xn_done, n + 1)
    for j in range(GT):
        last = pe.transpose(k.turn[:, j * P:(j + 1) * P], k.xn[:, j, :], k.ident[:, :])
    last.then_inc(k.xn_turned, 1)


def post_turn_scalar(k, act, n, g):
    act.wait_ge(k.xn_turned, n + 1)
    act.activation(lo_hi(k, g)(k.xh), k.turn[:, :].rearrange("p (b s) -> p b s", b=GB), ACT.Copy)\
        .then_inc(k.hi_done, 1)


def post_turn_vector(k, dve, n, g):
    dve.wait_ge(k.hi_done, n + 1)
    view = lo_hi(k, g)
    dve.tensor_tensor(view(k.xl), k.turn[:, :].rearrange("p (b s) -> p b s", b=GB), view(k.xh).bitcast(F32),
                      ALU.subtract).then_inc(k.lo_done, 1)



class Route:

    def __init__(self, kind, experts, index):
        self.kind, self.e, self.index = kind, experts, index
        self.halves = 2 if experts == 64 else 1
        self.rows = 3 * experts // self.halves
        self.logits = 1 if kind == "steps" else experts


class Chain:

    def __init__(self, eng, sem, base):
        self.eng, self.sem, self.base, self.n = eng, sem, base, 0

    def then(self, instruction):
        self.n += 1
        instruction.then_inc(self.sem, 1)
        self.eng.wait_ge(self.sem, self.base + self.n)


ROUTE_LINKS = {"top8": 9, "top2": 12, "steps": 7, "zone": 25}


def share_routes(k):
    k.mask = k.sb("mask", [96, 2, TOKENS], BF16)
    k.lower = k.sb("lower8", [P, 8, 8])
    k.mod4 = k.sb("mod4", [P, 4])
    k.turn4 = k.sb("step_expert", [P, 4, 4])
    k.sel64 = k.sb("sel64", [96, 16, P], BF16)
    k.sel8 = k.sb("sel8", [24, 8, P], BF16)
    k.sel4 = k.sb("sel4", [12, 4, P], BF16)
    k.logits_done = k.sem("logits_done")
    k.logits_copied = k.sem("logits_copied")
    k.logits_turned = k.sem("logits_turned")
    k.aff_done = k.sem("aff_done")
    k.dist_done = k.sem("dist_done")
    k.exps_done = k.sem("exps_done")
    k.route_link = k.sem("route_link")
    k.parts_done = k.sem("parts_done")
    k.parts_turned = k.sem("parts_turned")
    k.masks_done = k.sem("masks_done")
    k.tables_done = k.sem("tables_done")
    k.tables_link = k.sem("tables_link")
    k.params_in = k.sem("params_in")
    k.params_done = k.sem("params_done")
    k.route_base = 0


def route_scratch(k, name, stack):
    sb = lambda what, shape, dt=F32: k.sb(f"{name}_{what}", shape, dt, stack)
    k.routes = k.ps(f"{name}_routes", stack=stack)
    k.logT = sb("logits_experts", [P, GROUP])
    k.aff = sb("affinity", [P, GT, 64])
    k.best = sb("best8", [P, GT, 8])
    k.rep = sb("best_marked", [P, GT, 64])
    k.sel = sb("selected", [P, GT, 64])
    k.tot = sb("selected_sum", [P, GT])
    k.inv = sb("selected_inverse", [P, GT])
    k.parts = sb("weights_bf16", [P, GT, 192], BF16)
    k.rest = sb("weights_rest", [P, GT, 64])
    k.w = sb("weights", [P, GT, 64])
    k.pair = sb("pairs", [P, 2, GT, 64])
    k.rank = sb("rank", [P, GT, 8])
    k.exps = sb("zone_exps", [P, 2, GT, 8])
    k.zone = sb("zone_parts", [P, 4, GT, 8])
    k.small = sb("zone_sums", [P, 4, GT])
    with k.nc.Block() as block:
        @block.vector
        def _(dve):
            dve.memset(k.logT[:, :], 0.0)


def build_tables(k, block):
    @block.gpsimd
    def _(pool):
        link = Chain(pool, k.tables_link, 0)
        link.then(pool.memset(k.sel64[:, :, :], 0.0))
        link.then(pool.memset(k.sel8[:, :, :], 0.0))
        link.then(pool.memset(k.sel4[:, :, :], 0.0))
        link.then(pool.memset(k.lower[:, :, :], 1.0))
        for part in range(3):
            link.then(pool.affine_select(
                out=k.sel64[:, :, :].rearrange("p c (e i) -> p c e i", e=2),
                in_=k.sel64[:, :, :].rearrange("p c (e i) -> p c e i", e=2), compare_op=ALU.not_equal,
                fill=1.0, base=-32 * part, pattern=[[-2, 16], [-1, 2], [0, 64]], channel_multiplier=1))
            link.then(pool.affine_select(
                out=k.sel8[:, :, :], in_=k.sel8[:, :, :], compare_op=ALU.not_equal, fill=1.0,
                base=-8 * part, pattern=[[-1, 8], [0, P]], channel_multiplier=1))
            link.then(pool.affine_select(
                out=k.sel4[:, :, :], in_=k.sel4[:, :, :], compare_op=ALU.not_equal, fill=1.0,
                base=-4 * part, pattern=[[-1, 4], [0, P]], channel_multiplier=1))
        link.then(pool.affine_select(out=k.lower[:, :, :], in_=k.lower[:, :, :], compare_op=ALU.is_gt,
                                     fill=0.0, base=0, pattern=[[1, 8], [-1, 8]], channel_multiplier=0))

    @block.vector
    def _(dve):
        dve.tensor_reduce(k.mod4[:, :], k.ident[:, :].rearrange("p (q m) -> p m q", m=4), AX_X, ALU.add)\
            .then_inc(k.tables_done, 1)
        dve.wait_ge(k.tables_done, 1)
        for e in range(4):
            for i in range(4):
                m = (e - i) % 4
                dve.tensor_copy(k.turn4[:, e, i:i + 1], k.mod4[:, m:m + 1]).then_inc(k.tables_done, 1)


def route_tensor(k, pe, step, n, g, r):
    m = r.index * GROUPS + g
    if step == 0:
        pe.wait_ge(k.lo_done, n + 1)
        if not isinstance(m, int) or m > 0:
            pe.wait_ge(k.masks_done, m)
        view = lo_hi(k, g)
        mm3(pe, k.routes[:, :], k.router_hi[r.kind], k.router_lo[r.kind], view(k.xh), view(k.xl))\
            .then_inc(k.logits_done, 1)
    if step == 1:
        pe.wait_ge(k.logits_copied, m + 1)
        for j in range(GT):
            last = pe.transpose(k.routes[:, j * P:(j + 1) * P], k.logT[:, j * P:(j + 1) * P], k.ident[:, :])
        last.then_inc(k.logits_turned, 1)
    if step == 2:
        pe.wait_ge(k.parts_done, m + 1)
        turnb = k.routes[:, :].bitcast(BF16).rearrange("p (h s) -> p h s", h=2)
        for h in range(r.halves):
            for j in range(GT):
                last = pe.transpose(turnb[0:r.rows, h, j * P:(j + 1) * P],
                                    k.parts[:, j, h * r.rows:(h + 1) * r.rows], k.identb[:, :])
        last.then_inc(k.parts_turned, 1)


def route_scalar(k, act, step, n, g, r):
    m = r.index * GROUPS + g
    e = r.logits
    logits = k.routes[:, :].rearrange("p (j e) -> p j e", j=GT)[:, :, 0:e]
    if step == 0:
        act.wait_ge(k.logits_done, m + 1)
        act.activation(k.logT[0:e, :], k.routes[0:e, :], ACT.Copy).then_inc(k.logits_copied, 1)
    if step == 1:
        act.wait_ge(k.logits_turned, m + 1)
        if r.kind == "zone":
            act.activation(k.aff[:, :, 0:e], logits, ACT.Sigmoid, scale=k.inv_temp[:, 0:1]).then_inc(k.aff_done, 1)
        elif r.kind == "steps":
            act.activation(k.aff[:, :, 0:e], logits, ACT.Sigmoid, bias=k.bu[:, 0:1]).then_inc(k.aff_done, 1)
        else:
            act.activation(k.aff[:, :, 0:e], logits, ACT.Sigmoid).then_inc(k.aff_done, 1)
    if step == 2 and r.kind == "zone":
        act.wait_ge(k.dist_done, g + 1)
        act.activation(k.exps[:, 0, :, :], k.zone[:, 0, :, :], ACT.Exp, scale=-1.0 / 0.1)
        act.activation(k.exps[:, 1, :, :], k.zone[:, 0, :, :], ACT.Exp, scale=-1.0 / 0.3).then_inc(k.exps_done, 1)
    if step == 3:
        act.wait_ge(k.parts_turned, m + 1)
        turnb = k.routes[:, :].bitcast(BF16).rearrange("p (h s) -> p h s", h=2)
        act.activation(k.mask[0:r.rows, 0:r.halves, bass.ds(g * GROUP, GROUP)], turnb[0:r.rows, 0:r.halves, :],
                       ACT.Copy).then_inc(k.masks_done, 1)


def top2_vector(k, dve, link, p):
    gt, eq = (k.pair[:, i, :, :].rearrange("p j (e f) -> p j e f", e=8) for i in range(2))
    other = p.unsqueeze(2).to_broadcast([P, GT, 8, 8])
    own = p.unsqueeze(3).to_broadcast([P, GT, 8, 8])
    dve.tensor_tensor(gt, other, own, ALU.is_gt)
    link.then(dve.tensor_tensor(eq, other, own, ALU.is_equal))
    link.then(dve.tensor_tensor(eq, eq, k.lower[:, :, :].unsqueeze(1).to_broadcast([P, GT, 8, 8]), ALU.mult))
    link.then(dve.tensor_tensor(gt, gt, eq, ALU.add))
    link.then(dve.tensor_reduce(k.rank[:, :, :], gt, AX_X, ALU.add))
    link.then(dve.scalar_tensor_tensor(out=k.sel[:, :, 0:8], in0=k.rank[:, :, :], scalar=2.0, in1=p,
                                       op0=ALU.is_lt, op1=ALU.mult))


def route_vector(k, dve, step, n, g, r):
    m = r.index * GROUPS + g
    e = r.e
    links = ROUTE_LINKS[r.kind]
    C0, LOW, HIGH = 1.0 / 2.718281828459045, 0.5 - 0.28768207245178085, 0.5
    aff = k.aff[:, :, 0:r.logits]
    if step == 0 and r.kind == "zone":
        link = Chain(dve, k.route_link, k.route_base + g * links)
        dve.wait_ge(k.aff_done, m + 1)
        link.then(dve.tensor_scalar(k.zone[:, 1, :, :], aff, C0, None, ALU.subtract))
        link.then(dve.tensor_scalar(k.zone[:, 2, :, :], aff, LOW, None, ALU.is_ge))
        link.then(dve.scalar_tensor_tensor(out=k.zone[:, 3, :, :], in0=aff, scalar=HIGH, in1=k.zone[:, 2, :, :],
                                           op0=ALU.is_le, op1=ALU.mult))
        dve.scalar_tensor_tensor(out=k.zone[:, 0, :, :], in0=k.zone[:, 1, :, :], scalar=-1.0,
                                 in1=k.zone[:, 1, :, :], op0=ALU.mult, op1=ALU.max).then_inc(k.dist_done, 1)
    if step != 1:
        return
    link = Chain(dve, k.route_link, k.route_base + g * links)
    dve.wait_ge(k.aff_done, m + 1)
    sel, w = k.sel[:, :, 0:e], k.w[:, :, 0:e]

    def scale(out, values, total, floor, how):
        link.then(dve.tensor_scalar(k.tot[:, :], total, floor, None, how))
        link.then(dve.reciprocal(k.inv[:, :], k.tot[:, :]))
        link.then(dve.tensor_tensor(out, values, k.inv[:, :].unsqueeze(2).to_broadcast([P, GT, e]), ALU.mult))

    if r.kind == "top8":
        dve.memset(k.tick[:, :], 0.0)
        for j in range(GT):
            last = dve.max(k.best[:, j, :], k.aff[:, j, :])
        link.then(last)
        dve.memset(k.tick[:, :], 0.0)
        for j in range(GT):
            dve.match_replace(k.rep[:, j, :], k.best[:, j, :], k.aff[:, j, :], -1.0)
        link.then(dve.tensor_reduce(k.small[:, 0, :], k.best[:, :, :], AX_X, ALU.add))
        link.then(dve.scalar_tensor_tensor(out=sel, in0=k.rep[:, :, :], scalar=-1.0, in1=aff,
                                           op0=ALU.is_equal, op1=ALU.mult))
        scale(w, sel, k.small[:, 0, :], 1e-9, ALU.add)
    if r.kind == "top2":
        top2_vector(k, dve, link, aff)
        link.then(dve.tensor_reduce(k.small[:, 0, :], sel, AX_X, ALU.add))
        scale(w, sel, k.small[:, 0, :], 1e-20, ALU.add)
    if r.kind == "steps":
        u = k.aff[:, :, 0:1]
        for i in range(4):
            last = dve.scalar_tensor_tensor(out=k.sel[:, :, i:i + 1], in0=u, scalar=i / 4.0, in1=u,
                                            op0=ALU.is_gt, op1=ALU.mult)
        link.then(last)
        for i in range(4):
            last = dve.tensor_scalar(k.rank[:, :, i:i + 1], k.sel[:, :, i:i + 1], 1.0 / (i + 1), None, ALU.mult)
        link.then(last)
        pick = k.pair[:, 0, :, 0:16].rearrange("p j (e i) -> p j e i", e=4)
        link.then(dve.tensor_tensor(pick, k.rank[:, :, 0:4].unsqueeze(2).to_broadcast([P, GT, 4, 4]),
                                    k.turn4[:, :, :].unsqueeze(1).to_broadcast([P, GT, 4, 4]), ALU.mult))
        link.then(dve.tensor_reduce(w, pick, AX_X, ALU.add))
    if r.kind == "zone":
        link.n = 3
        dve.wait_ge(k.exps_done, g + 1)
        inzone, fallback = k.zone[:, 2, :, :], k.exps[:, 1, :, :]
        link.then(dve.tensor_tensor(inzone, k.exps[:, 0, :, :], k.zone[:, 3, :, :], ALU.mult))
        link.then(dve.tensor_reduce(k.small[:, 1, :], inzone, AX_X, ALU.add))
        link.then(dve.tensor_scalar(k.small[:, 2, :], k.small[:, 1, :], 1e-8, None, ALU.is_lt))
        top2_vector(k, dve, link, fallback)
        link.then(dve.tensor_reduce(k.small[:, 0, :], sel, AX_X, ALU.add))
        scale(w, sel, k.small[:, 0, :], 1e-8, ALU.max)
        link.then(dve.tensor_tensor(w, w, inzone, ALU.subtract))
        link.then(dve.tensor_tensor(w, w, k.small[:, 2, :].unsqueeze(2).to_broadcast([P, GT, e]), ALU.mult))
        link.then(dve.tensor_tensor(sel, w, inzone, ALU.add))
        link.then(dve.tensor_reduce(k.small[:, 3, :], sel, AX_X, ALU.add))
        scale(w, sel, k.small[:, 3, :], 1e-8, ALU.max)
    half = e // r.halves
    parts = k.parts[:, :, 0:r.halves * r.rows].rearrange("p j (h q e) -> p j h q e", h=r.halves, q=3)

    def each(op):
        for h in range(r.halves):
            last = op(parts[:, :, h, :, :], slice(h * half, (h + 1) * half))
        return last

    link.then(each(lambda q, s: dve.tensor_copy(q[:, :, 0, :], k.w[:, :, s])))
    link.then(each(lambda q, s: dve.tensor_tensor(k.rest[:, :, s], k.w[:, :, s], q[:, :, 0, :], ALU.subtract)))
    link.then(each(lambda q, s: dve.tensor_copy(q[:, :, 1, :], k.rest[:, :, s])))
    assert link.n == links, (r.kind, link.n)
    each(lambda q, s: dve.tensor_tensor(q[:, :, 2, :], k.rest[:, :, s], q[:, :, 1, :], ALU.subtract))\
        .then_inc(k.parts_done, 1)



STEPS = 16


def post_tensor(k, pe, step, n, g, route):
    if step == 1:
        post_add_tensor(k, pe, n)
    if step == 4:
        post_turn_tensor(k, pe, n)
    if route and step in (7, 9, 14):
        route_tensor(k, pe, {7: 0, 9: 1, 14: 2}[step], n, g, route)


def post_scalar(k, act, step, n, g, route, bias=None):
    if step == 0:
        post_add_scalar(k, act, n, bias)
    if step == 5:
        post_turn_scalar(k, act, n, g)
    if route and step in (8, 10, 12, 15):
        route_scalar(k, act, {8: 0, 10: 1, 12: 2, 15: 3}[step], n, g, route)


def post_vector(k, dve, step, n, g, route):
    if step == 2:
        post_add_vector(k, dve, n, g)
        post_norm_vector(k, dve, n, g)
    if step == 20:
        post_add_vector(k, dve, n, g)
    if 20 < step <= 25:
        post_norm_part(k, dve, n, g, step - 21)
    if step == 6:
        post_turn_vector(k, dve, n, g)
    if route and step in (11, 13):
        route_vector(k, dve, {11: 0, 13: 1}[step], n, g, route)


def post_gpsimd(k, pool, n):
    post_norm_gpsimd(k, pool, n)


def steps_at(c, chunks):
    return [s for s in range(STEPS) if s * chunks // STEPS == c]



class Moe:

    def __init__(self, name, kind, chunks, route, sel, sel_of, sources, shared=None, load=None):
        self.name, self.kind, self.chunks, self.route = name, kind, chunks, route
        self.sel, self.sel_of, self.sources, self.shared = sel, sel_of, sources, shared
        self.all = chunks + (shared is not None)
        self.step = load or chunks
        self.slots = 2 if load else 1

    def allocate(self, k, stack):
        n = len(self.sources)
        self.hi = k.sb(f"{self.name}_hi", [P, n, self.all, P], F32R, stack)
        self.lo = k.sb(f"{self.name}_lo", [P, n, self.all, P], F32R, stack)
        self.raw = k.sb(f"{self.name}_raw", [P, n, self.slots * self.step, P], F32, stack)
        self.loaded = k.loads[:self.slots]
        self.before = k.load_count[:self.slots]
        self.split0 = k.split0
        for load in range(self.load_of(self.all - 1) + 1):
            k.load_count[load % self.slots] += 16 * n

    def load_of(self, c):
        return c // self.step

    def wait_load(self, eng, c):
        load = self.load_of(c)
        slot = load % self.slots
        eng.wait_ge(self.loaded[slot], self.before[slot] + 16 * len(self.sources) * (load // self.slots + 1))

    def load(self, sp, lo_split):
        for at in range(0, self.all, self.step):
            load = self.load_of(at)
            slot = load % self.slots
            if load >= self.slots:
                sp.wait_ge(lo_split, self.split0 + (load - self.slots + 1) * self.step)
            here = slot * self.step
            for i, src in enumerate(self.sources):
                experts, chunks = src.shape[1], self.chunks
                out = self.raw[:, i, here:here + self.step, :]
                if at < chunks:
                    src = src[:, at * experts // chunks:(at + self.step) * experts // chunks, :]
                else:
                    src = self.shared[i]
                    out = self.raw[0:64, i, here, :] if i == 2 else self.raw[:, i, here, 0:64]
                sp.dma_start(out, src).then_inc(self.loaded[slot], 16)

    def pieces(self, c):
        at = c % (self.slots * self.step)
        if self.shared and c == self.all - 1:
            return [(self.raw[:, 0:2, at, 0:64], self.hi[:, 0:2, c, 0:64], self.lo[:, 0:2, c, 0:64]),
                    (self.raw[0:64, 2, at, :], self.hi[0:64, 2, c, :], self.lo[0:64, 2, c, :])]
        return [(self.raw[:, :, at, :], self.hi[:, :, c, :], self.lo[:, :, c, :])]


def share_moe(k):
    k.chunk0 = k.mid0 = k.split0 = k.moe_groups = 0
    k.padded = k.sem("padded")
    k.hi_split = k.sem("hi_split")
    k.lo_split = k.sem("lo_split")
    k.g_done = k.sem("g_done")
    k.u_done = k.sem("u_done")
    k.r_done = k.sem("r_done")
    k.t_done = k.sem("t_done")
    k.a_done = k.sem("a_done")
    k.ahi_done = k.sem("ahi_done")
    k.alo_done = k.sem("alo_done")
    k.down_done = k.sem("down_done")


POST_AT = {8: {3: (0,), 4: (1, 20), 5: (21, 22), 6: (23,), 7: (24, 25, 4, 5, 6)},
           16: {3: (0,), 4: (1,), 5: (20,), 6: (21,), 7: (22,), 8: (23,), 10: (24,), 11: (25,), 13: (4,),
                14: (5,), 15: (6,)},
           33: {2: (0,), 4: (1,), 6: (20,), 8: (21,), 10: (22,), 12: (23,), 15: (24,), 17: (25,), 20: (4,),
                22: (5,), 24: (6,)}}


def moe_stage(k, s, load_here=False, bias1=None, b2=None, last=False):
    nc, C = k.nc, s.all
    base, chunk0, mid0, split0 = k.turn0, k.chunk0, k.mid0, k.split0
    gated = s.kind == "gated"
    n_down = len(s.sources) - 1
    if last:
        k.turn_left = k.x_done
    RING_A = 3 if C % 3 == 0 else 4
    LAG = RING_A - 1
    assert C % RING_A == 0
    with ExitStack() as st:
        sb = lambda name, shape, dt=F32: k.sb(f"{s.name}_{name}", shape, dt, st)
        a, ahi, alo = ([sb(f"{n}{i}", [P, GROUP], dt) for i in range(RING_A)]
                       for n, dt in (("a", F32), ("ahi", F32R), ("alo", F32R)))
        RING_G = 2 if gated else 4
        G = [k.ps(f"{s.name}_G{i}", stack=st) for i in range(RING_G)]
        U = [k.ps(f"{s.name}_U{i}", stack=st) for i in range(2)] if gated else []
        M = [k.ps(f"{s.name}_M{i}", stack=st) for i in range(2)]

        def masked(c):
            return not (s.shared and c == C - 1)

        def banks(c):
            return (G[c % RING_G], U[c % 2] if gated else None) if masked(c) else (M[0], M[1])

        def at(g, c):
            return chunk0 + g * C + c

        def exists(g, c, n):
            return not isinstance(g, int) or g * C + c >= n

        def behind(f, g, c, n):
            if exists(g, c, n):
                f(*((g, c - n) if c >= n else (g - 1, C + c - n)))

        def post(f, eng, g, c):
            if exists(g, c, C) and c in POST_AT[C]:
                for step in POST_AT[C][c]:
                    if step in (0, 1, 20) or not last:
                        f(k, eng, step, base + g - 1, g - 1, None)

        def groups(eng, main, finish):
            main(0)
            with eng.Fori(1, GROUPS) as g:
                main(g)
            finish()

        with nc.Block() as block:
            @block.tensor
            def _(pe):
                def gate_up(g, c):
                    view = lo_hi(k, g)
                    xh, xl = view(k.xh), view(k.xl)
                    b = c % 2
                    if isinstance(g, int) and g == 0:
                        if not masked(c):
                            pe.wait_ge(k.padded, 4)
                        pe.wait_ge(k.lo_split, split0 + c + 1)
                    if exists(g, c, RING_G):
                        pe.wait_ge(k.r_done, at(g, c) - RING_G + 1)
                    if exists(g, c, 2) and not masked(c):
                        pe.wait_ge(k.a_done, at(g, c) - 1)
                    gate, up = banks(c)
                    pe.matmul(gate[:, :], s.hi[:, 0, c, :], xh, start=True, stop=False)
                    pe.matmul(gate[:, :], s.hi[:, 0, c, :], xl, start=False, stop=False)
                    if not gated and exists(g, c, 2):
                        pe.wait_ge(k.a_done, at(g, c) - 1)
                    product = pe.matmul(gate[:, :], s.lo[:, 0, c, :], xh, start=False, stop=True)
                    product.then_inc(k.g_done, 1)
                    if gated:
                        if not masked(c):
                            pe.wait_ge(k.a_done, at(g, c))
                        elif exists(g, c, 2):
                            pe.wait_ge(k.a_done, at(g, c) - 1)
                        product = mm3(pe, up[:, :], s.hi[:, 1, c, :], s.lo[:, 1, c, :], xh, xl)
                    if masked(c):
                        if s.shared and c == 0 and exists(g, c, 1):
                            pe.wait_ge(k.r_done, at(g, c))
                        half, which = s.sel_of(c)
                        product = pe.matmul(M[b][:, :], s.sel[0:s.route.rows, which, :],
                                            k.mask[0:s.route.rows, half, bass.ds(g * GROUP, GROUP)],
                                            start=True, stop=True)
                    product.then_inc(k.u_done, 1)

                def down(g, c):
                    pe.wait_ge(k.ahi_done, at(g, c) + 1)
                    pe.wait_ge(k.alo_done, at(g, c) + 1)
                    if c == 0:
                        pe.wait_ge(k.y_copied, base + g)
                    i = c % RING_A
                    product = mm3(pe, k.ypsum[:, :], s.hi[:, n_down, c, :], s.lo[:, n_down, c, :], ahi[i][:, :], alo[i][:, :],
                                  start=(c == 0), stop=(c == C - 1))
                    product.then_inc(k.down_done, 1)
                    if c == 0 and b2 is not None:
                        for q in range(3):
                            pe.matmul(k.ypsum[:, :], b2[0:s.route.rows, q, :],
                                      k.mask[0:s.route.rows, 0, bass.ds(g * GROUP, GROUP)], start=False, stop=False)

                def main(g):
                    for c in range(C):
                        post(post_tensor, pe, g, c)
                        gate_up(g, c)
                        behind(down, g, c, LAG)

                def finish():
                    for c in range(C - LAG, C):
                        down(GROUPS - 1, c)
                    for step in (1,) if last else (1, 4):
                        post_tensor(k, pe, step, base + GROUPS - 1, GROUPS - 1, None)

                groups(pe, main, finish)

            @block.scalar
            def _(act):
                how = ACT.Silu if gated else ACT.Relu

                def split(c):
                    s.wait_load(act, c)
                    for raw, hi, _ in s.pieces(c):
                        last = act.activation(hi, raw, ACT.Copy)
                    last.then_inc(k.hi_split, 1)

                def rounded(g, c):
                    i = c % RING_A
                    act.wait_ge(k.a_done, at(g, c) + 1)
                    if exists(g, c, RING_A):
                        act.wait_ge(k.down_done, at(g, c) - RING_A + 1)
                    act.activation(ahi[i][:, :], a[i][:, :], ACT.Copy).then_inc(k.ahi_done, 1)

                def activate(g, c):
                    if exists(g, c, RING_A):
                        act.wait_ge(k.alo_done, at(g, c) - RING_A + 1)
                    act.wait_ge(k.g_done, at(g, c) + 1)
                    kw = {"bias": bias1[:, c:c + 1]} if bias1 is not None else {}
                    act.activation(a[c % RING_A][:, :], banks(c)[0][:, :], how, **kw).then_inc(k.r_done, 1)

                def main(g):
                    for c in range(C):
                        if isinstance(g, int) and g == 0 and c + 2 < C:
                            split(c + 2)
                        post(scalar_step, act, g, c)
                        activate(g, c)
                        behind(rounded, g, c, 1)

                def scalar_step(k, act, step, n, g, route):
                    if step == 0:
                        act.wait_ge(k.down_done, at(g, C - 1) + 1)
                        post_copy_scalar(k, act, None)
                    else:
                        post_scalar(k, act, step, n, g, route)

                def finish():
                    rounded(GROUPS - 1, C - 1)
                    for step in (0, 5):
                        if step == 0 or not last:
                            scalar_step(k, act, step, base + GROUPS - 1, GROUPS - 1, None)

                split(0)
                split(1)
                groups(act, main, finish)

            def rest(eng, g, c):
                i = c % RING_A
                eng.wait_ge(k.ahi_done, at(g, c) + 1)
                eng.tensor_tensor(alo[i][:, :], a[i][:, :], ahi[i][:, :].bitcast(F32), ALU.subtract).then_inc(k.alo_done, 1)

            rest_on_pool = s.kind == "relu2"

            @block.vector
            def _(dve):
                def split(c):
                    dve.wait_ge(k.hi_split, split0 + c + 1)
                    for raw, hi, lo in s.pieces(c):
                        last = dve.tensor_tensor(lo, raw, hi.bitcast(F32), ALU.subtract)
                    last.then_inc(k.lo_split, 1)

                def scale(g, c):
                    i = c % RING_A
                    dve.wait_ge(k.u_done, at(g, c) + 1)
                    dve.wait_ge(k.r_done, at(g, c) + 1)
                    up, mask = banks(c)[1][:, :] if gated else None, M[c % 2][:, :]
                    out = a[i][:, :]

                    def rest_before():
                        if not rest_on_pool:
                            behind(lambda g, c: rest(dve, g, c), g, c, 1)

                    if s.kind == "relu":
                        dve.tensor_tensor(out, out, mask, ALU.mult).then_inc(k.a_done, 1)
                        rest_before()
                    elif not masked(c):
                        dve.tensor_tensor(out, out, up, ALU.mult).then_inc(k.a_done, 1)
                        rest_before()
                        dve.memset(k.tick[:, :], 0.0).then_inc(k.t_done, 1)
                    else:
                        dve.tensor_tensor(out, out, mask if gated else out, ALU.mult).then_inc(k.t_done, 1)
                        rest_before()
                        dve.wait_ge(k.t_done, mid0 + g * C + c + 1)
                        dve.tensor_tensor(out, out, up if gated else mask, ALU.mult).then_inc(k.a_done, 1)

                def main(g):
                    for c in range(C):
                        if isinstance(g, int) and g == 0 and c + 2 < C:
                            split(c + 2)
                        post(vector_step, dve, g, c)
                        scale(g, c)

                def vector_step(k, dve, step, n, g, route):
                    if not last:
                        post_vector(k, dve, step, n, g, route)
                    elif step in (2, 20):
                        post_add_vector(k, dve, n, g)

                def finish():
                    if not rest_on_pool:
                        rest(dve, GROUPS - 1, C - 1)
                    for step in (2,) if last else (2, 6):
                        vector_step(k, dve, step, base + GROUPS - 1, GROUPS - 1, None)

                split(0)
                split(1)
                groups(dve, main, finish)

            @block.gpsimd
            def _(pool):
                if s.shared:
                    link = Chain(pool, k.padded, 0)
                    for part in (s.hi, s.lo):
                        link.then(pool.memset(part[:, 0:2, C - 1, 64:].bitcast(F32), 0.0))
                        link.then(pool.memset(part[64:, 2, C - 1, :].bitcast(F32), 0.0))

                def main(g):
                    for c in range(C):
                        if exists(g, c, C) and c == 6 and not last:
                            post_gpsimd(k, pool, base + g - 1)
                        if rest_on_pool:
                            behind(lambda g, c: rest(pool, g, c), g, c, 1)

                def finish():
                    if rest_on_pool:
                        rest(pool, GROUPS - 1, C - 1)
                    if not last:
                        post_gpsimd(k, pool, base + GROUPS - 1)

                if rest_on_pool:
                    groups(pool, main, finish)
                elif not last:
                    with pool.Fori(0, GROUPS) as g:
                        post_gpsimd(k, pool, base + g)

            @block.sync
            def _(sp):
                if load_here:
                    s.load(sp, k.lo_split)
                if last:
                    out = k.io["out"].rearrange("(t p) d -> p t d", p=P)
                    for g in range(GROUPS):
                        sp.wait_ge(k.x_done, base + g + 1)
                        sp.dma_start(out[:, g * GT:(g + 1) * GT, :], k.x[:, g * GT:(g + 1) * GT, :])\
                          .then_inc(k.stored, 16)
                    sp.wait_ge(k.stored, 16 * GROUPS)
    k.turn0 += GROUPS
    k.moe_groups += GROUPS
    k.chunk0 += GROUPS * C
    k.mid0 += 0 if s.kind == "relu" else GROUPS * C
    k.split0 += C


def share_params(k):
    k.inv_temp = k.sb("inv_temp", [P, 1])
    k.bu = k.sb("bu", [P, 1])
    k.b1 = k.sb("ffn2_b1", [P, 16])
    k.b2p = k.sb("ffn2_b2_parts", [12, 3, P], BF16)
    first = {"top8": 0, "top2": 64, "steps": 72, "zone": 73}
    k.router_used, width = 81, 73 + P + 1
    router_hi, router_lo = k.sb("router_hi", [P, width], F32R), k.sb("router_lo", [P, width], F32R)
    k.router_parts = (router_hi, router_lo)
    k.router_hi = {kind: router_hi[:, at:at + P] for kind, at in first.items()}
    k.router_lo = {kind: router_lo[:, at:at + P] for kind, at in first.items()}


def load_params(k, block, early):
    io, (router_hi, router_lo) = k.io, k.router_parts
    router = k.sb("router_raw", [P, router_hi.shape[1]], F32, early)
    temp, b2, b2r = (k.sb(n, s, F32, early) for n, s in (("temp", [P, 1]), ("b2", [12, P]), ("b2_rest", [12, P])))

    @block.sync
    def _(sp):
        n = 0
        with k.nc.allow_non_contiguous_dma(reason="a few columns of parameters"):
            for out, src in (
                (router[:, 0:64], io["L0_ffn_router_w"]),
                (router[:, 64:72], io["L1_ffn_router_w"].rearrange("e d -> d e")),
                (router[:, 72:73], io["L2_ffn_Wu"]),
                (router[:, 73:81], io["L3_ffn_Wr"]),
                (temp[:, :], io["L3_ffn_temperature"].partition_broadcast(P)),
                (k.bu[:, :], io["L2_ffn_bu"].partition_broadcast(P)),
                (k.b1[:, :], io["L2_ffn_b1"].rearrange("e (c p) -> p (e c)", p=P)),
                (b2[0:4, :], io["L2_ffn_b2"]),
                (b2[4:8, :], io["L2_ffn_b2"]),
                (b2[8:12, :], io["L2_ffn_b2"]),
            ):
                sp.dma_start(out, src).then_inc(k.params_in, 16)
                n += 16
        k.params_total = n
        sp.wait_ge(k.params_in, n)

    @block.vector
    def _(dve):
        link = Chain(dve, k.params_done, 0)
        link.then(dve.memset(router[:, k.router_used:], 0.0))
        dve.wait_ge(k.params_in, k.params_total)
        link.then(dve.tensor_copy(router_hi[:, :], router[:, :]))
        link.then(dve.tensor_tensor(router_lo[:, :], router[:, :], router_hi[:, :].bitcast(F32), ALU.subtract))
        link.then(dve.reciprocal(k.inv_temp[:, :], temp[:, :]))
        link.then(dve.tensor_copy(k.b2p[:, 0, :], b2[:, :]))
        link.then(dve.tensor_tensor(b2r[:, :], b2[:, :], k.b2p[:, 0, :], ALU.subtract))
        link.then(dve.tensor_copy(k.b2p[:, 1, :], b2r[:, :]))
        link.then(dve.tensor_tensor(k.b2p[:, 2, :], b2r[:, :], k.b2p[:, 1, :], ALU.subtract))


ROUTES = {"ffn0": Route("top8", 64, 0), "ffn1": Route("top2", 8, 1),
          "ffn2": Route("steps", 4, 2), "ffn3": Route("zone", 8, 3)}


def ffn0(io):
    each = lambda name: io[f"L0_ffn_expert_{name}_k"].rearrange("e h i -> h e i")
    return Moe("ffn0", "gated", 32, ROUTES["ffn0"], None, lambda c: (c // 16, c % 16),
               (each("gate"), each("up"), io["L0_ffn_expert_down_k"].rearrange("(c e) i h -> (e i) c h", e=2)),
               shared=(io["L0_ffn_shared_gate_w"], io["L0_ffn_shared_up_w"], io["L0_ffn_shared_down_w"]), load=2)


def ffn1(io):
    return Moe("ffn1", "relu2", 8, ROUTES["ffn1"], None, lambda c: (0, c),
               (io["L1_ffn_w1"].rearrange("d (e w) -> d e w", e=8),
                io["L1_ffn_w2"].rearrange("(e w) d -> w e d", e=8)))


def ffn2(io):
    return Moe("ffn2", "relu", 16, ROUTES["ffn2"], None, lambda c: (0, c // 4),
               (io["L2_ffn_W1"].rearrange("e d f -> d e f"), io["L2_ffn_W2"].rearrange("e (c f) d -> f (e c) d", f=P)))


def ffn3(io):
    return Moe("ffn3", "gated", 8, ROUTES["ffn3"], None, lambda c: (0, c),
               (io["L3_ffn_Wg"].rearrange("e d i -> d e i"), io["L3_ffn_Wu"].rearrange("e d i -> d e i"),
                io["L3_ffn_Wd"].rearrange("e i d -> i e d")))



def events(k, stage, names, stack):
    return {n: k.sem(f"{stage}_{n}", stack) for n in names.split()}


def load_attn(k):
    io, nc = k.io, k.nc
    sb = k.sb
    raw = {}

    a = k.a = {}
    split_shapes = [("shell_w", [P, 65])] + [(n, [P, P]) for n in (
        "vo_w", "q_w", "k_w", "v_w", "tap0", "tap1", "tap2", "now_k", "now_v", "now_r", "old_k", "old_v", "old_r")]
    for name, shape in split_shapes:
        a[name] = (sb(name + "_hi", shape, F32R), sb(name + "_lo", shape, F32R))
    for name, shape in (("omega_t", [65, 33]), ("combine_t", [64, 320]), ("vo_bias", [P, 1]), ("wp_t", [P, P]),
                        ("wp_bias", [P, 1]), ("wo_t", [P, P]), ("w_log", [P, 1]), ("rff", [P, 64]),
                        ("decay", [P, 384]), ("causal", [P, 384]), ("blocks", [P, P]), ("ones", [P, 1]),
                        ("u", [P, 1]), ("b_shell", [65, 1])):
        a[name] = sb("a_" + name, shape)
    with ExitStack() as early:
        def load(name, shape, src):
            raw[name] = sb(f"raw_{name}", shape, F32, early)
            loads.append((raw[name], src))
            return raw[name]

        loads = []
        square = ("L1_attn_W_v", "L1_attn_W_out", "L2_attn_Wq", "L2_attn_Wk", "L2_attn_Wv", "L2_attn_Wp",
                  "L3_attn_Wk", "L3_attn_Wv", "L3_attn_Wr", "L3_attn_Wo")
        for name in square:
            load(name, [P, P], io[name])
        load("shell", [64, P], io["L1_attn_W_shell"])
        load("charge", [P, 1], io["L1_attn_W_charge"].rearrange("a d -> d a"))
        load("omega", [32, 64], io["L1_attn_omega"])
        load("combine", [64, 320], io["L1_attn_W_combine"])
        column = lambda x: x.rearrange("(p a) -> p a", a=1)
        load("b_v", [P, 1], column(io["L1_attn_b_v"]))
        load("b_out", [P, 1], column(io["L1_attn_b_out"]))
        load("conv_b", [P, 1], column(io["L2_attn_conv_b"]))
        load("conv_w", [P, 3], io["L2_attn_conv_w"])
        load("bp", [P, 1], column(io["L2_attn_bp"]))
        load("log_temp", [P, 1], io["L1_attn_log_temp"].partition_broadcast(P))
        load("rff_row", [P, 32], io["L1_attn_rff_bias"].partition_broadcast(P))
        for m in "kvr":
            load(f"mix_{m}", [P, 1], io[f"L3_attn_mix_{m}"].rearrange("a b d -> d (a b)"))
        load("decay", [P, 1], column(io["L3_attn_time_decay"]))
        loads += [(a["u"], column(io["L3_attn_time_first"])),
                  (a["b_shell"][0:64, :], column(io["L1_attn_b_shell"])),
                  (a["b_shell"][64:65, :], column(io["L1_attn_b_charge"]))]

        for name, shape in split_shapes:
            a[name] = (sb(f"{name}_full", shape, F32, early), *a[name])
        inv_temp, e0, e1, e2 = (sb(n, [P, 1], F32, early) for n in ("att_inv_temp", "tmp_e0", "tmp_e1", "tmp_e2"))
        wout_t = sb("wout_t", [P, P], F32, early)
        rest = {m: sb(f"rest_{m}", [P, 1], F32, early) for m in "kvr"}
        dist = sb("dist", [P, 384], F32, early)
        bank = [k.ps(f"prep{i}", stack=early) for i in range(5)]
        ev = events(k, "prep", "in tables act turned copied link pe2", early)
        first, others = loads[:len(square)], loads[len(square):]
        first_total, total = k.params_total + 16 * len(first), 16 * len(others)
        turns = [("L1_attn_W_out", wout_t[:, :]), ("L2_attn_Wq", a["q_w"][0][:, :]), ("L2_attn_Wk", a["k_w"][0][:, :]),
                 ("L2_attn_Wv", a["v_w"][0][:, :]), ("L2_attn_Wp", a["wp_t"][:, :]), ("L3_attn_Wo", a["wo_t"][:, :]),
                 ("L3_attn_Wk", None), ("L3_attn_Wv", None), ("L3_attn_Wr", None)]
        scale = (2.0 / 64) ** 0.5 * 2.718281828459045 ** -0.25
        factorial = [1.0, 1.0, 2.0, 6.0, 24.0]
        mags = [(1.0 / f + 1e-10) ** 0.5 * scale for f in factorial]

        with nc.Block() as block:
            def load_some(eng, half):
                with nc.allow_non_contiguous_dma(reason="a few columns of parameters"):
                    for t, src in first[half::2]:
                        eng.dma_start(t[:, :], src).then_inc(k.params_in, 16)
                    for t, src in others[half::2]:
                        eng.dma_start(t[:, :], src).then_inc(ev["in"], 16)

            @block.sync
            def _(sp):
                load_some(sp, 0)

            @block.scalar
            def _(act):
                load_some(act, 1)

            @block.gpsimd
            def _(pool):
                link = Chain(pool, ev["tables"], 0)
                link.then(pool.memset(a["ones"][:, :], 1.0))
                link.then(pool.iota(dist[:, 0:128], pattern=[[-1, 128]], base=0, channel_multiplier=1,
                                    allow_small_or_imprecise_dtypes=True))
                link.then(pool.iota(dist[:, 128:384], pattern=[[-1, 256]], base=128, channel_multiplier=1,
                                    allow_small_or_imprecise_dtypes=True))
                link.then(pool.memset(a["causal"][:, :], 0.0))
                link.then(pool.affine_select(out=a["causal"][:, 0:128], in_=a["causal"][:, 0:128], fill=-1e30,
                                             compare_op=ALU.is_ge, base=0, pattern=[[-1, 128]], channel_multiplier=1))
                link.then(pool.affine_select(out=a["causal"][:, 128:384], in_=a["causal"][:, 128:384], fill=-1e30,
                                             compare_op=ALU.is_ge, base=128, pattern=[[-1, 256]], channel_multiplier=1))
                b = a["blocks"][:, :].rearrange("p (h e) -> p h e", e=8)
                link.then(pool.memset(b, 1.0))
                link.then(pool.affine_select(out=b, in_=b, fill=0.0, compare_op=ALU.is_ge, base=0,
                                             pattern=[[-8, 16], [0, 8]], channel_multiplier=1))
                link.then(pool.affine_select(out=b, in_=b, fill=0.0, compare_op=ALU.is_ge, base=7,
                                             pattern=[[8, 16], [0, 8]], channel_multiplier=-1))

            @block.scalar
            def _(act):
                act.wait_ge(ev["in"], total)
                act.activation(e0[:, :], raw["log_temp"][:, :], ACT.Abs).then_inc(ev["act"], 1)
                act.wait_ge(ev["act"], 1)
                act.activation(e1[:, :], e0[:, :], ACT.Exp, scale=-1.0).then_inc(ev["act"], 1)
                act.wait_ge(ev["act"], 2)
                act.activation(e2[:, :], e1[:, :], ACT.Ln, bias=1.0).then_inc(ev["act"], 1)
                act.wait_ge(ev["tables"], 3)
                act.activation(a["decay"][:, :], dist[:, :], ACT.Exp, scale=-0.3 / 10.0).then_inc(ev["act"], 1)
                act.activation(a["w_log"][:, :], raw["decay"][:, :], ACT.Exp).then_inc(ev["act"], 1)

            @block.tensor
            def _(pe):
                pe.wait_ge(k.params_in, first_total)
                for i, (name, _) in enumerate(turns):
                    pe.transpose(bank[i // 4][:, (i % 4) * P:(i % 4 + 1) * P], raw[name][:, :], k.ident[:, :])\
                      .then_inc(ev["turned"], 1)
                pe.wait_ge(ev["in"], total)
                pe.transpose(bank[2][:, 128:192], raw["shell"][:, :], k.ident[0:64, 0:64])
                pe.transpose(bank[2][0:64, 192:224], raw["omega"][:, :], k.ident[0:32, 0:32])
                for m in range(5):
                    last = pe.transpose(bank[3][0:64, m * 64:(m + 1) * 64], raw["combine"][:, m * 64:(m + 1) * 64],
                                        k.ident[0:64, 0:64])
                last.then_inc(ev["turned"], 1)
                pe.wait_ge(ev["copied"], 9)
                pe.matmul(bank[4][:, 0:128], raw["L1_attn_W_v"][:, :], wout_t[:, :], start=True, stop=True)
                pe.matmul(bank[4][:, 128:129], wout_t[:, :], raw["b_v"][:, :], start=True, stop=True)
                pe.matmul(bank[4][:, 129:130], a["wp_t"][:, :], raw["conv_b"][:, :], start=True, stop=True)\
                  .then_inc(ev["pe2"], 1)

            @block.vector
            def _(dve):
                link = Chain(dve, ev["link"], 0)
                link.then(dve.memset(a["omega_t"][:, :], 0.0))
                src = lambda i: bank[i // 4][:, (i % 4) * P:(i % 4 + 1) * P]
                for i, (name, out) in enumerate(turns):
                    if i % 4 == 0:
                        dve.wait_ge(ev["turned"], min(i + 4, len(turns) + 1))
                    if i == 6:
                        dve.wait_ge(ev["in"], total)
                        for m in "kvr":
                            last = dve.tensor_scalar(rest[m][:, :], raw[f"mix_{m}"][:, :], -1.0, 1.0, ALU.mult, ALU.add)
                        link.then(last)
                    if out is not None:
                        dve.tensor_copy(out, src(i)).then_inc(ev["copied"], 1)
                    else:
                        m = name[-1].lower()
                        dve.tensor_scalar(a[f"now_{m}"][0][:, :], src(i), raw[f"mix_{m}"][:, 0:1], None, ALU.mult)
                        dve.tensor_scalar(a[f"old_{m}"][0][:, :], src(i), rest[m][:, 0:1], None, ALU.mult)\
                           .then_inc(ev["copied"], 1)
                dve.tensor_copy(a["shell_w"][0][:, 0:64], bank[2][:, 128:192])
                dve.tensor_copy(a["shell_w"][0][:, 64:65], raw["charge"][:, :])
                dve.tensor_copy(a["omega_t"][0:64, 0:32], bank[2][0:64, 192:224])
                dve.memset(a["omega_t"][64:65, 32:33], 1.0)
                for m in range(5):
                    dve.tensor_scalar(a["combine_t"][:, m * 64:(m + 1) * 64], bank[3][0:64, m * 64:(m + 1) * 64],
                                      mags[m], None, ALU.mult)
                dve.tensor_scalar(a["rff"][:, 0:32], raw["rff_row"][:, :], 1.5707963267948966, None, ALU.add)
                dve.tensor_copy(a["rff"][:, 32:64], raw["rff_row"][:, :])
                dve.wait_ge(ev["act"], 5)
                link.then(dve.tensor_scalar(e0[:, :], raw["log_temp"][:, :], 0.0, 0.1, ALU.max, ALU.add))
                link.then(dve.tensor_tensor(e0[:, :], e0[:, :], e2[:, :], ALU.add))
                link.then(dve.reciprocal(inv_temp[:, :], e0[:, :]))
                link.then(dve.tensor_scalar(a["decay"][:, :], a["decay"][:, :], inv_temp[:, 0:1], None, ALU.mult))
                link.then(dve.tensor_scalar(a["w_log"][:, :], a["w_log"][:, :], -1.0, None, ALU.mult))
                dve.wait_ge(ev["copied"], 9)
                for j in range(3):
                    last = dve.tensor_scalar(a[f"tap{j}"][0][:, :], a["wp_t"][:, :], raw["conv_w"][:, j:j + 1], None,
                                             ALU.mult)
                link.then(last)
                dve.wait_ge(ev["pe2"], 1)
                dve.tensor_copy(a["vo_w"][0][:, :], bank[4][:, 0:128])
                dve.tensor_tensor(a["vo_bias"][:, :], bank[4][:, 128:129], raw["b_out"][:, :], ALU.add)
                link.then(dve.tensor_tensor(a["wp_bias"][:, :], bank[4][:, 129:130], raw["bp"][:, :], ALU.add))
                pairs = [v for v in a.values() if isinstance(v, tuple)]
                for full, hi, _ in pairs:
                    last = dve.tensor_copy(hi[:, :], full[:, :])
                link.then(last)
                for full, hi, lo in pairs:
                    last = dve.tensor_tensor(lo[:, :], full[:, :], hi[:, :].bitcast(F32), ALU.subtract)
                link.then(last)


class Pipeline:

    def __init__(self, g, first, last):
        self.g, self.first, self.last = g, first, last

    def part(self, lag, f, *args):
        if self.first >= lag and self.last - lag < GROUPS:
            f(self.g - lag, *args)


def pipelined(eng, depth, body):
    for g in range(depth):
        body(Pipeline(g, g, g))
    with eng.Fori(depth, GROUPS) as g:
        body(Pipeline(g, depth, GROUPS - 1))
    for g in range(GROUPS, GROUPS + depth):
        body(Pipeline(g, g, g))


def gpsimd_stage(k, pool, gpsimd):
    base = k.turn0
    with pool.Fori(0, GROUPS) as g:
        if gpsimd is not None:
            gpsimd(pool, g)
        post_gpsimd(k, pool, base + g)


def prefetch(k, block, weights):
    @block.sync
    def _(sp):
        weights.load(sp, k.lo_split)


def finish_stage(k, next_route):
    k.turn0 += GROUPS
    if next_route:
        k.route_base += GROUPS * ROUTE_LINKS[next_route.kind]


def attn1(k, weights):
    a = k.a
    TWO_PI, MAGIC = 6.283185307179586, 12582912.0
    C1 = 6.28125
    C2 = TWO_PI - C1
    with ExitStack() as st:
        sb = lambda name, shape, dt=F32: k.sb(f"at1_{name}", shape, dt, st)
        shell, square = sb("shell", [65, GROUP]), sb("square", [64, GROUP])
        r2, r, q = sb("r2", [P, GT]), sb("r", [P, GT]), sb("q", [P, GT])
        ang, turns = sb("ang", [P, GT, 64]), sb("turns", [P, GT, 64])
        phis, phi = sb("phis", [P, GT, P]), sb("phi", [P, GT, P])
        phisT, phiT = sb("phisT", [64, GROUP]), sb("phiT", [64, GROUP])
        Z = sb("Z", [P, GT, 320])
        VT, V = sb("VT", [P, GROUP]), sb("V", [P, GT, D])
        L = sb("L", [P, GB, 384])
        PT = sb("PT", [P, GB, 384])
        top, total, inv = sb("top", [P, GB, 2]), sb("total", [P, GB, 2]), sb("inv", [P, GB, 2])
        A = [k.ps(f"at1_bank{i}", stack=st) for i in range(5)]
        route_scratch(k, "at1", st)
        ev = events(k, "at1", "shell_psum shell_done proj_done r2_done r_done q_done ang_done phis_done phis_turned "
                    "phisT_done z_psum z_copied phi_done phi_turned phiT_done v_psum vT_done v_turned v_done "
                    "logits_psum top_done exp_done p_done p_turned pT_done link link_b", st)
        FEATURE_LINKS, ATTEND_LINKS = 9, 6
        base = k.turn0

        with k.nc.Block() as block:
            @block.vector
            def _(dve):
                dve.memset(phis[:, :, :], 0.0)
                dve.memset(phi[:, :, :], 0.0)

        with k.nc.Block() as block:
            prefetch(k, block, weights)

            @block.tensor
            def _(pe):
                def project(g):
                    view = lo_hi(k, g)
                    xh, xl = view(k.xh), view(k.xl)
                    if not isinstance(g, int) or g:
                        pe.wait_ge(ev["z_copied"], g * GT)
                        pe.wait_ge(ev["v_done"], g)
                    mm3(pe, A[0][0:65, :], a["shell_w"][1][:, :], a["shell_w"][2][:, :], xh, xl)\
                        .then_inc(ev["shell_psum"], 1)
                    mm3(pe, A[2][:, :], a["vo_w"][1][:, :], a["vo_w"][2][:, :], xh, xl).then_inc(ev["v_psum"], 1)

                def angles(g):
                    pe.wait_ge(ev["shell_done"], g + 1)
                    if not isinstance(g, int) or g:
                        pe.wait_ge(ev["phiT_done"], g)
                    for j in range(GT):
                        tile = slice(j * P, (j + 1) * P)
                        pe.matmul(A[1][:, j * 33:(j + 1) * 33], shell[:, tile], a["omega_t"][:, :],
                                  start=True, stop=True)
                    for j in range(GT):
                        tile = slice(j * P, (j + 1) * P)
                        last = pe.matmul(A[1][:, 132 + j:133 + j], square[:, tile], a["ones"][0:64, :],
                                         start=True, stop=True)
                    last.then_inc(ev["proj_done"], 1)

                def values(g):
                    pe.wait_ge(ev["vT_done"], g + 1)
                    for j in range(GT):
                        last = pe.transpose(A[2][:, j * P:(j + 1) * P], VT[:, j * P:(j + 1) * P], k.ident[:, :])
                    last.then_inc(ev["v_turned"], 1)

                def fourier(g):
                    pe.wait_ge(ev["phis_done"], g + 1)
                    for j in range(GT):
                        last = pe.transpose(A[0][:, j * P:(j + 1) * P], phis[:, j, :], k.ident[:, :])
                    last.then_inc(ev["phis_turned"], 1)

                def combine(g):
                    pe.wait_ge(ev["phisT_done"], g + 1)
                    for j in range(GT):
                        if j >= 2:
                            pe.wait_ge(ev["z_copied"], g * GT + j - 1)
                        pe.matmul(A[1 - j % 2][:, 0:320], phisT[:, j * P:(j + 1) * P], a["combine_t"][:, :],
                                  start=True, stop=True).then_inc(ev["z_psum"], 1)

                def features(g):
                    pe.wait_ge(ev["phi_done"], g + 1)
                    for j in range(GT):
                        last = pe.transpose(A[1][:, j * P:(j + 1) * P], phi[:, j, :], k.ident[:, :])
                    last.then_inc(ev["phi_turned"], 1)

                def logits(g):
                    pe.wait_ge(ev["phiT_done"], g + 1)
                    for b in range(GB):
                        q0 = phiT[:, b * SEQ:b * SEQ + P]
                        q1 = phiT[:, b * SEQ + P:(b + 1) * SEQ]
                        pe.matmul(A[3 + b][:, 0:128], q0, q0, start=True, stop=True)
                        pe.matmul(A[3 + b][:, 128:384], q1, phiT[:, b * SEQ:(b + 1) * SEQ], start=True, stop=True)\
                          .then_inc(ev["logits_psum"], 1)

                def turn(g):
                    for b in range(GB):
                        pe.wait_ge(ev["p_done"], g * GB + b + 1)
                        pe.transpose(A[3 + b][:, 0:128], L[:, b, 0:128], k.ident[:, :])
                        pe.transpose(A[3 + b][:, 128:256], L[:, b, 128:256], k.ident[:, :])
                        pe.transpose(A[3 + b][:, 256:384], L[:, b, 256:384], k.ident[:, :])\
                          .then_inc(ev["p_turned"], 1)

                def attend(g):
                    pe.wait_ge(ev["v_done"], g + 1)
                    pe.wait_ge(k.y_copied, base + g)
                    for b in range(GB):
                        pe.wait_ge(ev["pT_done"], g * GB + b + 1)
                        pe.matmul(k.ypsum[:, b * SEQ:(b + 1) * SEQ], V[:, 2 * b, :], PT[:, b, 0:256],
                                  start=True, stop=False)
                        last = pe.matmul(k.ypsum[:, b * SEQ + P:(b + 1) * SEQ], V[:, 2 * b + 1, :],
                                         PT[:, b, 256:384], start=False, stop=True)
                    last.then_inc(k.y_done, 1)

                def post(g, *steps):
                    for step in steps:
                        post_tensor(k, pe, step, base + g, g, weights.route)

                def body(p):
                    p.part(2, logits)
                    p.part(5, post, 9)
                    p.part(1, angles)
                    p.part(4, post, 4)
                    p.part(1, values)
                    p.part(1, fourier)
                    p.part(2, turn)
                    p.part(3, post, 1)
                    p.part(1, combine)
                    p.part(5, post, 14)
                    p.part(2, attend)
                    p.part(0, project)
                    p.part(1, features)
                    p.part(4, post, 7)

                pipelined(pe, 5, body)

            @block.scalar
            def _(act):
                def shells(g):
                    act.wait_ge(ev["shell_psum"], g + 1)
                    act.activation(shell[:, :], A[0][0:65, :], ACT.Identity, bias=a["b_shell"][:, 0:1])
                    act.activation(square[:, :], A[0][0:64, :], ACT.Square, bias=a["b_shell"][0:64, 0:1])\
                       .then_inc(ev["shell_done"], 1)
                    act.wait_ge(ev["v_psum"], g + 1)
                    act.activation(VT[:, :], A[2][:, :], ACT.Identity, bias=a["vo_bias"][:, 0:1])\
                       .then_inc(ev["vT_done"], 1)

                def charges(g):
                    act.wait_ge(ev["r2_done"], g + 1)
                    act.activation(q[:, :], A[1][:, 0:132].rearrange("p (j e) -> p j e", j=GT)[:, :, 32], ACT.Tanh)\
                       .then_inc(ev["q_done"], 1)

                def fourier(g):
                    act.wait_ge(ev["ang_done"], g + 1)
                    act.activation(phis[:, :, 0:64], ang[:, :, :], ACT.Sin).then_inc(ev["phis_done"], 1)
                    act.wait_ge(ev["phis_turned"], g + 1)
                    act.activation(phisT[:, :], A[0][0:64, :], ACT.Copy).then_inc(ev["phisT_done"], 1)

                def combine(g):
                    for j in range(GT):
                        act.wait_ge(ev["z_psum"], g * GT + j + 1)
                        act.activation(Z[:, j, :], A[1 - j % 2][:, 0:320], ACT.Copy).then_inc(ev["z_copied"], 1)

                def values(g):
                    act.wait_ge(ev["v_turned"], g + 1)
                    act.activation(V[:, :, :], A[2][:, :].rearrange("p (j d) -> p j d", j=GT), ACT.Copy)\
                       .then_inc(ev["v_done"], 1)

                def features(g):
                    act.wait_ge(ev["phi_turned"], g + 1)
                    act.activation(phiT[:, :], A[1][0:64, :], ACT.Copy).then_inc(ev["phiT_done"], 1)

                def exponentials(g):
                    for b in range(GB):
                        act.wait_ge(ev["top_done"], g * GB + b + 1)
                        act.activation(L[:, b, 0:128], L[:, b, 0:128], ACT.Exp, bias=top[:, b, 0:1],
                                       accum_out=total[:, b, 0:1])
                        act.activation(L[:, b, 128:384], L[:, b, 128:384], ACT.Exp, bias=top[:, b, 1:2],
                                       accum_out=total[:, b, 1:2]).then_inc(ev["exp_done"], 1)

                def turned(g):
                    for b in range(GB):
                        act.wait_ge(ev["p_turned"], g * GB + b + 1)
                        act.activation(PT[:, b, :], A[3 + b][:, 0:384], ACT.Copy).then_inc(ev["pT_done"], 1)

                def attended(g):
                    act.wait_ge(k.y_done, base + g + 1 - k.moe_groups)

                def post(g, *steps):
                    for step in steps:
                        post_scalar(k, act, step, base + g, g, weights.route)

                def body(p):
                    p.part(5, post, 10)
                    p.part(3, post, 0)
                    p.part(1, charges)
                    p.part(2, exponentials)
                    p.part(4, post, 5)
                    p.part(1, fourier)
                    p.part(2, turned)
                    p.part(1, combine)
                    p.part(5, post, 15)
                    p.part(2, attended)
                    p.part(1, values)
                    p.part(0, shells)
                    p.part(1, features)
                    p.part(4, post, 8)

                pipelined(act, 5, body)

            @block.vector
            def _(dve):
                def lengths(g):
                    dve.wait_ge(ev["proj_done"], g + 1)
                    dve.tensor_scalar(r2[:, :], A[1][:, 132:136], 1e-24, None, ALU.max).then_inc(ev["r2_done"], 1)

                def angles(g):
                    link = Chain(dve, ev["link"], g * FEATURE_LINKS)
                    dve.wait_ge(ev["q_done"], g + 1)
                    dve.wait_ge(ev["r_done"], g + 1)
                    proj = A[1][:, 0:132].rearrange("p (j e) -> p j e", j=GT)[:, :, 0:32]
                    rr = r[:, :].unsqueeze(2).to_broadcast([P, GT, 32])
                    dve.tensor_tensor(ang[:, :, 0:32], proj, rr, ALU.mult)
                    link.then(dve.tensor_tensor(ang[:, :, 32:64], proj, rr, ALU.mult))
                    link.then(dve.tensor_tensor(ang[:, :, :], ang[:, :, :], a["rff"][:, :].unsqueeze(1)
                                                .to_broadcast([P, GT, 64]), ALU.add))
                    link.then(dve.tensor_scalar(turns[:, :, :], ang[:, :, :], 1.0 / TWO_PI, MAGIC,
                                                ALU.mult, ALU.add))
                    link.then(dve.tensor_scalar(turns[:, :, :], turns[:, :, :], MAGIC, None, ALU.subtract))
                    link.then(dve.scalar_tensor_tensor(out=ang[:, :, :], in0=turns[:, :, :], scalar=-C1,
                                                       in1=ang[:, :, :], op0=ALU.mult, op1=ALU.add))
                    link.then(dve.scalar_tensor_tensor(out=ang[:, :, :], in0=turns[:, :, :], scalar=-C2,
                                                       in1=ang[:, :, :], op0=ALU.mult, op1=ALU.add))
                    dve.tensor_scalar(ang[:, :, :], ang[:, :, :], 3.1415925, -3.1415925, ALU.min, ALU.max)\
                       .then_inc(ev["ang_done"], 1)

                def features(g):
                    link = Chain(dve, ev["link"], g * FEATURE_LINKS + 6)
                    dve.wait_ge(ev["z_copied"], g * GT + GT)
                    for m in (3, 2, 1, 0):
                        for j in range(GT):
                            prev = Z[:, j, 256:320] if m == 3 else phi[:, j, 0:64]
                            last = dve.scalar_tensor_tensor(out=phi[:, j, 0:64], in0=prev, scalar=q[:, j:j + 1],
                                                            in1=Z[:, j, m * 64:(m + 1) * 64], op0=ALU.mult,
                                                            op1=ALU.add)
                        if m:
                            link.then(last)
                    last.then_inc(ev["phi_done"], 1)
                    assert link.n + 6 == FEATURE_LINKS

                def peaks(g):
                    link = Chain(dve, ev["link_b"], g * ATTEND_LINKS)
                    for b in range(GB):
                        dve.wait_ge(ev["logits_psum"], g * GB + b + 1)
                        link.then(dve.tensor_tensor(L[:, b, :], A[3 + b][:, 0:384], a["decay"][:, :], ALU.mult))
                        link.then(dve.tensor_tensor(L[:, b, :], L[:, b, :], a["causal"][:, :], ALU.add))
                        dve.tensor_reduce(top[:, b, 0:1], L[:, b, 0:128], AX_X, ALU.max, negate=True)
                        dve.tensor_reduce(top[:, b, 1:2], L[:, b, 128:384], AX_X, ALU.max, negate=True)\
                           .then_inc(ev["top_done"], 1)

                def divide(g):
                    link = Chain(dve, ev["link_b"], g * ATTEND_LINKS + 4)
                    for b in range(GB):
                        dve.wait_ge(ev["exp_done"], g * GB + b + 1)
                        link.then(dve.reciprocal(inv[:, b, :], total[:, b, :]))
                        dve.tensor_scalar(L[:, b, 0:128], L[:, b, 0:128], inv[:, b, 0:1], None, ALU.mult)
                        dve.tensor_scalar(L[:, b, 128:384], L[:, b, 128:384], inv[:, b, 1:2], None, ALU.mult)\
                           .then_inc(ev["p_done"], 1)
                    assert link.n + 4 == ATTEND_LINKS

                def post(g, *steps):
                    for step in steps:
                        post_vector(k, dve, step, base + g, g, weights.route)

                def body(p):
                    p.part(1, peaks)
                    p.part(0, lengths)
                    p.part(0, angles)
                    p.part(1, divide)
                    p.part(3, post, 6)
                    p.part(4, post, 13)
                    p.part(2, post, 2)
                    p.part(0, features)

                pipelined(dve, 4, body)

            @block.gpsimd
            def _(pool):
                def lengths(g):
                    pool.wait_ge(ev["r2_done"], g + 1)
                    pool.tensor_tensor(r[:, :], r2[:, :], k.half_neg[:, 0:1].to_broadcast([P, GT]), ALU.pow)\
                        .then_inc(ev["r_done"], 1)

                def post(g):
                    post_gpsimd(k, pool, base + g)

                def body(p):
                    p.part(0, lengths)
                    p.part(2, post)

                pipelined(pool, 2, body)
    finish_stage(k, weights.route)


def attn2(k, weights):
    a = k.a
    with ExitStack() as st:
        sb = lambda name, shape, dt=F32: k.sb(f"at2_{name}", shape, dt, st)
        low = [sb(f"low_{x}", [P, GROUP]) for x in "qk"]
        ex = [sb(f"exp_{x}", [P, GROUP]) for x in "qk"]
        pos = [sb(f"pos_{x}", [P, GROUP]) for x in "qk"]
        vT = sb("vT", [P, GROUP])
        kt, vt = sb("k_tokens", [P, GT, D]), sb("v_tokens", [P, GT, D])
        ks = sb("k_sum", [P, GB])
        kv, ksm = sb("kv", [P, GB, D]), sb("k_sum_heads", [P, GB, D])
        den, rec, att = sb("den", [P, GROUP]), sb("rec", [P, GROUP]), sb("att", [P, GROUP])
        A = [k.ps(f"at2_bank{i}", stack=st) for i in range(5)]
        route_scratch(k, "at2", st)
        ev = events(k, "at2", "q_psum k_psum v_psum q_low k_low q_exp k_exp q_done k_done vT_done k_turned v_turned "
                    "k_copied v_copied kv_psum kv_done num_psum att_done link", st)
        LINKS = 3

        base = k.turn0

        with k.nc.Block() as block:
            prefetch(k, block, weights)

            @block.tensor
            def _(pe):
                def project(g):
                    view = lo_hi(k, g)
                    for i, x in enumerate("qkv"):
                        if x == "q" and (not isinstance(g, int) or g):
                            pe.wait_ge(ev["q_done"], g)
                        mm3(pe, A[i][:, :], a[f"{x}_w"][1][:, :], a[f"{x}_w"][2][:, :], view(k.xh), view(k.xl))\
                            .then_inc(ev[f"{x}_psum"], 1)

                def convolve(g):
                    view = lo_hi(k, g)
                    pe.wait_ge(k.y_copied, base + g)
                    for j in range(3):
                        mm3(pe, k.ypsum[:, :], a[f"tap{j}"][1][:, :], a[f"tap{j}"][2][:, :], view(k.xh, j - 1),
                            view(k.xl, j - 1), start=(j == 0), stop=False)

                def turn(g):
                    for i, (name, src, done) in enumerate((("k", pos[1], "k_done"), ("v", vT, "vT_done"))):
                        pe.wait_ge(ev[done], g + 1)
                        for j in range(GT):
                            last = pe.transpose(A[1 + i][:, j * P:(j + 1) * P], src[:, j * P:(j + 1) * P],
                                                k.ident[:, :])
                        last.then_inc(ev[f"{name}_turned"], 1)

                def state(g):
                    pe.wait_ge(ev["k_copied"], g + 1)
                    pe.wait_ge(ev["v_copied"], g + 1)
                    if not isinstance(g, int) or g:
                        pe.wait_ge(ev["att_done"], g)
                    for b in range(GB):
                        for j in range(2):
                            last = pe.matmul(A[3][:, b * D:(b + 1) * D], kt[:, 2 * b + j, :], vt[:, 2 * b + j, :],
                                             start=(j == 0), stop=(j == 1))
                    last.then_inc(ev["kv_psum"], 1)

                def attend(g):
                    pe.wait_ge(ev["q_done"], g + 1)
                    pe.wait_ge(ev["kv_done"], g + 1)
                    for b in range(GB):
                        cols = slice(b * SEQ, (b + 1) * SEQ)
                        pe.matmul(A[4][:, cols], kv[:, b, :], pos[0][:, cols], start=True, stop=True)
                        last = pe.matmul(A[3][:, cols], ksm[:, b, :], pos[0][:, cols], start=True, stop=True)
                    last.then_inc(ev["num_psum"], 1)

                def output(g):
                    pe.wait_ge(ev["att_done"], g + 1)
                    pe.matmul(k.ypsum[:, :], a["wp_t"][:, :], att[:, :], start=False, stop=True).then_inc(k.y_done, 1)

                def post(g, *steps):
                    for step in steps:
                        post_tensor(k, pe, step, base + g, g, weights.route)

                def body(p):
                    p.part(0, project)
                    p.part(3, post, 7)
                    p.part(2, post, 1)
                    p.part(1, attend)
                    p.part(1, convolve)
                    p.part(3, post, 9)
                    p.part(1, output)
                    p.part(0, turn)
                    p.part(0, state)
                    p.part(2, post, 4)
                    p.part(3, post, 14)

                pipelined(pe, 3, body)

            @block.scalar
            def _(act):
                def exponentials(g):
                    for i, x in enumerate("qk"):
                        act.wait_ge(ev[f"{x}_low"], g + 1)
                        act.activation(ex[i][:, :], low[i][:, :], ACT.Exp).then_inc(ev[f"{x}_exp"], 1)
                    act.wait_ge(ev["v_psum"], g + 1)
                    act.activation(vT[:, :], A[2][:, :], ACT.Copy).then_inc(ev["vT_done"], 1)

                def copies(g):
                    for i, (name, out) in enumerate((("k", kt), ("v", vt))):
                        act.wait_ge(ev[f"{name}_turned"], g + 1)
                        act.activation(out[:, :, :], A[1 + i][:, :].rearrange("p (j d) -> p j d", j=GT), ACT.Copy)\
                           .then_inc(ev[f"{name}_copied"], 1)

                def post(g, *steps):
                    for step in steps:
                        post_scalar(k, act, step, base + g, g, weights.route, a["wp_bias"][:, 0:1])

                def body(p):
                    p.part(2, post, 0)
                    p.part(0, exponentials)
                    p.part(3, post, 8, 10)
                    p.part(0, copies)
                    p.part(2, post, 5)
                    p.part(3, post, 15)

                pipelined(act, 3, body)

            @block.vector
            def _(dve):
                def below(g):
                    for i, x in enumerate("qk"):
                        dve.wait_ge(ev[f"{x}_psum"], g + 1)
                        dve.tensor_scalar(low[i][:, :], A[i][:, :], 0.0, None, ALU.min).then_inc(ev[f"{x}_low"], 1)

                def features(g):
                    for i, x in reversed(list(enumerate("qk"))):
                        dve.wait_ge(ev[f"{x}_exp"], g + 1)
                        dve.scalar_tensor_tensor(out=pos[i][:, :], in0=A[i][:, :], scalar=0.0, in1=ex[i][:, :],
                                                 op0=ALU.max, op1=ALU.add).then_inc(ev[f"{x}_done"], 1)

                def state(g):
                    link = Chain(dve, ev["link"], g * LINKS)
                    dve.wait_ge(ev["k_done"], g + 1)
                    link.then(dve.tensor_reduce(ks[:, :], pos[1][:, :].rearrange("p (b s) -> p b s", b=GB), AX_X,
                                                ALU.add))
                    for b in range(GB):
                        dve.tensor_scalar(ksm[:, b, :], a["blocks"][:, :], ks[:, b:b + 1], None, ALU.mult)
                    dve.wait_ge(ev["kv_psum"], g + 1)
                    dve.tensor_tensor(kv[:, :, :], A[3][:, 0:GB * D].rearrange("p (b d) -> p b d", b=GB),
                                      a["blocks"][:, :].unsqueeze(1).to_broadcast([P, GB, D]), ALU.mult)\
                       .then_inc(ev["kv_done"], 1)

                def divide(g):
                    link = Chain(dve, ev["link"], g * LINKS + 1)
                    dve.wait_ge(ev["num_psum"], g + 1)
                    link.then(dve.tensor_scalar(den[:, :], A[3][:, :], 1e-6, None, ALU.max))
                    link.then(dve.reciprocal(rec[:, :], den[:, :]))
                    dve.tensor_tensor(att[:, :], A[4][:, :], rec[:, :], ALU.mult).then_inc(ev["att_done"], 1)

                def post(g, *steps):
                    for step in steps:
                        post_vector(k, dve, step, base + g, g, weights.route)

                def body(p):
                    p.part(0, below)
                    p.part(2, post, 20, 21, 22, 23)
                    p.part(1, divide)
                    p.part(0, features)
                    p.part(2, post, 24, 25)
                    p.part(0, state)
                    p.part(3, post, 13)
                    p.part(2, post, 6)

                pipelined(dve, 3, body)

            @block.gpsimd
            def _(pool):
                gpsimd_stage(k, pool, None)
    finish_stage(k, weights.route)


def attn3(k, weights):
    a = k.a
    NONE = -1e38
    with ExitStack() as st:
        sb = lambda name, shape, dt=F32: k.sb(f"at3_{name}", shape, dt, st)
        peak, num, den = (sb(n, [P, GB, SEQ + 1]) for n in ("peak", "num", "den"))
        most = sb("most", [P, GB, SEQ])
        args, exps = sb("args", [P, 4, GROUP]), sb("exps", [P, 4, GROUP])
        rneg, rexp = sb("rneg", [P, GROUP]), sb("rexp", [P, GROUP])
        sv, ov, o1, o2, inv = (sb(n, [P, GB, SEQ]) for n in ("sv", "ov", "o1", "o2", "inv"))
        out, vs = sb("out", [P, GROUP]), sb("values", [P, GROUP])
        before, after = peak[:, :, 0:SEQ], peak[:, :, 1:SEQ + 1]
        A = [k.ps(f"at3_bank{i}", stack=st) for i in range(3)]
        route_scratch(k, "at3", st)
        ev = events(k, "at3", "k_psum v_psum r_psum args_done exps_done out_done link rneg_done v_copied "
                    "most_done e1_done sv_done num_done o1_done rexp_done pool_link", st)
        LINKS = 5

        def split(t):
            return t.rearrange("p (b s) -> p b s", b=GB)

        base = k.turn0

        with k.nc.Block() as block:
            @block.vector
            def _(dve):
                dve.memset(peak[:, :, 0:1], NONE)
                dve.memset(num[:, :, 0:1], 0.0)
                dve.memset(den[:, :, 0:1], 0.0)

        with k.nc.Block() as block:
            prefetch(k, block, weights)

            @block.tensor
            def _(pe):
                def project(g):
                    view = lo_hi(k, g)
                    if not isinstance(g, int) or g:
                        pe.wait_ge(ev["rneg_done"], g)
                        pe.wait_ge(ev["v_copied"], g)
                    for i, x in enumerate("kvr"):
                        mm3(pe, A[i][:, :], a[f"now_{x}"][1][:, :], a[f"now_{x}"][2][:, :], view(k.xh), view(k.xl),
                            stop=False)
                        mm3(pe, A[i][:, :], a[f"old_{x}"][1][:, :], a[f"old_{x}"][2][:, :], view(k.xh, -1),
                            view(k.xl, -1), start=False).then_inc(ev[f"{x}_psum"], 1)

                def output(g):
                    pe.wait_ge(ev["out_done"], g + 1)
                    pe.wait_ge(k.y_copied, base + g)
                    pe.matmul(k.ypsum[:, :], a["wo_t"][:, :], out[:, :], start=True, stop=True).then_inc(k.y_done, 1)

                def post(g, *steps):
                    for step in steps:
                        post_tensor(k, pe, step, base + g, g, weights.route)

                def body(p):
                    p.part(2, post, 1)
                    p.part(3, post, 7)
                    p.part(3, post, 9)
                    p.part(2, post, 4)
                    p.part(0, project)
                    p.part(3, post, 14)
                    p.part(1, output)

                pipelined(pe, 3, body)

            @block.scalar
            def _(act):
                def values(g):
                    act.wait_ge(ev["v_psum"], g + 1)
                    if not isinstance(g, int) or g:
                        act.wait_ge(ev["out_done"], g)
                    act.activation(vs[:, :], A[1][:, :], ACT.Copy).then_inc(ev["v_copied"], 1)

                def exponentials(g):
                    act.wait_ge(ev["e1_done"], g + 1)
                    act.wait_ge(ev["args_done"], g + 1)
                    act.activation(exps[:, :, :], args[:, :, :], ACT.Exp).then_inc(ev["exps_done"], 1)
                    act.wait_ge(ev["rneg_done"], g + 1)
                    act.activation(rexp[:, :], rneg[:, :], ACT.Exp).then_inc(ev["rexp_done"], 1)

                def post(g, *steps):
                    for step in steps:
                        post_scalar(k, act, step, base + g, g, weights.route)

                def body(p):
                    p.part(0, values)
                    p.part(1, post, 0)
                    p.part(2, post, 8)
                    p.part(0, exponentials)
                    p.part(2, post, 10)
                    p.part(1, post, 5)
                    p.part(2, post, 12, 15)

                pipelined(act, 2, body)

            @block.vector
            def _(dve):
                K, V = split(A[0][:, :]), split(vs[:, :])
                _, e2a, s1a, s2a = (split(args[:, i, :]) for i in range(4))
                e1, e2, _, s2 = (split(exps[:, i, :]) for i in range(4))
                u, w = a["u"][:, 0:1], a["w_log"][:, 0:1]

                def peaks(g):
                    link = Chain(dve, ev["link"], g * LINKS)
                    dve.wait_ge(ev["k_psum"], g + 1)
                    for b in range(GB):
                        last = dve.tensor_tensor_scan(peak[:, b, 1:SEQ + 1], w.to_broadcast([P, SEQ]),
                                                      A[0][:, b * SEQ:(b + 1) * SEQ], NONE, ALU.add, ALU.max)
                    link.then(last)
                    dve.scalar_tensor_tensor(out=most[:, :, :], in0=K, scalar=u, in1=before,
                                             op0=ALU.add, op1=ALU.max).then_inc(ev["most_done"], 1)
                    dve.wait_ge(ev["most_done"], g + 1)
                    dve.scalar_tensor_tensor(out=e2a, in0=K, scalar=u, in1=most[:, :, :], op0=ALU.add,
                                             op1=ALU.subtract)
                    dve.scalar_tensor_tensor(out=s1a, in0=before, scalar=w, in1=after, op0=ALU.add, op1=ALU.subtract)
                    dve.tensor_tensor(s2a, K, after, ALU.subtract).then_inc(ev["args_done"], 1)
                    dve.wait_ge(ev["r_psum"], g + 1)
                    dve.tensor_scalar(rneg[:, :], A[2][:, :], -1.0, 80.0, ALU.mult, ALU.min)\
                       .then_inc(ev["rneg_done"], 1)

                def sums(g):
                    dve.wait_ge(ev["exps_done"], g + 1)
                    for b in range(GB):
                        cols = slice(b * SEQ, (b + 1) * SEQ)
                        dve.tensor_tensor_scan(den[:, b, 1:SEQ + 1], exps[:, 2, cols], exps[:, 3, cols], 0.0,
                                               ALU.mult, ALU.add)
                    dve.wait_ge(ev["sv_done"], g + 1)
                    for b in range(GB):
                        cols = slice(b * SEQ, (b + 1) * SEQ)
                        last = dve.tensor_tensor_scan(num[:, b, 1:SEQ + 1], exps[:, 2, cols], sv[:, b, :], 0.0,
                                                      ALU.mult, ALU.add)
                    last.then_inc(ev["num_done"], 1)
                    dve.wait_ge(ev["num_done"], g + 1)

                def quotient(g):
                    link = Chain(dve, ev["link"], g * LINKS + 1)
                    link.then(dve.tensor_tensor(o2[:, :, :], e1, den[:, :, 0:SEQ], ALU.mult))
                    link.then(dve.tensor_tensor(o2[:, :, :], o2[:, :, :], e2, ALU.add))
                    dve.wait_ge(ev["rexp_done"], g + 1)
                    link.then(dve.scalar_tensor_tensor(out=o2[:, :, :], in0=split(rexp[:, :]), scalar=1.0,
                                                       in1=o2[:, :, :], op0=ALU.add, op1=ALU.mult))
                    link.then(dve.reciprocal(inv[:, :, :], o2[:, :, :]))
                    dve.wait_ge(ev["o1_done"], g + 1)
                    dve.tensor_tensor(split(out[:, :]), o1[:, :, :], inv[:, :, :], ALU.mult)\
                       .then_inc(ev["out_done"], 1)
                    assert link.n == LINKS - 1

                def post(g, *steps):
                    for step in steps:
                        post_vector(k, dve, step, base + g, g, weights.route)

                def body(p):
                    p.part(0, peaks)
                    p.part(1, post, 2)
                    p.part(0, sums)
                    p.part(1, post, 6)
                    p.part(2, post, 11)
                    p.part(0, quotient)
                    p.part(2, post, 13)

                pipelined(dve, 2, body)

            @block.gpsimd
            def _(pool):
                e1, e2, _, s2 = (split(exps[:, i, :]) for i in range(4))

                def exponent(g):
                    pool.wait_ge(ev["most_done"], g + 1)
                    pool.tensor_tensor(split(args[:, 0, :]), before, most[:, :, :], ALU.subtract)\
                        .then_inc(ev["e1_done"], 1)

                def products(g):
                    pool.wait_ge(ev["v_copied"], g + 1)
                    pool.wait_ge(ev["exps_done"], g + 1)
                    pool.tensor_tensor(sv[:, :, :], s2, split(vs[:, :]), ALU.mult).then_inc(ev["sv_done"], 1)
                    link = Chain(pool, ev["pool_link"], g * 2)
                    pool.wait_ge(ev["sv_done"], g + 1)
                    link.then(pool.tensor_tensor(ov[:, :, :], e2, split(vs[:, :]), ALU.mult))

                def numerator(g):
                    link = Chain(pool, ev["pool_link"], g * 2 + 1)
                    pool.wait_ge(ev["num_done"], g + 1)
                    link.then(pool.tensor_tensor(o1[:, :, :], e1, num[:, :, 0:SEQ], ALU.mult))
                    pool.tensor_tensor(o1[:, :, :], o1[:, :, :], ov[:, :, :], ALU.add).then_inc(ev["o1_done"], 1)

                def post(g):
                    post_gpsimd(k, pool, base + g)

                def body(p):
                    p.part(0, exponent)
                    p.part(1, post)
                    p.part(0, products)
                    p.part(0, numerator)

                pipelined(pool, 1, body)
    finish_stage(k, weights.route)



CH, ST, TAPS = 256, 16, 4
CT = CH // P
PAD = SEQ + P
PACK = P // ST
PACKS = CH // PACK
TCH = 8
LOADS = CH // TCH
RING = 2


def ssm(k, next_route):
    io, nc = k.io, k.nc
    with ExitStack() as st:
        sb = lambda name, shape, dt=F32, stack=st: k.sb(f"ssm_{name}", shape, dt, stack)
        scratch_a = nc.dram_tensor("scratch_a16", (CH, ST * ST), F32, kind="Internal").ap()
        scratch_k = nc.dram_tensor("scratch_kernels", (CH, PAD * 3), BF16, kind="Internal").ap()
        wout = sb("wout", [P, CT, D])
        win_hi, win_lo = sb("win_hi", [P, CH], F32R), sb("win_lo", [P, CH], F32R)
        bias_t = sb("bias_t", [P, SEQ])
        Y = sb("Y", [P, CH, 2, BATCH])
        load_x(k, st)
        kernels(k, scratch_a, scratch_k, wout, win_hi, win_lo, bias_t)
        recurrence(k, scratch_k, win_hi, win_lo, Y)
        project(k, wout, bias_t, Y, next_route)
    finish_stage(k, next_route)


def load_x(k, st):
    nc = k.nc
    with ExitStack() as early:
        sb = lambda name, shape: k.sb(f"ln0_{name}", shape, F32, early)
        eps_rms, t1, rstd, t3, t4 = sb("eps", [P, 1]), *(sb(f"t{i}", [P, TILES]) for i in range(4))
        scale, h = sb("scale", [P, TILES]), [sb(f"h{i}", [P, GT, D]) for i in range(2)]
        xn = [sb(f"xn{i}", [P, GT, D]) for i in range(2)]
        flip = sb("flip", [P, P])
        stats, moments = sb("stats", [P, TILES, 6]), sb("moments", [P, TILES, 2])
        turn = [k.turn, k.ypsum]
        ev = events(k, "ln0", "stats aggr pool scale_done h_done turned hi lo eps flip", early)
        for g in range(GROUPS):
            k.load_count[g] += 16
        with nc.Block() as block:
            @block.sync
            def _(sp):
                src = k.io["L0_attn_x"].rearrange("b (h p) d -> p (b h) d", p=P)
                for g in range(GROUPS):
                    sp.dma_start(k.x[:, g * GT:(g + 1) * GT, :], src[:, g * GT:(g + 1) * GT, :])\
                      .then_inc(k.loads[g], 16)

            @block.vector
            def _(dve):
                dve.memset(eps_rms[:, :], 1e-6).then_inc(ev["eps"], 1)
                for g in range(GROUPS):
                    dve.wait_ge(k.loads[g], 16)
                    for j in range(GT):
                        last = dve.bn_stats(stats[:, g * GT + j, :], k.x[:, g * GT + j, :])
                last.then_inc(ev["stats"], 1)
                dve.wait_ge(ev["stats"], 1)
                for j in range(TILES):
                    last = dve.bn_aggr(moments[:, j, :], stats[:, j, :])
                last.then_inc(ev["aggr"], 1)
                dve.wait_ge(ev["aggr"], 1)
                dve.wait_ge(ev["scale_done"], 1)

                def rest(g):
                    dve.wait_ge(ev["hi"], g + 1)
                    view = lo_hi(k, g)
                    dve.tensor_tensor(view(k.xl), turn[g % 2][:, :].rearrange("p (b s) -> p b s", b=GB),
                                      view(k.xh).bitcast(F32), ALU.subtract).then_inc(ev["lo"], 1)

                for g in range(GROUPS):
                    if g >= 2:
                        dve.wait_ge(ev["turned"], g - 1)
                    for j in range(GT):
                        at = g * GT + j
                        mean = moments[:, at, 0:1]
                        dve.tensor_scalar(h[g % 2][:, j, :], k.x[:, at, :], mean, scale[:, at:at + 1],
                                          ALU.subtract, ALU.mult)
                        last = dve.tensor_scalar(xn[g % 2][:, j, :], k.x[:, at, :], mean, rstd[:, at:at + 1],
                                                 ALU.subtract, ALU.mult)
                    last.then_inc(ev["h_done"], 1)
                    if g:
                        rest(g - 1)
                    dve.wait_ge(ev["h_done"], g + 1)
                    xs = k.x[:, g * GT:(g + 1) * GT, :]
                    dve.tensor_tensor(xs, xs, xn[g % 2][:, :, :], ALU.add)
                rest(GROUPS - 1)

            @block.gpsimd
            def _(pool):
                pool.memset(flip[:, :], 0.0).then_inc(ev["flip"], 1)
                pool.wait_ge(ev["flip"], 1)
                pool.affine_select(out=flip[:, :], in_=flip[:, :], compare_op=ALU.not_equal, fill=1.0,
                                   base=1 - P, pattern=[[1, P]], channel_multiplier=1).then_inc(ev["flip"], 1)
                pool.wait_ge(ev["flip"], 2)
                pool.wait_ge(ev["eps"], 1)
                pool.wait_ge(ev["aggr"], 1)
                neg = k.half_neg[:, 0:1].to_broadcast([P, TILES])
                link = Chain(pool, ev["pool"], 0)
                link.then(pool.tensor_tensor(t1[:, :], moments[:, :, 1], k.eps[:, 0:1].to_broadcast([P, TILES]),
                                             ALU.add))
                link.then(pool.tensor_tensor(rstd[:, :], t1[:, :], neg, ALU.pow))
                link.then(pool.tensor_tensor(t3[:, :], moments[:, :, 1], rstd[:, :], ALU.mult))
                link.then(pool.tensor_tensor(t3[:, :], t3[:, :], rstd[:, :], ALU.mult))
                link.then(pool.tensor_tensor(t3[:, :], t3[:, :], eps_rms[:, 0:1].to_broadcast([P, TILES]), ALU.add))
                link.then(pool.tensor_tensor(t4[:, :], t3[:, :], neg, ALU.pow))
                pool.tensor_tensor(scale[:, :], t4[:, :], rstd[:, :], ALU.mult).then_inc(ev["scale_done"], 1)

            @block.tensor
            def _(pe):
                pe.wait_ge(ev["flip"], 2)
                for g in range(GROUPS):
                    pe.wait_ge(ev["h_done"], g + 1)
                    if g >= 2:
                        pe.wait_ge(ev["lo"], g - 1)
                    for j in range(GT):
                        last = pe.matmul(turn[g % 2][:, j * P:(j + 1) * P], h[g % 2][:, j, :], flip[:, :],
                                         start=True, stop=True)
                    last.then_inc(ev["turned"], 1)

            @block.scalar
            def _(act):
                for g in range(GROUPS):
                    act.wait_ge(ev["turned"], g + 1)
                    act.activation(lo_hi(k, g)(k.xh), turn[g % 2][:, :].rearrange("p (b s) -> p b s", b=GB), ACT.Copy)\
                       .then_inc(ev["hi"], 1)

            load_params(k, block, early)
            build_tables(k, block)


def kernels(k, scratch_a, scratch_k, wout, win_hi, win_lo, bias_t):
    io, nc = k.io, k.nc
    with ExitStack() as st:
        sb = lambda name, shape, dt=F32: k.sb(f"kern_{name}", shape, dt, st)
        compact = sb("compact", [P, PACKS, ST])
        mask = sb("mask", [P, PACK, ST])
        A, AT = sb("A", [P, PACKS, P]), sb("AT", [P, PACKS, P])
        rows = sb("rows", [P, CT, ST, ST])
        rows16 = sb("rows16", [P, CT, ST, ST])
        baby, giant = sb("baby", [P, CT, ST, ST]), sb("giant", [P, CT, ST, ST])
        part = sb("part", [P, CT, ST, ST])
        wide = [sb("wide", [P, ST, ST, ST])[:, :, :, :],
                A[:, :, :].rearrange("p g m -> p (g m)").rearrange("p (i j s) -> p i j s", i=ST, j=ST)]
        K, KC = sb("K", [P, CT, TAPS - 1 + SEQ]), sb("KC", [P, CT, SEQ])
        sums = sb("sums", [P, 2, CT, SEQ])
        bias = sb("bias", [P, CT, SEQ])
        packed = sb("packed", [P, CT, PAD, 3], BF16)
        rest = part[:, :, :, :].rearrange("p t r s -> p t (r s)")
        taps, conv_b, b_in = sb("taps", [P, CT, TAPS]), sb("conv_b", [P, CT]), sb("b_in", [P, CT])
        norm_w, b_out, win = sb("norm_w", [P, 1]), sb("b_out", [P, 1]), sb("win", [P, CH])
        ones = sb("ones", [P, 1])
        bank = [k.ps(f"kern_bank{i}", stack=st) for i in range(6)]
        ev = events(k, "kern", "a_in in pool_done bd_done at_turned at_copied squared a_copied a16_out a16_in "
                    "link kern_done bias_psum k_out mask_link bias_done", st)
        LEVELS = 4
        QUADS = PACKS // 4

        def wide_factors(t):
            return (giant[:, t, :, :].unsqueeze(2).to_broadcast([P, ST, ST, ST]),
                    baby[:, t, :, :].unsqueeze(1).to_broadcast([P, ST, ST, ST]))

        channels = lambda v: v.rearrange("(t p) r -> p t r", p=P)
        with nc.Block() as block:
            @block.sync
            def _(sp):
                sp.dma_start(compact[:, :, :], io["L0_attn_A"].rearrange("(g c) r s -> (c r) g s", c=PACK))\
                  .then_inc(ev["a_in"], 16)
                loads = [
                    (rows[:, :, :, :].rearrange("p t r s -> p t (r s)"),
                     io["L0_attn_A"].rearrange("(t p) r s -> p t (r s)", p=P)),
                    (giant[:, :, 0, :], channels(io["L0_attn_Bm"].rearrange("d r a -> d (r a)"))),
                    (baby[:, :, 0, :], channels(io["L0_attn_Cm"].rearrange("d a r -> d (a r)"))),
                    (taps[:, :, :], channels(io["L0_attn_conv_w"].rearrange("d a r -> d (a r)"))),
                    (win[:, :], io["L0_attn_Win"]),
                    (wout[:, :, :], channels(io["L0_attn_Wout"])),
                    (conv_b[:, :], io["L0_attn_conv_b"].rearrange("(t p) -> p t", p=P)),
                    (b_in[:, :], io["L0_attn_b_in"].rearrange("(t p) -> p t", p=P)),
                    (norm_w[:, :], io["L0_attn_norm_w"].rearrange("(p a) -> p a", a=1)),
                    (b_out[:, :], io["L0_attn_b_out"].rearrange("(p a) -> p a", a=1)),
                ]
                with nc.allow_non_contiguous_dma(reason="a few columns of parameters"):
                    for out, src in loads:
                        sp.dma_start(out, src).then_inc(ev["in"], 16)
                k.kern_loads = 16 * len(loads)
                sp.wait_ge(ev["a_copied"], QUADS * (LEVELS + 1) - QUADS)
                to = scratch_a.rearrange("(g c) (r s) -> c r g s", c=PACK, r=ST)
                for c in range(PACK):
                    sp.dma_start(to[c], A[ST * c:ST * (c + 1), :, ST * c:ST * (c + 1)]).then_inc(ev["a16_out"], 16)
                sp.wait_ge(ev["a16_out"], 16 * PACK)
                sp.dma_start(rows16[:, :, :, :].rearrange("p t r s -> p t (r s)"), channels(scratch_a))\
                  .then_inc(ev["a16_in"], 16)
                sp.wait_ge(ev["kern_done"], 1)
                sp.dma_start(channels(scratch_k), packed[:, :, :, :].rearrange("p t a q -> p t (a q)"))\
                  .then_inc(ev["k_out"], 16)
                sp.wait_ge(ev["k_out"], 16)

            @block.gpsimd
            def _(pool):
                link = Chain(pool, ev["mask_link"], 0)
                link.then(pool.memset(mask[:, :, :], 1.0))
                link.then(pool.affine_select(out=mask[:, :, :], in_=mask[:, :, :], fill=0.0, compare_op=ALU.is_ge,
                                             base=0, pattern=[[-ST, PACK], [0, ST]], channel_multiplier=1))
                pool.affine_select(out=mask[:, :, :], in_=mask[:, :, :], fill=0.0, compare_op=ALU.is_ge,
                                   base=ST - 1, pattern=[[ST, PACK], [0, ST]], channel_multiplier=-1)\
                    .then_inc(ev["pool_done"], 1)

            @block.tensor
            def _(pe):
                for q in range(QUADS):
                    pe.wait_ge(ev["bd_done"], q + 1)
                    if q >= 6:
                        pe.wait_ge(ev["at_copied"], q - 5)
                    for i in range(4):
                        last = pe.transpose(bank[q % 6][:, i * P:(i + 1) * P], A[:, 4 * q + i, :], k.ident[:, :])
                    last.then_inc(ev["at_turned"], 1)
                n = 0
                for level in range(LEVELS):
                    for q in range(QUADS):
                        pe.wait_ge(ev["at_copied"], QUADS * level + q + 1)
                        if level:
                            pe.wait_ge(ev["a_copied"], QUADS * (level - 1) + q + 1)
                        b0, b1 = bank[2 * (n % 3)], bank[2 * (n % 3) + 1]
                        if n >= 3:
                            pe.wait_ge(ev["a_copied"], n - 2)
                            if QUADS + n - 2 <= QUADS * LEVELS:
                                pe.wait_ge(ev["at_copied"], QUADS + n - 2)
                        else:
                            pe.wait_ge(ev["at_copied"], QUADS)
                        for i in range(4):
                            g = 4 * q + i
                            last = pe.matmul(b0[:, i * P:(i + 1) * P], AT[:, g, :], A[:, g, :], start=True, stop=True)
                            if level < LEVELS - 1:
                                last = pe.matmul(b1[:, i * P:(i + 1) * P], A[:, g, :], AT[:, g, :],
                                                 start=True, stop=True)
                        last.then_inc(ev["squared"], 1)
                        n += 1
                pe.wait_ge(ev["bias_done"], 1)
                for t in range(CT):
                    last = pe.matmul(bank[0][:, 0:SEQ], wout[:, t, :], bias[:, t, :], start=(t == 0), stop=(t == CT - 1))
                last.then_inc(ev["bias_psum"], 1)

            @block.scalar
            def _(act):
                for q in range(QUADS):
                    act.wait_ge(ev["at_turned"], q + 1)
                    act.activation(AT[:, 4 * q:4 * q + 4, :], bank[q % 6][:, :].rearrange("p (i m) -> p i m", i=4),
                                   ACT.Copy).then_inc(ev["at_copied"], 1)
                n = 0
                for level in range(LEVELS - 1):
                    for q in range(QUADS):
                        act.wait_ge(ev["squared"], n + 1)
                        act.activation(AT[:, 4 * q:4 * q + 4, :],
                                       bank[2 * (n % 3) + 1][:, :].rearrange("p (i m) -> p i m", i=4), ACT.Copy)\
                           .then_inc(ev["at_copied"], 1)
                        n += 1

            @block.vector
            def _(dve):
                dve.wait_ge(ev["a_in"], 16)
                dve.wait_ge(ev["pool_done"], 1)
                for q in range(QUADS):
                    dve.tensor_tensor(A[:, 4 * q:4 * q + 4, :].rearrange("p g (c s) -> p g c s", c=PACK),
                                      compact[:, 4 * q:4 * q + 4, :].unsqueeze(2).to_broadcast([P, 4, PACK, ST]),
                                      mask[:, :, :].unsqueeze(1).to_broadcast([P, 4, PACK, ST]), ALU.mult)\
                       .then_inc(ev["bd_done"], 1)
                link = Chain(dve, ev["link"], 0)
                dve.memset(ones[:, :], 1.0)
                dve.memset(packed[:, :, :, :], 0.0)
                link.then(dve.memset(K[:, :, 0:TAPS - 1], 0.0))
                dve.wait_ge(ev["in"], k.kern_loads)
                link.then(dve.tensor_scalar(win[:, :], win[:, :], norm_w[:, 0:1], None, ALU.mult))
                link.then(dve.tensor_copy(win_hi[:, :], win[:, :]))
                dve.tensor_tensor(win_lo[:, :], win[:, :], win_hi[:, :].bitcast(F32), ALU.subtract)

                def baby_step(j):
                    link.then(dve.tensor_tensor(part[:, :, :, :], rows[:, :, :, :],
                                                baby[:, :, j, :].unsqueeze(2).to_broadcast([P, CT, ST, ST]), ALU.mult))
                    link.then(dve.tensor_reduce(baby[:, :, j + 1, :], part[:, :, :, :], AX_X, ALU.add))

                n, steps = 0, iter(range(ST - 1))
                for level in range(LEVELS):
                    for q in range(QUADS):
                        if q % 2 == 1 and (j := next(steps, None)) is not None:
                            baby_step(j)
                        dve.wait_ge(ev["squared"], n + 1)
                        dve.tensor_copy(A[:, 4 * q:4 * q + 4, :],
                                        bank[2 * (n % 3)][:, :].rearrange("p (i m) -> p i m", i=4))\
                           .then_inc(ev["a_copied"], 1)
                        n += 1
                for j in steps:
                    baby_step(j)
                dve.wait_ge(ev["a16_in"], 16)
                for i in range(ST - 1):
                    link.then(dve.tensor_tensor(part[:, :, :, :], rows16[:, :, :, :].rearrange("p t r s -> p t s r"),
                                                giant[:, :, i, :].unsqueeze(2).to_broadcast([P, CT, ST, ST]), ALU.mult))
                    link.then(dve.tensor_reduce(giant[:, :, i + 1, :], part[:, :, :, :], AX_X, ALU.add))
                k.steps_through = link.n
                for t in range(CT):
                    if t == 0:
                        link.then(dve.tensor_tensor(wide[t], *wide_factors(t), ALU.mult))
                    else:
                        dve.wait_ge(ev["pool_done"], 2)
                    link.then(dve.tensor_reduce(K[:, t, TAPS - 1:].rearrange("p (i j) -> p i j", i=ST),
                                                wide[t], AX_X, ALU.add))
                    lag = lambda m: K[:, t, TAPS - 1 - m:TAPS - 1 - m + SEQ]
                    link.then(dve.tensor_scalar(KC[:, t, :], lag(0), taps[:, t, 3:4], None, ALU.mult))
                    for m in range(1, TAPS):
                        link.then(dve.scalar_tensor_tensor(out=KC[:, t, :], in0=lag(m), scalar=taps[:, t, 3 - m:4 - m],
                                                           in1=KC[:, t, :], op0=ALU.mult, op1=ALU.add))
                link.then(dve.tensor_copy(packed[:, :, P:, 0], KC[:, :, :]))
                link.then(dve.tensor_tensor(rest[:, :, :], KC[:, :, :], packed[:, :, P:, 0], ALU.subtract))
                link.then(dve.tensor_copy(packed[:, :, P:, 1], rest[:, :, :]))
                dve.tensor_tensor(packed[:, :, P:, 2], rest[:, :, :], packed[:, :, P:, 1], ALU.subtract)\
                   .then_inc(ev["kern_done"], 1)
                for t in range(CT):
                    dve.tensor_tensor_scan(sums[:, 0, t, :], ones[:, 0:1].to_broadcast([P, SEQ]), K[:, t, TAPS - 1:],
                                           0.0, ALU.mult, ALU.add)
                    last = dve.tensor_tensor_scan(sums[:, 1, t, :], ones[:, 0:1].to_broadcast([P, SEQ]), KC[:, t, :],
                                                  0.0, ALU.mult, ALU.add)
                link.then(last)
                for t in range(CT):
                    last = dve.tensor_scalar(bias[:, t, :], sums[:, 0, t, :], conv_b[:, t:t + 1], None, ALU.mult)
                link.then(last)
                for t in range(CT):
                    last = dve.scalar_tensor_tensor(out=bias[:, t, :], in0=sums[:, 1, t, :], scalar=b_in[:, t:t + 1],
                                                    in1=bias[:, t, :], op0=ALU.mult, op1=ALU.add)
                last.then_inc(ev["bias_done"], 1)
                dve.wait_ge(ev["bias_psum"], 1)
                dve.tensor_scalar(bias_t[:, :], bank[0][:, 0:SEQ], b_out[:, 0:1], None, ALU.add)

            @block.gpsimd
            def _(pool):
                pool.wait_ge(ev["link"], k.steps_through)
                pool.tensor_tensor(wide[1], *wide_factors(1), ALU.mult).then_inc(ev["pool_done"], 1)


def recurrence(k, scratch_k, win_hi, win_lo, Y):
    nc = k.nc
    with ExitStack() as st:
        sb = lambda name, shape, dt=F32: k.sb(f"rec_{name}", shape, dt, st)
        COLS = 3 * BATCH
        U = sb("U", [P, 2, CH, COLS], BF16)
        T = [sb(f"T{i}", [P, TCH, SEQ * 3], BF16) for i in range(RING)]
        rest = [sb(f"rest{i}", [P, 2, CH]) for i in range(2)]
        bank = [k.ps(f"rec_bank{i}", stack=st) for i in range(4)]
        ev = events(k, "rec", "u_psum u_hi u_rest u_mid u_done t_used y_psum y_done", st)
        arrived = [k.sem(f"toeplitz_in{i}", st) for i in range(RING)]
        width = PAD * 3

        def toeplitz(load):
            return bass.AP(scratch_k.tensor, load * TCH * width + 3, [[3, P], [width, TCH], [1, SEQ * 3]])

        def part(b, q):
            at = bass.ds(b, 1) if not isinstance(b, int) else slice(b, b + 1)
            return U[:, :, :, :].rearrange("p h c (q b) -> p h c q b", q=3)[:, :, :, q, at]\
                .rearrange("p h c a -> p h (c a)")

        def halves(t):
            return t.rearrange("p (h c) -> p h c", h=2)

        with nc.Block() as block:
            @block.sync
            def _(sp):
                for load in range(LOADS):
                    if load >= RING:
                        sp.wait_ge(ev["t_used"], load - RING + 1)
                    sp.dma_start(T[load % RING][:, :, :], toeplitz(load)).then_inc(arrived[load % RING], 16)

            @block.tensor
            def _(pe):
                for b in range(BATCH):
                    if b >= 2:
                        pe.wait_ge(ev["u_rest"], b - 1)
                    for half in range(2):
                        at = b * PADDED + 1 + half * P
                        last = mm3(pe, bank[b % 2][:, half * CH:(half + 1) * CH], k.xh[:, at:at + P],
                                   k.xl[:, at:at + P], win_hi[:, :], win_lo[:, :])
                    last.then_inc(ev["u_psum"], 1)
                pe.wait_ge(ev["u_done"], BATCH)
                with pe.Fori(0, LOADS // RING) as r:
                    for i in range(RING):
                        load = r * RING + i
                        pe.wait_ge(arrived[i], 16 * r + 16)
                        for c in range(TCH):
                            out = bank[2 * (i % 2) + c // 4]
                            if c % 4 == 0:
                                pe.wait_ge(ev["y_done"], 2 * load + c // 4 + 1)
                            t3 = T[i][:, c, :].rearrange("p (t q) -> p t q", q=3)
                            near, far = t3[:, 0:P, :], t3[:, P:SEQ, :]
                            u0, u1 = (U[:, h, bass.ds(load * TCH + c, 1), :].rearrange("p a n -> p (a n)")
                                      for h in range(2))
                            first = out[:, (c % 4) * 2 * COLS:(c % 4) * 2 * COLS + COLS]
                            second = out[:, (c % 4) * 2 * COLS + COLS:(c % 4 + 1) * 2 * COLS]
                            for q in range(3):
                                pe.matmul(first, near[:, :, q], u0, start=(q == 0), stop=(q == 2))
                            for q in range(3):
                                pe.matmul(second, far[:, :, q], u0, start=(q == 0), stop=False)
                                last = pe.matmul(second, near[:, :, q], u1, start=False, stop=(q == 2))
                            if c % 4 == 3:
                                last.then_inc(ev["y_psum"], 1)
                        last = pe.matmul(k.turn[0:32, 0:8], k.identb[:, 0:32], k.identb[:, 0:8], start=True, stop=True)
                        last.then_inc(ev["t_used"], 1)

            @block.scalar
            def _(act):
                def rounded(b, i):
                    act.wait_ge(ev["u_psum"], b + 1)
                    act.activation(part(b, 0), halves(bank[i][:, :]), ACT.Copy).then_inc(ev["u_hi"], 1)

                def middle(b, i):
                    act.wait_ge(ev["u_rest"], b + 1)
                    act.activation(part(b, 1), rest[i][:, :, :], ACT.Copy).then_inc(ev["u_mid"], 1)

                rounded(0, 0)
                rounded(1, 1)
                middle(0, 0)
                with act.Fori(0, BATCH // 2 - 1) as r:
                    for i in range(2):
                        rounded(r * 2 + i + 2, i)
                        middle(r * 2 + i + 1, 1 - i)
                middle(BATCH - 1, 1)

            @block.vector
            def _(dve):
                dve.memset(k.tick[:, :], 0.0).then_inc(ev["y_done"], 4)

                def first_rest(b, i):
                    dve.wait_ge(ev["u_hi"], b + 1)
                    dve.tensor_tensor(rest[i][:, :, :], halves(bank[i][:, :]), part(b, 0), ALU.subtract)\
                       .then_inc(ev["u_rest"], 1)

                def last_rest(b, i):
                    dve.wait_ge(ev["u_mid"], b + 1)
                    dve.tensor_tensor(part(b, 2), rest[i][:, :, :], part(b, 1), ALU.subtract)\
                       .then_inc(ev["u_done"], 1)

                first_rest(0, 0)
                first_rest(1, 1)
                last_rest(0, 0)
                with dve.Fori(0, BATCH // 2 - 1) as r:
                    for i in range(2):
                        dve.wait_ge(ev["u_done"], r * 2 + i + 1)
                        first_rest(r * 2 + i + 2, i)
                        last_rest(r * 2 + i + 1, 1 - i)
                last_rest(BATCH - 1, 1)
                with dve.Fori(0, LOADS // RING) as r:
                    for i in range(RING):
                        load = r * RING + i
                        for h in range(2):
                            dve.wait_ge(ev["y_psum"], 2 * load + h + 1)
                            parts = bank[2 * (i % 2) + h][:, 0:8 * COLS].rearrange("p (c q b) -> p c b q", q=3, b=BATCH)
                            out = Y[:, bass.ds(load * TCH + 4 * h, 4), :, :].rearrange("p c h b -> p (c h) b")
                            dve.tensor_reduce(out, parts, AX_X, ALU.add).then_inc(ev["y_done"], 1)


def project(k, wout, bias_t, Y, next_route):
    nc = k.nc
    base = k.turn0
    with ExitStack() as st:
        yc = [[k.sb(f"proj_y{i}{t}", [P, GROUP], F32, st) for t in range(CT)] for i in range(2)]
        bank = [k.ps(f"proj_bank{i}", stack=st) for i in range(4)]
        route_scratch(k, "proj", st)
        ev = events(k, "proj", "turned copied", st)
        turns = range(GROUPS + 3)

        with nc.Block() as block:
            @block.tensor
            def _(pe):
                def turn(g):
                    for t in range(CT):
                        if g >= 2:
                            pe.wait_ge(ev["copied"], CT * (g - 2) + t + 1)
                        for j in range(GT):
                            b, half = g * GB + j // 2, j % 2
                            last = pe.transpose(bank[2 * (g % 2) + t][:, j * P:(j + 1) * P],
                                                Y[:, t * P:(t + 1) * P, half, b], k.ident[:, :])
                        last.then_inc(ev["turned"], 1)

                def output(g):
                    pe.wait_ge(ev["copied"], CT * (g + 1))
                    if g:
                        pe.wait_ge(k.y_copied, base + g)
                    for t in range(CT):
                        pe.matmul(k.ypsum[:, :], wout[:, t, :], yc[g % 2][t][:, :], start=(t == 0), stop=False)
                    for b in range(GB):
                        last = pe.matmul(k.ypsum[:, b * SEQ:(b + 1) * SEQ], k.ident[:, :], bias_t[:, :],
                                         start=False, stop=(b == GB - 1))
                    last.then_inc(k.y_done, 1)

                def post(g, *steps):
                    for step in steps:
                        post_tensor(k, pe, step, base + g, g, next_route)

                for g in turns:
                    p = Pipeline(g, g, g)
                    p.part(3, post, 7)
                    p.part(2, post, 1)
                    p.part(0, turn)
                    p.part(3, post, 9)
                    p.part(2, post, 4)
                    p.part(1, output)
                    p.part(3, post, 14)

            @block.scalar
            def _(act):
                def copy(g):
                    for t in range(CT):
                        act.wait_ge(ev["turned"], CT * g + t + 1)
                        act.activation(yc[g % 2][t][:, :], bank[2 * (g % 2) + t][:, :], ACT.Copy)\
                           .then_inc(ev["copied"], 1)

                def post(g, *steps):
                    for step in steps:
                        post_scalar(k, act, step, base + g, g, next_route)

                for g in turns:
                    p = Pipeline(g, g, g)
                    p.part(2, post, 0)
                    p.part(3, post, 8)
                    p.part(0, copy)
                    p.part(3, post, 10)
                    p.part(2, post, 5)
                    p.part(3, post, 15)

            @block.vector
            def _(dve):
                def post(g, *steps):
                    for step in steps:
                        post_vector(k, dve, step, base + g, g, next_route)

                def body(p):
                    p.part(0, post, 2)
                    p.part(1, post, 13)
                    p.part(0, post, 6)

                pipelined(dve, 1, body)

            @block.gpsimd
            def _(pool):
                gpsimd_stage(k, pool, None)


def build(nc, io):
    with ExitStack() as stack:
        k = Chip(nc, io, stack)
        share(k)
        share_routes(k)
        share_moe(k)
        build_constants(k)
        share_params(k)
        ssm(k, ROUTES["ffn0"])
        with ExitStack() as st:
            weights = ffn0(io)
            weights.sel = k.sel64
            weights.allocate(k, st)
            moe_stage(k, weights, load_here=True)
        load_attn(k)
        for attention, ffn, sel, kw in ((attn1, ffn1, k.sel8, {}),
                                        (attn2, ffn2, k.sel4, {"bias1": k.b1, "b2": k.b2p}),
                                        (attn3, ffn3, k.sel8, {"last": True})):
            with ExitStack() as st:
                weights = ffn(io)
                weights.sel = sel
                weights.allocate(k, st)
                attention(k, weights)
                moe_stage(k, weights, **kw)



def kernel(**inputs):
    import numpy as np
    from concourse import bacc
    from concourse.bass_utils import run_bass_kernel_spmd

    nc = bacc.Bacc("TRN2", target_bir_lowering=False, num_devices=1)
    arrays, io = {}, {}
    for name, value in inputs.items():
        a = np.ascontiguousarray(value)
        a = a.reshape(1) if a.ndim == 0 else a
        arrays[f"in_{name}"] = a
        io[name] = nc.dram_tensor(f"in_{name}", a.shape, mybir.dt.from_np(a.dtype), kind="ExternalInput").ap()
    io["out"] = nc.dram_tensor("out", (TOKENS, D), F32, kind="ExternalOutput").ap()
    build(nc, io)
    r = run_bass_kernel_spmd(nc, [arrays], core_ids=[0])
    return r.results[0]["out"].reshape(BATCH, SEQ, D)
```
